# Optimizing a Trainium2 kernel written in Bass

```python
import numpy as np
import jax
import jax.numpy as jnp

def _softmax(x, axis=-1):
    return jax.nn.softmax(x, axis=axis)

def _gelu(x):
    return jax.nn.gelu(x, approximate=True)

def _silu(x):
    return jax.nn.silu(x)

def _sigmoid(x):
    return jax.nn.sigmoid(x)

def _layernorm(x, axis=-1, eps=1e-05):
    m = jnp.mean(x, axis=axis, keepdims=True)
    v = jnp.var(x, axis=axis, keepdims=True)
    return (x - m) / jnp.sqrt(v + eps)

def _scatter_add(tgt, idx, src, axis=0):
    return tgt.at[idx].add(src)

def _segment_sum(src, seg, n):
    return jax.ops.segment_sum(src, seg, n)
kernel_name = 'mk_metaformer_d4_conv_nchw256_r4_7f69bf'

def setup_inputs(seed: int=0):
    np.random.seed(seed)
    _w = jnp.asarray

    def _rec_inputs():
        import jax
        import jax.numpy as jnp
        _gk = jax.random.key(seed)
        x = -0.0003929 + 0.9999 * jax.random.normal(jax.random.fold_in(_gk, 1), (16, 64, 16, 16), jnp.float32)
        return x
    x = _rec_inputs()

    def _L0_conv_setup():
        import jax, jax.numpy as jnp
        import numpy as np
        HEADS = 8
        DIM_HEAD = 16
        SCALE = DIM_HEAD ** (-0.5)
        EPS = 1e-05
        key = jax.random.key(seed)
        ks = jax.random.split(key, 5)
        b, dim, h, w = (16, 64, 16, 16)
        hidden = HEADS * DIM_HEAD
        mem = 16
        x = jax.random.normal(ks[0], (b, dim, h, w), dtype=jnp.float32)
        memory = jax.random.normal(ks[1], (1, dim, 1, mem), dtype=jnp.float32)
        W_qkv = jax.random.normal(ks[2], (hidden * 3, dim), dtype=jnp.float32) * 0.05
        W_out = jax.random.normal(ks[3], (dim, hidden), dtype=jnp.float32) * 0.05
        b_out = jnp.zeros((dim,), dtype=jnp.float32)
        ln_g = jnp.ones((dim,), dtype=jnp.float32)
        ln_b = jnp.zeros((dim,), dtype=jnp.float32)
        return {'x': x, 'memory': memory, 'W_qkv': W_qkv, 'W_out': W_out, 'b_out': b_out, 'ln_g': ln_g, 'ln_b': ln_b}
    _L0_conv_all = _L0_conv_setup()
    _L0_conv_in = {k: v for k, v in _L0_conv_all.items() if k in ('memory', 'W_qkv', 'W_out', 'b_out', 'ln_g', 'ln_b')}
    del _L0_conv_all

    def _L0_ffn_setup():
        import jax, jax.numpy as jnp
        import numpy as np
        N_EXPERTS = 8
        TOP_K = 2
        key = jax.random.key(seed)
        ks = jax.random.split(key, 5)
        B, T, C, E, H = (8, 512, 64, 8, 682)
        scale = 1.0 / np.sqrt(C)
        return {'x': jax.random.normal(ks[0], (B, T, C), dtype=jnp.float32), 'router_w': jax.random.normal(ks[1], (E, C), dtype=jnp.float32) * scale, 'w1': jax.random.normal(ks[2], (E, H, C), dtype=jnp.float32) * scale, 'w2': jax.random.normal(ks[3], (E, C, H), dtype=jnp.float32) * (1.0 / np.sqrt(H)), 'w3': jax.random.normal(ks[4], (E, H, C), dtype=jnp.float32) * scale}
    _L0_ffn_all = _L0_ffn_setup()
    _L0_ffn_in = {k: v for k, v in _L0_ffn_all.items() if k in ('router_w', 'w1', 'w2', 'w3')}
    del _L0_ffn_all

    def _L1_conv_setup():
        import jax, jax.numpy as jnp
        import numpy as np
        H_DIM = 64
        N_HEADS = 8
        HALF = H_DIM // 2

        def _lin(x, W, b):
            y = x @ W.T
            return y + b if b is not None else y

        def _rel_pos_index(h, w):
            ch, cw = np.meshgrid(np.arange(h), np.arange(w), indexing='ij')
            coords = np.stack([ch.reshape(-1), cw.reshape(-1)])
            rel = coords[:, :, None] - coords[:, None, :]
            rel = rel.transpose(1, 2, 0)
            rel[:, :, 0] += h - 1
            rel[:, :, 1] += w - 1
            return rel[:, :, 0] * (2 * w - 1) + rel[:, :, 1]

        def _forward(x, q1_w, q1_b, q2_w, q2_b, k1_w, k1_b, k2_w, k2_b, v1_w, v1_b, v2_w, v2_b, proj1_w, proj1_b, proj2_w, proj2_b, logit_scale, mlp_w1, mlp_b1, mlp_w2):
            b, c, h, w = x.shape
            N = h * w
            nh = N_HEADS
            hd = c // nh
            x3 = jnp.transpose(x, (0, 2, 3, 1)).reshape(b, N, c)
            x0, x1 = (x3[..., :c // 2], x3[..., c // 2:])

            def qkv(W0, b0, W1, b1):
                t = jnp.concatenate([x0 + _lin(x0, W0, b0), x1 + _lin(x1, W1, b1)], axis=-1)
                return t.reshape(b, N, nh, hd).transpose(0, 2, 1, 3)
            q = qkv(q1_w, q1_b, q2_w, q2_b)
            k = qkv(k1_w, k1_b, k2_w, k2_b)
            v = qkv(v1_w, v1_b, v2_w, v2_b)
            eps = 1e-12
            qn = q / jnp.maximum(jnp.linalg.norm(q, axis=-1, keepdims=True), eps)
            kn = k / jnp.maximum(jnp.linalg.norm(k, axis=-1, keepdims=True), eps)
            attn = jnp.einsum('bhnd,bhmd->bhnm', qn, kn)
            scale = jnp.exp(jnp.minimum(logit_scale, jnp.log(1.0 / 0.01)))
            attn = attn * scale[None]
            rch = jnp.arange(-(h - 1), h, dtype=jnp.float32) / (h - 1 + 1e-08)
            rcw = jnp.arange(-(w - 1), w, dtype=jnp.float32) / (w - 1 + 1e-08)
            gh, gw = jnp.meshgrid(rch, rcw, indexing='ij')
            tab = jnp.stack([gh, gw], axis=-1) * 3.2
            tab = jnp.sign(tab) * (1.0 - jnp.exp(-jnp.abs(tab)))
            tab = jax.nn.relu(_lin(tab, mlp_w1, mlp_b1))
            tab = _lin(tab, mlp_w2, None).reshape(-1, nh)
            idx = jnp.asarray(_rel_pos_index(h, w))
            bias = tab[idx.reshape(-1)].reshape(N, N, nh).transpose(2, 0, 1)
            bias = 16.0 * jax.nn.sigmoid(bias)
            attn = attn + bias[None]
            attn = jax.nn.softmax(attn, axis=-1)
            out = jnp.einsum('bhnm,bhmd->bhnd', attn, v).transpose(0, 2, 1, 3).reshape(b, N, c)
            o0, o1 = (out[..., :c // 2], out[..., c // 2:])
            out = jnp.concatenate([_lin(o0, proj1_w, proj1_b), _lin(o1, proj2_w, proj2_b)], axis=-1)
            return out.reshape(b, h, w, c).transpose(0, 3, 1, 2)
        key = jax.random.key(seed)
        ks = jax.random.split(key, 16)
        s = 0.02
        d = {'x': jax.random.normal(ks[0], (16, H_DIM, 32, 32), jnp.float32), 'q1_w': jax.random.normal(ks[1], (HALF, HALF), jnp.float32) * s, 'q1_b': jnp.zeros((HALF,), jnp.float32), 'q2_w': jax.random.normal(ks[2], (HALF, HALF), jnp.float32) * s, 'q2_b': jnp.zeros((HALF,), jnp.float32), 'k1_w': jax.random.normal(ks[3], (HALF, HALF), jnp.float32) * s, 'k1_b': jnp.zeros((HALF,), jnp.float32), 'k2_w': jax.random.normal(ks[4], (HALF, HALF), jnp.float32) * s, 'k2_b': jnp.zeros((HALF,), jnp.float32), 'v1_w': jax.random.normal(ks[5], (HALF, HALF), jnp.float32) * s, 'v1_b': jnp.zeros((HALF,), jnp.float32), 'v2_w': jax.random.normal(ks[6], (HALF, HALF), jnp.float32) * s, 'v2_b': jnp.zeros((HALF,), jnp.float32), 'proj1_w': jax.random.normal(ks[7], (HALF, HALF), jnp.float32) * s, 'proj1_b': jnp.zeros((HALF,), jnp.float32), 'proj2_w': jax.random.normal(ks[8], (HALF, HALF), jnp.float32) * s, 'proj2_b': jnp.zeros((HALF,), jnp.float32), 'logit_scale': jnp.log(10.0 * jnp.ones((N_HEADS, 1, 1), jnp.float32)), 'mlp_w1': jax.random.normal(ks[9], (32, 2), jnp.float32) * s, 'mlp_b1': jnp.zeros((32,), jnp.float32), 'mlp_w2': jax.random.normal(ks[10], (N_HEADS, 32), jnp.float32) * s}
        return d
    _L1_conv_all = _L1_conv_setup()
    _L1_conv_in = {k: v for k, v in _L1_conv_all.items() if k in ('q1_w', 'q1_b', 'q2_w', 'q2_b', 'k1_w', 'k1_b', 'k2_w', 'k2_b', 'v1_w', 'v1_b', 'v2_w', 'v2_b', 'proj1_w', 'proj1_b', 'proj2_w', 'proj2_b', 'logit_scale', 'mlp_w1', 'mlp_b1', 'mlp_w2')}
    del _L1_conv_all

    def _L1_ffn_setup():
        import jax, jax.numpy as jnp
        import numpy as np
        B, T, D, H, E = (16, 1024, 64, 128, 8)
        key = jax.random.key(seed)
        ks = jax.random.split(key, 5)
        x = jax.random.normal(ks[0], (B, T, D), dtype=jnp.float32)
        gate_w = jax.random.normal(ks[1], (D, E), dtype=jnp.float32) * 0.02
        gate_b = jnp.zeros((E,), dtype=jnp.float32)
        W1 = jax.random.normal(ks[2], (E, D, H), dtype=jnp.float32) * 0.02
        b1 = jnp.zeros((E, H), dtype=jnp.float32)
        W2 = jax.random.normal(ks[3], (E, H, D), dtype=jnp.float32) * 0.02
        b2 = jnp.zeros((E, D), dtype=jnp.float32)
        return {'x': x, 'gate_w': gate_w, 'gate_b': gate_b, 'W1': W1, 'b1': b1, 'W2': W2, 'b2': b2}
    _L1_ffn_all = _L1_ffn_setup()
    _L1_ffn_in = {k: v for k, v in _L1_ffn_all.items() if k in ('gate_w', 'gate_b', 'W1', 'b1', 'W2', 'b2')}
    del _L1_ffn_all

    def _L2_conv_setup():
        import jax, jax.numpy as jnp
        import numpy as np
        EPS = 1e-08
        key = jax.random.key(seed)
        k1, k2, k3 = jax.random.split(key, 3)
        b, c, h, w = (4, 64, 16, 16)
        x = jax.random.normal(k1, (b, c, h, w), dtype=jnp.float32)
        W = jax.random.normal(k2, (64, 64), dtype=jnp.float32) * (1.0 / np.sqrt(64))
        bias = jax.random.normal(k3, (64,), dtype=jnp.float32) * 0.01
        return {'x': x, 'W': W, 'bias': bias}
    _L2_conv_all = _L2_conv_setup()
    _L2_conv_in = {k: v for k, v in _L2_conv_all.items() if k in ('W', 'bias')}
    del _L2_conv_all

    def _L2_ffn_setup():
        import jax, jax.numpy as jnp
        import numpy as np
        TOP_K = 2
        key = jax.random.key(seed)
        ks = jax.random.split(key, 4)
        B, L, D, H, E = (8, 1024, 64, 256, 8)
        s = 0.02
        return {'x': jax.random.normal(ks[0], (B, L, D), jnp.float32), 'Wg': jax.random.normal(ks[1], (D, E), jnp.float32) * s, 'bg': jnp.zeros((E,), jnp.float32), 'W1': jax.random.normal(ks[2], (E, D, H), jnp.float32) * s, 'b1': jnp.zeros((E, H), jnp.float32), 'W2': jax.random.normal(ks[3], (E, H, D), jnp.float32) * s, 'b2': jnp.zeros((E, D), jnp.float32)}
    _L2_ffn_all = _L2_ffn_setup()
    _L2_ffn_in = {k: v for k, v in _L2_ffn_all.items() if k in ('Wg', 'bg', 'W1', 'b1', 'W2', 'b2')}
    del _L2_ffn_all

    def _L3_conv_setup():
        import jax, jax.numpy as jnp
        import numpy as np
        BOUND = 1.0
        key = jax.random.key(seed)
        kx, kw = jax.random.split(key)
        x = jax.random.normal(kx, (32, 64, 56, 56), dtype=jnp.float32)
        fan_in = 64 * 3 * 3
        fan_out = 64 * 3 * 3
        std = 2.0 * np.sqrt(2.0 / (fan_in + fan_out))
        W = jax.random.normal(kw, (64, 64, 3, 3), dtype=jnp.float32) * std
        return {'x': x, 'W': W}
    _L3_conv_all = _L3_conv_setup()
    _L3_conv_in = {k: v for k, v in _L3_conv_all.items() if k in ('W',)}
    del _L3_conv_all

    def _L3_ffn_setup():
        import jax, jax.numpy as jnp
        import numpy as np
        NUM_EXPERTS = 8
        TOP_K = 2
        B, S, D = (8, 2048, 64)

        def _moe(tokens, router_w, w1, b1, w2, b2):
            N = tokens.shape[0]
            E = router_w.shape[0]
            logits = tokens.astype(jnp.float32) @ router_w.astype(jnp.float32).T
            probs = jax.nn.softmax(logits, axis=-1)
            rw, re = jax.lax.top_k(probs, TOP_K)
            if TOP_K > 1:
                rw = rw / jnp.maximum(rw.sum(-1, keepdims=True), 1e-12)
            rw = rw.astype(tokens.dtype)
            combine = jnp.zeros((N, E), tokens.dtype).at[jnp.arange(N)[:, None], re].set(rw)
            out = tokens
            for e in range(E):
                h = jax.nn.gelu(tokens @ w1[e] + b1[e], approximate=False)
                y = h @ w2[e] + b2[e]
                out = out + combine[:, e:e + 1] * y
            return out
        key = jax.random.key(seed)
        ks = jax.random.split(key, 4)
        scale = 1.0 / np.sqrt(D).astype(np.float32)
        return {'input_embeddings': jax.random.normal(ks[0], (B, S, D), jnp.float32), 'router_w': jax.random.normal(ks[1], (NUM_EXPERTS, D), jnp.float32) * scale, 'w1': jax.random.normal(ks[2], (NUM_EXPERTS, D, D), jnp.float32) * scale, 'b1': jnp.zeros((NUM_EXPERTS, D), jnp.float32), 'w2': jax.random.normal(ks[3], (NUM_EXPERTS, D, D), jnp.float32) * scale, 'b2': jnp.zeros((NUM_EXPERTS, D), jnp.float32)}
    _L3_ffn_all = _L3_ffn_setup()
    _L3_ffn_in = {k: v for k, v in _L3_ffn_all.items() if k in ('router_w', 'w1', 'b1', 'w2', 'b2')}
    del _L3_ffn_all
    return {'x': x, 'L0_conv_memory': _L0_conv_in['memory'], 'L0_conv_W_qkv': _L0_conv_in['W_qkv'], 'L0_conv_W_out': _L0_conv_in['W_out'], 'L0_conv_b_out': _L0_conv_in['b_out'], 'L0_conv_ln_g': _L0_conv_in['ln_g'], 'L0_conv_ln_b': _L0_conv_in['ln_b'], 'L0_ffn_router_w': _L0_ffn_in['router_w'], 'L0_ffn_w1': _L0_ffn_in['w1'], 'L0_ffn_w2': _L0_ffn_in['w2'], 'L0_ffn_w3': _L0_ffn_in['w3'], 'L1_conv_q1_w': _L1_conv_in['q1_w'], 'L1_conv_q1_b': _L1_conv_in['q1_b'], 'L1_conv_q2_w': _L1_conv_in['q2_w'], 'L1_conv_q2_b': _L1_conv_in['q2_b'], 'L1_conv_k1_w': _L1_conv_in['k1_w'], 'L1_conv_k1_b': _L1_conv_in['k1_b'], 'L1_conv_k2_w': _L1_conv_in['k2_w'], 'L1_conv_k2_b': _L1_conv_in['k2_b'], 'L1_conv_v1_w': _L1_conv_in['v1_w'], 'L1_conv_v1_b': _L1_conv_in['v1_b'], 'L1_conv_v2_w': _L1_conv_in['v2_w'], 'L1_conv_v2_b': _L1_conv_in['v2_b'], 'L1_conv_proj1_w': _L1_conv_in['proj1_w'], 'L1_conv_proj1_b': _L1_conv_in['proj1_b'], 'L1_conv_proj2_w': _L1_conv_in['proj2_w'], 'L1_conv_proj2_b': _L1_conv_in['proj2_b'], 'L1_conv_logit_scale': _L1_conv_in['logit_scale'], 'L1_conv_mlp_w1': _L1_conv_in['mlp_w1'], 'L1_conv_mlp_b1': _L1_conv_in['mlp_b1'], 'L1_conv_mlp_w2': _L1_conv_in['mlp_w2'], 'L1_ffn_gate_w': _L1_ffn_in['gate_w'], 'L1_ffn_gate_b': _L1_ffn_in['gate_b'], 'L1_ffn_W1': _L1_ffn_in['W1'], 'L1_ffn_b1': _L1_ffn_in['b1'], 'L1_ffn_W2': _L1_ffn_in['W2'], 'L1_ffn_b2': _L1_ffn_in['b2'], 'L2_conv_W': _L2_conv_in['W'], 'L2_conv_bias': _L2_conv_in['bias'], 'L2_ffn_Wg': _L2_ffn_in['Wg'], 'L2_ffn_bg': _L2_ffn_in['bg'], 'L2_ffn_W1': _L2_ffn_in['W1'], 'L2_ffn_b1': _L2_ffn_in['b1'], 'L2_ffn_W2': _L2_ffn_in['W2'], 'L2_ffn_b2': _L2_ffn_in['b2'], 'L3_conv_W': _L3_conv_in['W'], 'L3_ffn_router_w': _L3_ffn_in['router_w'], 'L3_ffn_w1': _L3_ffn_in['w1'], 'L3_ffn_b1': _L3_ffn_in['b1'], 'L3_ffn_w2': _L3_ffn_in['w2'], 'L3_ffn_b2': _L3_ffn_in['b2']}

def reference(x, L0_conv_memory, L0_conv_W_qkv, L0_conv_W_out, L0_conv_b_out, L0_conv_ln_g, L0_conv_ln_b, L0_ffn_router_w, L0_ffn_w1, L0_ffn_w2, L0_ffn_w3, L1_conv_q1_w, L1_conv_q1_b, L1_conv_q2_w, L1_conv_q2_b, L1_conv_k1_w, L1_conv_k1_b, L1_conv_k2_w, L1_conv_k2_b, L1_conv_v1_w, L1_conv_v1_b, L1_conv_v2_w, L1_conv_v2_b, L1_conv_proj1_w, L1_conv_proj1_b, L1_conv_proj2_w, L1_conv_proj2_b, L1_conv_logit_scale, L1_conv_mlp_w1, L1_conv_mlp_b1, L1_conv_mlp_w2, L1_ffn_gate_w, L1_ffn_gate_b, L1_ffn_W1, L1_ffn_b1, L1_ffn_W2, L1_ffn_b2, L2_conv_W, L2_conv_bias, L2_ffn_Wg, L2_ffn_bg, L2_ffn_W1, L2_ffn_b1, L2_ffn_W2, L2_ffn_b2, L3_conv_W, L3_ffn_router_w, L3_ffn_w1, L3_ffn_b1, L3_ffn_w2, L3_ffn_b2):
    import jax
    import jax.numpy as jnp

    def _L0_conv_ref(x, memory, W_qkv, W_out, b_out, ln_g, ln_b):
        import jax, jax.numpy as jnp
        import numpy as np
        HEADS = 8
        DIM_HEAD = 16
        SCALE = DIM_HEAD ** (-0.5)
        EPS = 1e-05
        b, c, h, w = x.shape
        n = h * w
        mem = memory.shape[-1]
        x_ext = jnp.concatenate([x.reshape(b, c, n), jnp.broadcast_to(memory.reshape(1, c, mem), (b, c, mem))], axis=2)
        qkv = jnp.einsum('oc,bcn->bon', W_qkv, x_ext)
        q, k, v = jnp.split(qkv, 3, axis=1)

        def to_heads(t):
            return t.reshape(b, HEADS, DIM_HEAD, -1)
        q = jax.nn.softmax(to_heads(q), axis=2) * SCALE
        k = jax.nn.softmax(to_heads(k), axis=3)
        v = to_heads(v)
        context = jnp.einsum('bhdn,bhen->bhde', k, v)
        out = jnp.einsum('bhde,bhdn->bhen', context, q)
        out = out[..., :n].reshape(b, HEADS * DIM_HEAD, n)
        y = jnp.einsum('oc,bcn->bon', W_out, out) + b_out[None, :, None]
        mean = jnp.mean(y, axis=1, keepdims=True)
        var = jnp.var(y, axis=1, keepdims=True)
        y = (y - mean) / jnp.sqrt(var + EPS) * ln_g[None, :, None] + ln_b[None, :, None]
        return y.reshape(b, c, h, w)

    def _L0_ffn_ref(x, router_w, w1, w2, w3):
        import jax, jax.numpy as jnp
        import numpy as np
        N_EXPERTS = 8
        TOP_K = 2
        B, T, C = x.shape
        flat = x.reshape(-1, C)
        logits = flat @ router_w.T
        probs = jax.nn.softmax(logits, axis=-1)
        topk_probs, topk_idx = jax.lax.top_k(probs, TOP_K)
        topk_probs = topk_probs / (jnp.sum(topk_probs, axis=-1, keepdims=True) + 1e-09)
        onehot = jax.nn.one_hot(topk_idx, N_EXPERTS, dtype=flat.dtype)
        gates = jnp.einsum('nk,nke->ne', topk_probs, onehot)
        h1 = jnp.einsum('nc,ehc->neh', flat, w1)
        h3 = jnp.einsum('nc,ehc->neh', flat, w3)
        h = jax.nn.silu(h1) * h3
        y = jnp.einsum('neh,ech->nec', h, w2)
        out = jnp.einsum('ne,nec->nc', gates, y)
        return out.reshape(B, T, C)

    def _L1_conv_ref(x, q1_w, q1_b, q2_w, q2_b, k1_w, k1_b, k2_w, k2_b, v1_w, v1_b, v2_w, v2_b, proj1_w, proj1_b, proj2_w, proj2_b, logit_scale, mlp_w1, mlp_b1, mlp_w2):
        import jax, jax.numpy as jnp
        import numpy as np
        H_DIM = 64
        N_HEADS = 8
        HALF = H_DIM // 2

        def _lin(x, W, b):
            y = x @ W.T
            return y + b if b is not None else y

        def _rel_pos_index(h, w):
            ch, cw = np.meshgrid(np.arange(h), np.arange(w), indexing='ij')
            coords = np.stack([ch.reshape(-1), cw.reshape(-1)])
            rel = coords[:, :, None] - coords[:, None, :]
            rel = rel.transpose(1, 2, 0)
            rel[:, :, 0] += h - 1
            rel[:, :, 1] += w - 1
            return rel[:, :, 0] * (2 * w - 1) + rel[:, :, 1]

        def _forward(x, q1_w, q1_b, q2_w, q2_b, k1_w, k1_b, k2_w, k2_b, v1_w, v1_b, v2_w, v2_b, proj1_w, proj1_b, proj2_w, proj2_b, logit_scale, mlp_w1, mlp_b1, mlp_w2):
            b, c, h, w = x.shape
            N = h * w
            nh = N_HEADS
            hd = c // nh
            x3 = jnp.transpose(x, (0, 2, 3, 1)).reshape(b, N, c)
            x0, x1 = (x3[..., :c // 2], x3[..., c // 2:])

            def qkv(W0, b0, W1, b1):
                t = jnp.concatenate([x0 + _lin(x0, W0, b0), x1 + _lin(x1, W1, b1)], axis=-1)
                return t.reshape(b, N, nh, hd).transpose(0, 2, 1, 3)
            q = qkv(q1_w, q1_b, q2_w, q2_b)
            k = qkv(k1_w, k1_b, k2_w, k2_b)
            v = qkv(v1_w, v1_b, v2_w, v2_b)
            eps = 1e-12
            qn = q / jnp.maximum(jnp.linalg.norm(q, axis=-1, keepdims=True), eps)
            kn = k / jnp.maximum(jnp.linalg.norm(k, axis=-1, keepdims=True), eps)
            attn = jnp.einsum('bhnd,bhmd->bhnm', qn, kn)
            scale = jnp.exp(jnp.minimum(logit_scale, jnp.log(1.0 / 0.01)))
            attn = attn * scale[None]
            rch = jnp.arange(-(h - 1), h, dtype=jnp.float32) / (h - 1 + 1e-08)
            rcw = jnp.arange(-(w - 1), w, dtype=jnp.float32) / (w - 1 + 1e-08)
            gh, gw = jnp.meshgrid(rch, rcw, indexing='ij')
            tab = jnp.stack([gh, gw], axis=-1) * 3.2
            tab = jnp.sign(tab) * (1.0 - jnp.exp(-jnp.abs(tab)))
            tab = jax.nn.relu(_lin(tab, mlp_w1, mlp_b1))
            tab = _lin(tab, mlp_w2, None).reshape(-1, nh)
            idx = jnp.asarray(_rel_pos_index(h, w))
            bias = tab[idx.reshape(-1)].reshape(N, N, nh).transpose(2, 0, 1)
            bias = 16.0 * jax.nn.sigmoid(bias)
            attn = attn + bias[None]
            attn = jax.nn.softmax(attn, axis=-1)
            out = jnp.einsum('bhnm,bhmd->bhnd', attn, v).transpose(0, 2, 1, 3).reshape(b, N, c)
            o0, o1 = (out[..., :c // 2], out[..., c // 2:])
            out = jnp.concatenate([_lin(o0, proj1_w, proj1_b), _lin(o1, proj2_w, proj2_b)], axis=-1)
            return out.reshape(b, h, w, c).transpose(0, 3, 1, 2)
        return _forward(x, q1_w, q1_b, q2_w, q2_b, k1_w, k1_b, k2_w, k2_b, v1_w, v1_b, v2_w, v2_b, proj1_w, proj1_b, proj2_w, proj2_b, logit_scale, mlp_w1, mlp_b1, mlp_w2)

    def _L1_ffn_ref(x, gate_w, gate_b, W1, b1, W2, b2):
        import jax, jax.numpy as jnp
        import numpy as np
        B, T, D, H, E = (16, 1024, 64, 128, 8)
        Bb, Tt, Dd = x.shape
        Ee = gate_w.shape[1]
        xf = x.reshape(-1, Dd)
        N = xf.shape[0]
        logits = xf @ gate_w + gate_b
        probs = jax.nn.softmax(logits, axis=-1)
        top2_vals, top2_idx = jax.lax.top_k(probs, 2)
        cw = jnp.zeros((N, Ee), dtype=xf.dtype).at[jnp.arange(N)[:, None], top2_idx].add(top2_vals)

        def step(acc, params):
            w1, bb1, w2, bb2, we = params
            h = jax.nn.gelu(xf @ w1 + bb1, approximate=False)
            y = h @ w2 + bb2
            return (acc + we[:, None] * y, None)
        out, _ = jax.lax.scan(step, jnp.zeros_like(xf), (W1, b1, W2, b2, cw.T))
        return out.reshape(Bb, Tt, Dd)

    def _L2_conv_ref(x, W, bias):
        import jax, jax.numpy as jnp
        import numpy as np
        EPS = 1e-08
        b, c, h, w = x.shape
        p = h * w
        xf = x.reshape(b, c, p)
        dots = jnp.einsum('bcp,bcq->bpq', xf, xf)
        norms = jnp.sqrt(jnp.sum(xf * xf, axis=1))
        denom = jnp.maximum(norms[:, :, None] * norms[:, None, :], EPS)
        sim = jnp.square(jax.nn.relu(dots / denom))
        tx = jnp.einsum('oc,bcq->boq', W, xf) + bias[None, :, None]
        out = jnp.einsum('bpq,boq->bop', sim, tx)
        return out.reshape(b, -1, h, w)

    def _L2_ffn_ref(x, Wg, bg, W1, b1, W2, b2):
        import jax, jax.numpy as jnp
        import numpy as np
        TOP_K = 2
        B, L, D = x.shape
        E = W1.shape[0]
        xf = x.reshape(-1, D)
        gate_logits = xf @ Wg + bg
        top_w, top_i = jax.lax.top_k(gate_logits, TOP_K)
        top_w = jax.nn.softmax(top_w, axis=-1)
        w_dense = jnp.sum(jax.nn.one_hot(top_i, E, dtype=xf.dtype) * top_w[..., None], axis=1)
        out = jnp.zeros_like(xf)
        for e in range(E):
            h = jax.nn.gelu(xf @ W1[e] + b1[e], approximate=False)
            out = out + w_dense[:, e:e + 1] * (h @ W2[e] + b2[e])
        return out.reshape(B, L, D)

    def _L3_conv_ref(x, W):
        import jax, jax.numpy as jnp
        import numpy as np
        BOUND = 1.0
        cw = jnp.clip(W, -BOUND, BOUND)
        bw = cw + jax.lax.stop_gradient(jnp.sign(W) - cw)
        out = jax.lax.conv_general_dilated(x, bw, window_strides=(1, 1), padding=((1, 1), (1, 1)), dimension_numbers=('NCHW', 'OIHW', 'NCHW'))
        return out

    def _L3_ffn_ref(input_embeddings, router_w, w1, b1, w2, b2):
        import jax, jax.numpy as jnp
        import numpy as np
        NUM_EXPERTS = 8
        TOP_K = 2
        B, S, D = (8, 2048, 64)

        def _moe(tokens, router_w, w1, b1, w2, b2):
            N = tokens.shape[0]
            E = router_w.shape[0]
            logits = tokens.astype(jnp.float32) @ router_w.astype(jnp.float32).T
            probs = jax.nn.softmax(logits, axis=-1)
            rw, re = jax.lax.top_k(probs, TOP_K)
            if TOP_K > 1:
                rw = rw / jnp.maximum(rw.sum(-1, keepdims=True), 1e-12)
            rw = rw.astype(tokens.dtype)
            combine = jnp.zeros((N, E), tokens.dtype).at[jnp.arange(N)[:, None], re].set(rw)
            out = tokens
            for e in range(E):
                h = jax.nn.gelu(tokens @ w1[e] + b1[e], approximate=False)
                y = h @ w2[e] + b2[e]
                out = out + combine[:, e:e + 1] * y
            return out
        b, s, d = input_embeddings.shape
        tokens = input_embeddings.reshape(b * s, d)
        return _moe(tokens, router_w, w1, b1, w2, b2).reshape(b, s, d)

    def _gn(v, G=32, eps=1e-05):
        B_, C_, H_, W_ = v.shape
        g = v.reshape(B_, G, C_ // G, H_, W_)
        m = jnp.mean(g, axis=(2, 3, 4), keepdims=True)
        s = jnp.var(g, axis=(2, 3, 4), keepdims=True)
        return ((g - m) / jnp.sqrt(s + eps)).reshape(v.shape)

    def _ln_c(v, eps=1e-06):
        m = jnp.mean(v, axis=1, keepdims=True)
        s = jnp.var(v, axis=1, keepdims=True)
        return (v - m) / jnp.sqrt(s + eps)

    def _ln_t(v, eps=1e-05):
        m = jnp.mean(v, axis=-1, keepdims=True)
        s = jnp.var(v, axis=-1, keepdims=True)
        return (v - m) / jnp.sqrt(s + eps)

    def _to_tokens(v):
        B_, C_, H_, W_ = v.shape
        return v.reshape(B_, C_, H_ * W_).transpose(0, 2, 1)

    def _from_tokens(t, like):
        B_, C_, H_, W_ = like.shape
        return t.transpose(0, 2, 1).reshape(B_, C_, H_, W_)
    x = x + _L0_conv_ref(_ln_c(x), L0_conv_memory, L0_conv_W_qkv, L0_conv_W_out, L0_conv_b_out, L0_conv_ln_g, L0_conv_ln_b)
    t = _to_tokens(x)
    t = t + _L0_ffn_ref(_ln_t(t), L0_ffn_router_w, L0_ffn_w1, L0_ffn_w2, L0_ffn_w3)
    x = _from_tokens(t, x)
    x = x + _L1_conv_ref(_ln_c(x), L1_conv_q1_w, L1_conv_q1_b, L1_conv_q2_w, L1_conv_q2_b, L1_conv_k1_w, L1_conv_k1_b, L1_conv_k2_w, L1_conv_k2_b, L1_conv_v1_w, L1_conv_v1_b, L1_conv_v2_w, L1_conv_v2_b, L1_conv_proj1_w, L1_conv_proj1_b, L1_conv_proj2_w, L1_conv_proj2_b, L1_conv_logit_scale, L1_conv_mlp_w1, L1_conv_mlp_b1, L1_conv_mlp_w2)
    t = _to_tokens(x)
    t = t + _L1_ffn_ref(_ln_t(t), L1_ffn_gate_w, L1_ffn_gate_b, L1_ffn_W1, L1_ffn_b1, L1_ffn_W2, L1_ffn_b2)
    x = _from_tokens(t, x)
    x = x + _L2_conv_ref(_ln_c(x), L2_conv_W, L2_conv_bias)
    t = _to_tokens(x)
    t = t + _L2_ffn_ref(_ln_t(t), L2_ffn_Wg, L2_ffn_bg, L2_ffn_W1, L2_ffn_b1, L2_ffn_W2, L2_ffn_b2)
    x = _from_tokens(t, x)
    x = x + _L3_conv_ref(_ln_c(x), L3_conv_W)
    t = _to_tokens(x)
    t = t + _L3_ffn_ref(_ln_t(t), L3_ffn_router_w, L3_ffn_w1, L3_ffn_b1, L3_ffn_w2, L3_ffn_b2)
    x = _from_tokens(t, x)
    return x

_drawn_inputs = setup_inputs


def setup_inputs(seed=0):
    import zlib

    import numpy as np

    out = dict(_drawn_inputs(seed))
    spreads = {'L0_conv_b_out': (0.0, 0.1),
     'L0_conv_ln_g': (1.0, 0.2),
     'L0_conv_ln_b': (0.0, 0.1),
     'L1_conv_q1_b': (0.0, 0.8),
     'L1_conv_q2_b': (0.0, 0.8),
     'L1_conv_k1_b': (0.0, 0.8),
     'L1_conv_k2_b': (0.0, 0.8),
     'L1_conv_v1_b': (0.0, 0.8),
     'L1_conv_v2_b': (0.0, 0.8),
     'L1_conv_proj1_b': (0.0, 0.1),
     'L1_conv_proj2_b': (0.0, 0.1),
     'L1_conv_logit_scale': (2.3025851249694824, 0.6),
     'L1_conv_mlp_b1': (0.0, 2.0),
     'L1_ffn_gate_b': (0.0, 0.8),
     'L1_ffn_b1': (0.0, 0.8),
     'L1_ffn_b2': (0.0, 0.451),
     'L2_ffn_bg': (0.0, 0.8),
     'L2_ffn_b1': (0.0, 0.8),
     'L2_ffn_b2': (0.0, 0.8),
     'L3_ffn_b1': (0.0, 0.8),
     'L3_ffn_b2': (0.0, 2.0)}
    factors = {'L0_conv_memory': 4.341,
     'L1_conv_q1_w': 8.0,
     'L1_conv_q2_w': 8.0,
     'L1_conv_k1_w': 8.0,
     'L1_conv_k2_w': 8.0,
     'L1_conv_v1_w': 6.838,
     'L1_conv_v2_w': 8.0,
     'L1_conv_mlp_w1': 41.55,
     'L1_conv_mlp_w2': 57.978,
     'L1_ffn_gate_w': 4.861,
     'L1_ffn_W1': 8.0,
     'L1_ffn_W2': 8.0,
     'L2_conv_bias': 4.2,
     'L2_ffn_Wg': 8.0,
     'L2_ffn_W1': 8.0,
     'L2_ffn_W2': 8.0,
     'L3_ffn_router_w': 8.0,
     'L3_ffn_w1': 6.24,
     'L3_ffn_w2': 7.548}
    for name, (base, spread) in spreads.items():
        noise = np.random.default_rng([zlib.crc32(name.encode()), seed]).standard_normal(out[name].shape)
        drawn = base * np.exp(spread * noise) if base else spread * noise
        out[name] = jnp.asarray(drawn.astype(out[name].dtype))
    for name, factor in factors.items():
        out[name] = (out[name] * factor).astype(out[name].dtype)
    return out
```

```python
from contextlib import ExitStack

import numpy as np

import concourse.bass as bass
from concourse import mybir

F32 = mybir.dt.float32
F16 = mybir.dt.float16
ALU = mybir.AluOpType
ACT = mybir.ActivationFunctionType
AX = mybir.AxisListType

P = 128
C = 64
KC = C + 1
B = 16
SIDE = 16
N = SIDE * SIDE
T = B * N
NT = T // P
TPG = 4
GROUPS = NT // TPG
GTOK = TPG * P
BANK = 512
E = 8
HEADS0, DH0, MEM = 8, 16, 16
HID0 = HEADS0 * DH0
HEADS1, DH1 = 8, 8
VW = DH1 + 1
H_L0, H_L1, H_L2, H_L3 = 682, 128, 256, 64
FULL0, TAIL0 = H_L0 // P, H_L0 % P
PAIR0 = 2 * FULL0 + 1
REL = 2 * SIDE - 1
PADS = SIDE + 2


class Chain:

    def __init__(self, sem):
        self.sem, self.eng, self.base, self.k, self.i, self.per = sem, None, 0, 0, None, 0

    def on(self, eng):
        self.eng = eng
        return self

    def loop(self, i, per):
        self.i, self.per = i, per

    def end(self, times):
        assert self.k == self.per, (self.k, self.per)
        self.base += times * self.per
        self.k, self.i, self.per = 0, None, 0

    def link(self, ins):
        ins.then_inc(self.sem, 1)
        self.k += 1
        at = self.base + self.k
        if self.i is None:
            self.base, self.k = at, 0
        self.eng.wait_ge(self.sem, at if self.i is None else self.i * self.per + at)


def metaformer(nc, x, ident, wt_rank, L0, F0, L1, F1, L2, F2, L3, F3, out, stop_after=99):
    ctx = ExitStack()
    with ctx:
        def sb(name, shape, dt=F32):
            return ctx.enter_context(nc.sbuf_tensor(name + "_sb", shape, dt))

        def sem(name):
            return ctx.enter_context(nc.semaphore(name))

        ps = ctx.enter_context(nc.psum_tensor("ps", [P, 8, BANK], F32))

        x_tok = sb("x_tok", [P, NT, C])
        xn_tok = sb("xn_tok", [P, NT, C])
        xn_ch = sb("xn_ch", [KC, T])
        idn = sb("idn", [P, P])
        idn16 = sb("idn16", [P, P], F16)
        rank = sb("rank", [P, E])
        sq = sb("sq", [P, NT, C])
        st = sb("st", [P, 4, NT])
        neg_half = sb("neg_half", [P, 1])
        gates = sb("gates", [P, NT, E])
        rt = sb("rt", [P, 6, NT, E])
        rs = sb("rs", [P, 6, NT])
        HIDDEN0 = 4 * PAIR0 * P
        w13 = sb("w13", [P, 2 * HIDDEN0])
        w1, w3 = w13[0:KC, 0:HIDDEN0], w13[0:KC, HIDDEN0:2 * HIDDEN0]
        w2 = sb("w2", [P, 4 * (PAIR0 + 1) * C])
        b2_row = sb("b2_row", [P, E * C])
        row0 = sb("row0", [P, P])
        router_w = sb("router_w", [KC, E])
        act_h = sb("act_h", [P, 4, GTOK])
        mul_h = sb("mul_h", [P, 4, GTOK])
        weighted = sb("weighted", [P, E, C])
        expert_sum = sb("expert_sum", [P, C])
        rel_bias = sb("rel_bias", [P, 2, HEADS1, N])
        vals = sb("vals", [P, NT, HEADS1, VW])

        dve_chain = Chain(sem("dve_chain"))
        act_chain = Chain(sem("act_chain"))
        pool_chain = Chain(sem("pool_chain"))
        loaded = {k: sem(f"loaded_{k}") for k in ("x", "const", "l0", "f", "l1", "l2", "l3", "bias")}
        want = dict.fromkeys(loaded, 0)
        stored = sem("stored")

        def load(eng, key, dst, src):
            eng.dma_start(dst, src).then_inc(loaded[key], 16)
            want[key] += 16

        s_centred, s_squared = sem("norm_centred"), sem("norm_squared")
        s_var, s_rstd = sem("norm_var"), sem("norm_rstd")
        s_scaled, s_turned = sem("norm_scaled"), sem("norm_turned")
        norms = [0]

        def norm_stage(eps):
            n0 = norms[0]
            norms[0] += 1
            halves = [slice(h * NT // 2, (h + 1) * NT // 2) for h in range(2)]

            def wide(v, s):
                return v.unsqueeze(2).broadcast_to((P, s.stop - s.start, C))

            with nc.Block() as block:
                if n0 == 0:
                    @block.sync
                    def _(sp):
                        load(sp, "x", x_tok[:, :, :], x)
                        load(sp, "const", idn[:, :], ident)
                        load(sp, "const", rank[:, :], wt_rank)

                @block.vector
                def _(dve):
                    c = dve_chain.on(dve)
                    if n0 == 0:
                        nc.vector.memset(xn_ch[C:KC, :], 1.0)
                        dve.wait_ge(loaded["x"], want["x"])
                    for s in halves:
                        c.link(nc.vector.tensor_reduce(st[:, 0, s], x_tok[:, s, :], AX.X, ALU.add, negate=True))
                        c.link(nc.vector.tensor_scalar(st[:, 0, s], st[:, 0, s], 1.0 / C, None, ALU.mult))
                        nc.vector.tensor_tensor(xn_tok[:, s, :], x_tok[:, s, :], wide(st[:, 0, s], s),
                                                ALU.add).then_inc(s_centred, 1)
                    for h, s in enumerate(halves):
                        dve.wait_ge(s_squared, 2 * n0 + h + 1)
                        c.link(nc.vector.tensor_reduce(st[:, 1, s], sq[:, s, :], AX.X, ALU.add))
                        nc.vector.tensor_scalar(st[:, 2, s], st[:, 1, s], 1.0 / C, float(eps),
                                                ALU.mult, ALU.add).then_inc(s_var, 1)
                    for h, s in enumerate(halves):
                        dve.wait_ge(s_rstd, 2 * n0 + h + 1)
                        nc.vector.tensor_tensor(xn_tok[:, s, :], xn_tok[:, s, :], wide(st[:, 3, s], s),
                                                ALU.mult).then_inc(s_scaled, 1)
                    for k in range(1, GROUPS, 2):
                        dve.wait_ge(s_turned, GROUPS * n0 + k + 1)
                        nc.vector.tensor_copy(xn_ch[0:C, k * GTOK:(k + 1) * GTOK], ps[0:C, k, :])

                @block.scalar
                def _(act):
                    for h, s in enumerate(halves):
                        act.wait_ge(s_centred, 2 * n0 + h + 1)
                        nc.scalar.activation(sq[:, s, :], xn_tok[:, s, :], ACT.Square).then_inc(s_squared, 1)
                    for k in range(0, GROUPS, 2):
                        act.wait_ge(s_turned, GROUPS * n0 + k + 1)
                        nc.scalar.copy(xn_ch[0:C, k * GTOK:(k + 1) * GTOK], ps[0:C, k, :])

                @block.gpsimd
                def _(pool):
                    if n0 == 0:
                        pool_chain.on(pool).link(nc.gpsimd.memset(neg_half[:, :], -0.5))
                    for h, s in enumerate(halves):
                        pool.wait_ge(s_var, 2 * n0 + h + 1)
                        nc.gpsimd.tensor_tensor(st[:, 3, s], st[:, 2, s],
                                                neg_half[:, :].broadcast_to((P, NT // 2)),
                                                ALU.pow).then_inc(s_rstd, 1)

                @block.tensor
                def _(pe):
                    if n0 == 0:
                        pe.wait_ge(loaded["const"], 32)
                    for k in range(GROUPS):
                        if k % (GROUPS // 2) == 0:
                            pe.wait_ge(s_scaled, 2 * n0 + k // (GROUPS // 2) + 1)
                        for t in range(TPG):
                            last = nc.tensor.transpose(ps[0:C, k, t * P:(t + 1) * P],
                                                       xn_tok[:, k * TPG + t, :], idn[:, :])
                        last.then_inc(s_turned, 1)

        def linear_attention():
            qv_w = sbl("qv_w", [KC, 2 * HID0])
            k_w = sbl("k_w", [KC, HID0])
            out_w = sbl("out_w", [HID0, C])
            memory = sbl("memory", [KC, MEM])
            head_mask = sbl("head_mask", [HID0, HID0])
            ln_rows = sbl("ln_rows", [P, 3, C])
            x_grp = sbl("x_grp", [KC, GTOK])
            k_mem = sbl("k_mem", [HID0, MEM])
            v_mem = sbl("v_mem", [MEM, HID0])
            nk_mem = sbl("nk_mem", [HID0, 1])
            nk_max = sbl("nk_max", [HID0, 2, 2])
            v_tok = sbl("v_tok", [P, TPG, HID0])
            k_exp = sbl("k_exp", [HID0, 2, N + MEM])
            k_sum = sbl("k_sum", [HID0, 2, 2])
            k_inv = sbl("k_inv", [HID0, 2])
            kt = sbl("kt", [P, TPG, HID0])
            kt_mem = sbl("kt_mem", [MEM, 2, HID0])
            ctx_t = sbl("ctx_t", [HID0, 2, HID0])
            mix = sbl("mix", [HID0, 2, C])
            q_tok = sbl("q_tok", [P, TPG, HEADS0, DH0])
            q_st = sbl("q_st", [P, 2, TPG, HEADS0])
            q_ch = sbl("q_ch", [HID0, GTOK])
            y_tok = sbl("y_tok", [P, 2, TPG, C])
            y_st = sbl("y_st", [P, 4, TPG])

            mem_ps, mem_kv = sem("l0_mem_ps"), sem("l0_mem_kv")
            x_copied, k_ps, qv_ps = sem("l0_x_copied"), sem("l0_k_ps"), sem("l0_qv_ps")
            k_max, k_exped, v_copied = sem("l0_k_max"), sem("l0_k_exped"), sem("l0_v_copied")
            q_shifted, q_exped, q_ready = sem("l0_q_shifted"), sem("l0_q_exped"), sem("l0_q_ready")
            kt_ps, kt_copied, ktm_copied = sem("l0_kt_ps"), sem("l0_kt_copied"), sem("l0_ktm_copied")
            ctx_ps, ctx_ready, mix_ps, mix_ready = sem("l0_ctx_ps"), sem("l0_ctx_ready"), sem("l0_mix_ps"), sem("l0_mix_ready")
            qt_ps, qt_copied, y_ps = sem("l0_qt_ps"), sem("l0_qt_copied"), sem("l0_y_ps")
            y_sq_in, y_sq, y_var, y_rstd = sem("l0_y_sq_in"), sem("l0_y_sq"), sem("l0_y_var"), sem("l0_y_rstd")

            qv = ps[:, 0:2, :].rearrange("p w (t c) -> p w t c", c=HID0)
            q_ps = qv[:, 0, :, :].rearrange("p t (h d) -> p t h d", d=DH0)
            v_ps = qv[:, 1, :, :]
            kp = ps[:, 2, :].rearrange("p (b n) -> p b n", b=2)

            with nc.Block() as block:
                @block.sync
                def _(sp):
                    for dst, src in ((qv_w, L0[0]), (k_w, L0[1]), (memory, L0[3]), (out_w, L0[2]),
                                     (head_mask, L0[4])):
                        load(sp, "l0", dst[:, :], src)
                    load(sp, "l0", ln_rows[:, :, :], L0[5].unsqueeze(0).broadcast_to((P, 3, C)))
                    load_experts(sp, F0, True)

                @block.scalar
                def _(act):
                    c = act_chain.on(act)
                    act.wait_ge(mem_ps, 1)
                    c.link(nc.scalar.copy(k_mem[:, :], ps[:, 4, 0:MEM]))
                    nc.scalar.copy(v_mem[:, :], ps[0:MEM, 4, 128:128 + HID0]).then_inc(mem_kv, 1)
                    with act.Fori(0, GROUPS) as g:
                        nc.scalar.copy(x_grp[:, :], xn_ch[:, bass.ds(g * GTOK, GTOK)]).then_inc(x_copied, 1)
                        act.wait_ge(qv_ps, g + 1)
                        nc.scalar.copy(v_tok[:, :, :], v_ps).then_inc(v_copied, 1)
                        act.wait_ge(k_max, g + 1)
                        for b in range(2):
                            nc.scalar.activation(k_exp[:, b, 0:N], kp[:, b, :], ACT.Exp,
                                                 bias=nk_max[:, b, 1:2], accum_out=k_sum[:, b, 0:1])
                            last = nc.scalar.activation(k_exp[:, b, N:], k_mem[:, :], ACT.Exp,
                                                        bias=nk_max[:, b, 1:2], accum_out=k_sum[:, b, 1:2])
                        last.then_inc(k_exped, 1)
                        act.wait_ge(q_shifted, g + 1)
                        nc.scalar.activation(q_tok[:, :, :, :], q_tok[:, :, :, :], ACT.Exp).then_inc(q_exped, 1)
                        act.wait_ge(kt_ps, g + 1)
                        nc.scalar.copy(kt_mem[:, :, :], ps[0:MEM, 4, 0:2 * HID0].rearrange(
                            "p (b d) -> p b d", b=2)).then_inc(ktm_copied, 1)
                        act.wait_ge(qt_ps, g + 1)
                        nc.scalar.copy(q_ch[:, :], ps[:, 7, :]).then_inc(qt_copied, 1)
                        act.wait_ge(y_sq_in, g + 1)
                        nc.scalar.activation(y_tok[:, 1, :, :], y_tok[:, 0, :, :], ACT.Square).then_inc(y_sq, 1)

                @block.tensor
                def _(pe):
                    pe.wait_ge(loaded["l0"], want["l0"])
                    nc.tensor.matmul(ps[:, 4, 0:MEM], k_w[:, :], memory[:, :], start=True, stop=True)
                    nc.tensor.matmul(ps[0:MEM, 4, 128:128 + HID0], memory[:, :], qv_w[:, HID0:],
                                     start=True, stop=True).then_inc(mem_ps, 1)
                    pe.wait_ge(mem_kv, 1)
                    with pe.Fori(0, GROUPS) as g:
                        pe.wait_ge(x_copied, g + 1)
                        nc.tensor.matmul(ps[:, 2, :], k_w[:, :], x_grp[:, :], start=True, stop=True).then_inc(k_ps, 1)
                        for t in range(TPG):
                            for w in range(2):
                                last = nc.tensor.matmul(qv[:, w, t, :], x_grp[:, t * P:(t + 1) * P],
                                                        qv_w[:, w * HID0:(w + 1) * HID0], start=True, stop=True)
                        last.then_inc(qv_ps, 1)
                        pe.wait_ge(k_exped, g + 1)
                        for b in range(2):
                            for j in range(2):
                                nc.tensor.transpose(ps[:, 3, (2 * b + j) * P:(2 * b + j + 1) * P],
                                                    k_exp[:, b, j * P:(j + 1) * P], idn[:, :])
                            last = nc.tensor.transpose(ps[0:MEM, 4, b * P:(b + 1) * P],
                                                       k_exp[:, b, N:], idn[:, :])
                        last.then_inc(kt_ps, 1)
                        pe.wait_ge(q_ready, g + 1)
                        for t in range(TPG):
                            last = nc.tensor.transpose(ps[:, 7, t * P:(t + 1) * P],
                                                       q_tok[:, t, :, :].rearrange("p h d -> p (h d)"), idn[:, :])
                        last.then_inc(qt_ps, 1)
                        pe.wait_ge(v_copied, g + 1)
                        pe.wait_ge(kt_copied, g + 1)
                        pe.wait_ge(ktm_copied, g + 1)
                        for b in range(2):
                            o = ps[:, 5, b * P:(b + 1) * P]
                            for j in range(2):
                                nc.tensor.matmul(o, v_tok[:, 2 * b + j, :], kt[:, 2 * b + j, :],
                                                 start=(j == 0), stop=False)
                            last = nc.tensor.matmul(o, v_mem[:, :], kt_mem[:, b, :], start=False, stop=True)
                        last.then_inc(ctx_ps, 1)
                        pe.wait_ge(ctx_ready, g + 1)
                        for b in range(2):
                            last = nc.tensor.matmul(ps[:, 6, b * C:(b + 1) * C], ctx_t[:, b, :], out_w[:, :],
                                                    start=True, stop=True)
                        last.then_inc(mix_ps, 1)
                        pe.wait_ge(mix_ready, g + 1)
                        pe.wait_ge(qt_copied, g + 1)
                        for t in range(TPG):
                            last = nc.tensor.matmul(ps[:, 6, 256 + t * C:256 + (t + 1) * C],
                                                    q_ch[:, t * P:(t + 1) * P], mix[:, t // 2, :],
                                                    start=True, stop=True)
                        last.then_inc(y_ps, 1)

                @block.gpsimd
                def _(pool):
                    with pool.Fori(0, GROUPS) as g:
                        pool.wait_ge(y_var, g + 1)
                        nc.gpsimd.tensor_tensor(y_st[:, 3, :], y_st[:, 2, :],
                                                neg_half[:, :].broadcast_to((P, TPG)), ALU.pow).then_inc(y_rstd, 1)

                @block.vector
                def _(dve):
                    c = dve_chain.on(dve)
                    dve.wait_ge(mem_kv, 1)
                    c.link(nc.vector.tensor_reduce(nk_mem[:, :], k_mem[:, :], AX.X, ALU.max, negate=True))
                    y, y2 = y_tok[:, 0, :, :], y_tok[:, 1, :, :]
                    with dve.Fori(0, GROUPS) as g:
                        c.loop(g, 15)

                        def wide4(v, n=C):
                            return v.unsqueeze(2).broadcast_to((P, TPG, n))

                        def rows(r):
                            return ln_rows[:, r, :].unsqueeze(1).broadcast_to((P, TPG, C))

                        dve.wait_ge(k_ps, g + 1)
                        c.link(nc.vector.tensor_reduce(nk_max[:, :, 0], kp, AX.X, ALU.max, negate=True))
                        nc.vector.tensor_tensor(nk_max[:, :, 1], nk_max[:, :, 0],
                                                nk_mem[:, :].broadcast_to((HID0, 2)), ALU.min).then_inc(k_max, 1)
                        dve.wait_ge(qv_ps, g + 1)
                        c.link(nc.vector.tensor_reduce(q_st[:, 0, :, :], q_ps, AX.X, ALU.max))
                        nc.vector.tensor_tensor(q_tok[:, :, :, :], q_ps,
                                                q_st[:, 0, :, :].unsqueeze(3).broadcast_to((P, TPG, HEADS0, DH0)),
                                                ALU.subtract).then_inc(q_shifted, 1)
                        dve.wait_ge(q_exped, g + 1)
                        c.link(nc.vector.tensor_reduce(q_st[:, 0, :, :], q_tok[:, :, :, :], AX.X, ALU.add))
                        c.link(nc.vector.reciprocal(q_st[:, 1, :, :], q_st[:, 0, :, :]))
                        nc.vector.tensor_tensor(q_tok[:, :, :, :], q_tok[:, :, :, :],
                                                q_st[:, 1, :, :].unsqueeze(3).broadcast_to((P, TPG, HEADS0, DH0)),
                                                ALU.mult).then_inc(q_ready, 1)
                        dve.wait_ge(kt_ps, g + 1)
                        nc.vector.tensor_copy(kt[:, :, :], ps[:, 3, :].rearrange(
                            "p (t d) -> p t d", t=TPG)).then_inc(kt_copied, 1)
                        c.link(nc.vector.tensor_tensor(k_inv[:, :], k_sum[:, :, 0], k_sum[:, :, 1], ALU.add))
                        c.link(nc.vector.reciprocal(k_inv[:, :], k_inv[:, :]))
                        c.link(nc.vector.tensor_scalar(k_inv[:, :], k_inv[:, :], DH0 ** -0.5, None, ALU.mult))
                        dve.wait_ge(ctx_ps, g + 1)
                        nc.vector.tensor_tensor(ctx_t[:, :, :],
                                                ps[:, 5, 0:2 * P].rearrange("p (b d) -> p b d", b=2),
                                                head_mask[:, :].unsqueeze(1).broadcast_to((P, 2, HID0)),
                                                ALU.mult).then_inc(ctx_ready, 1)
                        dve.wait_ge(mix_ps, g + 1)
                        for b in range(2):
                            last = nc.vector.tensor_scalar(mix[:, b, :], ps[:, 6, b * C:(b + 1) * C],
                                                           k_inv[:, b:b + 1], None, ALU.mult)
                        last.then_inc(mix_ready, 1)
                        dve.wait_ge(y_ps, g + 1)
                        c.link(nc.vector.tensor_tensor(y, ps[:, 6, 256:512].rearrange("p (t c) -> p t c", t=TPG),
                                                       rows(0), ALU.add))
                        c.link(nc.vector.tensor_reduce(y_st[:, 0, :], y, AX.X, ALU.add, negate=True))
                        c.link(nc.vector.tensor_scalar(y_st[:, 0, :], y_st[:, 0, :], 1.0 / C, None, ALU.mult))
                        nc.vector.tensor_tensor(y, y, wide4(y_st[:, 0, :]), ALU.add).then_inc(y_sq_in, 1)
                        dve.wait_ge(y_sq, g + 1)
                        c.link(nc.vector.tensor_reduce(y_st[:, 1, :], y2, AX.X, ALU.add))
                        nc.vector.tensor_scalar(y_st[:, 2, :], y_st[:, 1, :], 1.0 / C, 1e-5,
                                                ALU.mult, ALU.add).then_inc(y_var, 1)
                        dve.wait_ge(y_rstd, g + 1)
                        c.link(nc.vector.tensor_tensor(y, y, wide4(y_st[:, 3, :]), ALU.mult))
                        c.link(nc.vector.tensor_tensor(y, y, rows(1), ALU.mult))
                        c.link(nc.vector.tensor_tensor(y, y, rows(2), ALU.add))
                        xg = x_tok[:, bass.ds(g * TPG, TPG), :]
                        c.link(nc.vector.tensor_tensor(xg, xg, y, ALU.add))
                    c.end(GROUPS)

        router_ps, routed_in, exp_in, exp_done = sem("moe_router_ps"), sem("moe_routed_in"), sem("moe_exp_in"), sem("moe_exp_done")
        h_ps, h_act, h_ready = sem("moe_h_ps"), sem("moe_h_act"), sem("moe_h_ready")
        y_done, combined, h3_read = sem("moe_y_done"), sem("moe_combined"), sem("moe_h3_read")
        moe_at = dict(phase=0, h_ps=0, h_act=0, h_ready=0, y_done=0, combined=0)

        def load_experts(eng, F, swiglu):
            w1_d, w3_d, w2_d, b2_d, router_d = F
            load(eng, "f", w1[:, 0:w1_d.shape[1]], w1_d)
            load(eng, "f", w2[:, 0:w2_d.shape[1]], w2_d)
            load(eng, "f", router_w[:, :], router_d)
            if swiglu:
                load(eng, "f", w3[:, 0:w3_d.shape[1]], w3_d)
            else:
                load(eng, "f", b2_row[0:1, :], b2_d)

        def experts(tiles, func, swiglu, gating, next_loads=None, add_tokens=False):
            J = len(tiles)
            AHEAD = 2
            HB = 4
            assert J % HB == 0
            p0 = moe_at["phase"]
            ps0, act0, ready0, y0, comb0 = (moe_at[n] for n in ("h_ps", "h_act", "h_ready", "y_done", "combined"))
            moe_at["phase"] += 1
            moe_at["h_ps"] += J * GROUPS
            moe_at["h_act"] += J * GROUPS + (0 if swiglu else AHEAD)
            moe_at["h_ready"] += J * GROUPS + AHEAD if swiglu else 0
            moe_at["y_done"] += J * GROUPS + HB
            moe_at["combined"] += GROUPS + 1
            ready, r0 = (h_ready, ready0) if swiglu else (h_act, act0)
            hid = act_h if not swiglu else mul_h

            with nc.Block() as block:
                @block.tensor
                def _(pe):
                    pe.wait_ge(loaded["f"], want["f"])
                    for t in range(NT):
                        last = nc.tensor.matmul(ps[:, 4, t * E:(t + 1) * E], xn_ch[:, t * P:(t + 1) * P],
                                                router_w[:, :], start=True, stop=True)
                    last.then_inc(router_ps, 1)
                    with pe.Fori(0, GROUPS) as g:
                        xg = xn_ch[:, bass.ds(g * GTOK, GTOK)]

                        def hidden(j):
                            col = tiles[j][0]
                            pe.wait_ge(ready, g * J + (r0 + j + 1))
                            last = nc.tensor.matmul(ps[:, j % AHEAD, :], w1[:, col:col + P], xg, start=True, stop=True)
                            if swiglu:
                                last = nc.tensor.matmul(ps[:, AHEAD + j % AHEAD, :], w3[:, col:col + P], xg,
                                                        start=True, stop=True)
                            last.then_inc(h_ps, 1)

                        hidden(0)
                        for j, (_, w2_col, o, width, first, final) in enumerate(tiles):
                            if j + 1 < J:
                                hidden(j + 1)
                            if j == 0:
                                pe.wait_ge(combined, g + (comb0 + 1))
                                if not swiglu:
                                    for t in range(TPG):
                                        nc.tensor.matmul(ps[:, 4 + t, :], row0[:, :], b2_row[:, :],
                                                         start=True, stop=False, skip_group_check=True)
                            pe.wait_ge(ready, g * J + (r0 + AHEAD + j + 1))
                            for t in range(TPG):
                                last = nc.tensor.matmul(ps[:, 4 + t, o:o + width],
                                                        hid[:, j % HB, t * P:(t + 1) * P],
                                                        w2[:, w2_col:w2_col + width],
                                                        start=first and swiglu, stop=final,
                                                        skip_group_check=True)
                            last.then_inc(y_done, 1)

                @block.scalar
                def _(act):
                    act.wait_ge(exp_in, p0 + 1)
                    nc.scalar.activation(rt[:, 1, :, :], rt[:, 1, :, :], ACT.Exp).then_inc(exp_done, 1)
                    if not swiglu:
                        act.sem_inc(h_act, AHEAD)
                    with act.Fori(0, GROUPS) as g:
                        for j in range(J):
                            act.wait_ge(h_ps, g * J + (ps0 + j + 1))
                            if swiglu:
                                act.wait_ge(h_ready, g * J + (ready0 + j + 1))
                            else:
                                act.wait_ge(y_done, g * J + (y0 + j + 1))
                            nc.scalar.activation(act_h[:, j % (AHEAD if swiglu else HB), :], ps[:, j % AHEAD, :],
                                                 func).then_inc(h_act, 1)

                @block.vector
                def _(dve):
                    c = dve_chain.on(dve)
                    dve.wait_ge(router_ps, p0 + 1)
                    logits, ex = rt[:, 0, :, :], rt[:, 1, :, :]
                    hot1, hot2, tmp, rest = (rt[:, n, :, :] for n in (2, 3, 4, 5))
                    mx, r1, total, top, inv, inv2 = (rs[:, n, :] for n in range(6))

                    def wide(v):
                        return v.unsqueeze(2).broadcast_to((P, NT, E))

                    ranks = rank[:, :].unsqueeze(1).broadcast_to((P, NT, E))
                    nc.vector.tensor_copy(logits, ps[:, 4, 0:NT * E].rearrange(
                        "p (t e) -> p t e", e=E)).then_inc(combined, 1)
                    dve.wait_ge(combined, comb0 + 1)
                    if swiglu:
                        dve.sem_inc(h_ready, AHEAD)
                    c.link(nc.vector.tensor_reduce(mx, logits, AX.X, ALU.max))
                    nc.vector.tensor_tensor(ex, logits, wide(mx), ALU.subtract).then_inc(exp_in, 1)

                    def one_hot(hot, values):
                        c.link(nc.vector.tensor_tensor(tmp, values, wide(mx), ALU.is_equal))
                        c.link(nc.vector.tensor_tensor(tmp, tmp, ranks, ALU.mult))
                        c.link(nc.vector.tensor_reduce(r1, tmp, AX.X, ALU.max))
                        c.link(nc.vector.tensor_tensor(hot, ranks, wide(r1), ALU.is_equal))

                    one_hot(hot1, logits)
                    c.link(nc.vector.scalar_tensor_tensor(rest, hot1, -3e38, logits, ALU.mult, ALU.add))
                    c.link(nc.vector.tensor_reduce(mx, rest, AX.X, ALU.max))
                    one_hot(hot2, rest)
                    c.link(nc.vector.tensor_tensor(hot1, hot1, hot2, ALU.add))
                    dve.wait_ge(exp_done, p0 + 1)
                    c.link(nc.vector.tensor_tensor(hot1, hot1, ex, ALU.mult))
                    c.link(nc.vector.tensor_reduce(total, ex, AX.X, ALU.add))
                    c.link(nc.vector.tensor_reduce(top, hot1, AX.X, ALU.add))
                    if gating == "two":
                        c.link(nc.vector.reciprocal(inv, top))
                    else:
                        c.link(nc.vector.reciprocal(inv, total))
                    if gating in ("plus", "floor"):
                        op, eps = (ALU.add, 1e-9) if gating == "plus" else (ALU.max, 1e-12)
                        c.link(nc.vector.tensor_tensor(top, top, inv, ALU.mult))
                        c.link(nc.vector.tensor_scalar(top, top, eps, None, op))
                        c.link(nc.vector.reciprocal(inv2, top))
                        c.link(nc.vector.tensor_tensor(inv, inv, inv2, ALU.mult))
                    c.link(nc.vector.tensor_tensor(gates[:, :, :], hot1, wide(inv), ALU.mult))
                    if add_tokens:
                        c.link(nc.vector.tensor_tensor(x_tok[:, :, :], x_tok[:, :, :], xn_tok[:, :, :], ALU.add))

                    with dve.Fori(0, GROUPS) as g:
                        c.loop(g, 3 * TPG)
                        if swiglu:
                            for j in range(J):
                                dve.wait_ge(h_act, g * J + (act0 + j + 1))
                                dve.wait_ge(y_done, g * J + (y0 + j + 1))
                                nc.vector.tensor_tensor(mul_h[:, j % HB, :], act_h[:, j % AHEAD, :],
                                                        ps[:, AHEAD + j % AHEAD, :], ALU.mult).then_inc(h_ready, 1)
                        dve.wait_ge(y_done, g * J + (y0 + HB + J))
                        for t in range(TPG):
                            c.link(nc.vector.tensor_tensor(
                                weighted[:, :, :], ps[:, 4 + t, :].rearrange("p (e c) -> p e c", e=E),
                                gates[:, bass.ds(g * TPG + t, 1), :].rearrange("p a e -> p (a e)")
                                .unsqueeze(2).broadcast_to((P, E, C)), ALU.mult))
                            if t == TPG - 1:
                                dve.sem_inc(combined, 1)
                            c.link(nc.vector.tensor_reduce(expert_sum[:, :],
                                                           weighted[:, :, :].rearrange("p e c -> p c e"), AX.X, ALU.add))
                            xt = x_tok[:, bass.ds(g * TPG + t, 1), :].rearrange("p a c -> p (a c)")
                            c.link(nc.vector.tensor_tensor(xt, xt, expert_sum[:, :], ALU.add))
                    c.end(GROUPS)

                @block.gpsimd
                def _(pool):
                    pool.sem_inc(y_done, HB)

            if next_loads is not None:
                with nc.Block() as block:
                    @block.sync
                    def _(sp):
                        load_experts(sp, next_loads, False)

        def relative_bias():
            tab = sbl("tab", [3, REL * REL])
            m1 = sbl("m1", [3, 32])
            m2 = sbl("m2", [32, E])
            hid = sbl("bias_hid", [32, REL * REL])
            table = sbl("bias_table", [HEADS1, REL * REL])
            b_ps, b_hid, b_ps2, b_sig, b_tab, b_dram = (sem(f"bias_{n}") for n in ("ps", "hid", "ps2", "sig", "tab", "dram"))
            cuts = [(0, BANK), (BANK, REL * REL)]
            with nc.Block() as block:
                @block.sync
                def _(sp):
                    for dst, src in ((tab, L1["tab"]), (m1, L1["m1"]), (m2, L1["m2"])):
                        load(sp, "bias", dst[:, :], src)
                    sp.wait_ge(b_tab, 1)
                    bands = L1["scratch"]
                    for j in range(SIDE):
                        sp.dma_start(bands[j, :, :, :], table[:, :].rearrange("h (a b) -> h a b", b=REL)
                                     [:, :, SIDE - 1 - j:REL - j]).then_inc(b_dram, 16)
                    sp.wait_ge(b_dram, 16 * SIDE)
                    for i in range(SIDE):
                        r0 = i % (SIDE // 2) * SIDE
                        load(sp, "l1", rel_bias[r0:r0 + SIDE, i // (SIDE // 2), :, :],
                             bands[:, :, SIDE - 1 - i:REL - i, :].rearrange("j h k l -> j h (k l)"))

                @block.gpsimd
                def _(pool):
                    c = pool_chain.on(pool)
                    c.link(nc.gpsimd.memset(row0[:, :], 0.0))
                    c.link(nc.gpsimd.memset(row0[0:1, :], 1.0))
                    nc.gpsimd.memset(b2_row[:, :], 0.0)

                @block.tensor
                def _(pe):
                    pe.wait_ge(loaded["bias"], 48)
                    for k, (a, b) in enumerate(cuts):
                        last = nc.tensor.matmul(ps[0:32, k, 0:b - a], m1[:, :], tab[:, a:b], start=True, stop=True)
                    last.then_inc(b_ps, 1)
                    pe.wait_ge(b_hid, 1)
                    for k, (a, b) in enumerate(cuts):
                        last = nc.tensor.matmul(ps[0:HEADS1, 2 + k, 0:b - a], m2[:, :], hid[:, a:b], start=True, stop=True)
                    last.then_inc(b_ps2, 1)

                @block.scalar
                def _(act):
                    act.wait_ge(b_ps, 1)
                    for k, (a, b) in enumerate(cuts):
                        last = nc.scalar.activation(hid[:, a:b], ps[0:32, k, 0:b - a], ACT.Relu)
                    last.then_inc(b_hid, 1)
                    act.wait_ge(b_ps2, 1)
                    for k, (a, b) in enumerate(cuts):
                        last = nc.scalar.activation(table[:, a:b], ps[0:HEADS1, 2 + k, 0:b - a], ACT.Sigmoid)
                    last.then_inc(b_sig, 1)

                @block.vector
                def _(dve):
                    dve.wait_ge(b_sig, 1)
                    nc.vector.tensor_scalar(table[:, :], table[:, :], -16.0, None, ALU.mult).then_inc(b_tab, 1)

        def attention():
            qkv_w = sbl("qkv_w", [KC, 3 * C])
            proj_w = sbl("proj_w", [KC, C])
            scale = sbl("scale", [P, 2 * HEADS1])
            x_grp = sbl("x1_grp", [KC, GTOK])
            qk = sbl("qk", [P, NT, 2 * C])
            free = E * H_L1
            QK_T = B * 8 * P // 2
            qk_t = w13[:, free:free + QK_T].bitcast(F16).rearrange("p (b n) -> p b n", b=B)
            norm = w13[:, free + QK_T:free + QK_T + 6 * NT * HEADS1].rearrange(
                "p (k t h) -> p k t h", k=3, t=NT)
            parts = sbl("parts", [P, 1, TPG, 2, HEADS1, 4, DH1], F16)
            low = sbl("low", [P, TPG, 2 * C])
            qk_b = sbl("qk_b", [P, 2, 2, 2, 2, P], F16)
            prob = sbl("prob", [P, 2, 2, N])
            nmax = sbl("nmax", [P, 2, 2])
            prob_t = sbl("prob_t", [P, 2, 4 * P])
            inv_sum = sbl("inv_sum", [P, 2, HEADS1])
            o_tok = sbl("o_tok", [P, 2, HEADS1, DH1])
            o_ch = sbl("o_ch", [KC, N])

            x_copied, qkv_ps, qkv_copied, qk_sq, sums = (sem(f"l1_{n}") for n in ("x_copied", "qkv_ps", "qkv_copied", "qk_sq", "sums"))
            setup, w_ready = sem("l1_setup"), sem("l1_w_ready")
            rooted, inverted = sem("l1_rooted"), sem("l1_inverted")
            split, turned, t_copied = sem("l1_split"), sem("l1_turned"), sem("l1_t_copied")

            with nc.Block() as block:
                @block.sync
                def _(sp):
                    load(sp, "l1", qkv_w[:, :], L1["qkv_w"])
                    load(sp, "l1", proj_w[:, :], L1["proj_w"])
                    load(sp, "l1", scale[:, :], L1["scale"].unsqueeze(0).broadcast_to((P, 2 * HEADS1)))

                @block.gpsimd
                def _(pool):
                    pool_chain.on(pool).link(nc.gpsimd.memset(vals[:, :, :, DH1:VW], 1.0))
                    nc.gpsimd.memset(o_ch[C:KC, :], 1.0)

                @block.scalar
                def _(act):
                    with act.Fori(0, GROUPS) as g:
                        nc.scalar.copy(x_grp[:, :], xn_ch[:, bass.ds(g * GTOK, GTOK)]).then_inc(x_copied, 1)
                        act.wait_ge(qkv_ps, g + 1)
                        nc.scalar.copy(qk[:, bass.ds(g * TPG, TPG), :], ps[:, 0:TPG, 0:2 * C])
                        nc.scalar.copy(vals[:, bass.ds(g * TPG, TPG), :, 0:DH1],
                                       ps[:, 0:TPG, 2 * C:3 * C].rearrange("p t (h d) -> p t h d", d=DH1))
                        nc.scalar.activation(sq_qk[:, :, :], ps[:, 0:TPG, 0:2 * C], ACT.Square).then_inc(qk_sq, 1)
                        act.wait_ge(sums, g + 1)

                @block.tensor
                def _(pe):
                    pe.wait_ge(w_ready, 3)
                    with pe.Fori(0, GROUPS) as g:
                        pe.wait_ge(x_copied, g + 1)
                        for t in range(TPG):
                            last = nc.tensor.matmul(ps[:, t, 0:3 * C], x_grp[:, t * P:(t + 1) * P], qkv_w[:, :],
                                                    start=True, stop=True)
                        last.then_inc(qkv_ps, 1)

                @block.vector
                def _(dve):
                    dve.wait_ge(loaded["l1"], want["l1"])
                    for n in range(3):
                        w = qkv_w[0:C, n * C:(n + 1) * C]
                        nc.vector.tensor_tensor(w, w, idn[0:C, 0:C], ALU.add).then_inc(w_ready, 1)
                    with dve.Fori(0, GROUPS) as g:
                        dve.wait_ge(qk_sq, g + 1)
                        nc.vector.tensor_reduce(norm[:, 0, bass.ds(g * TPG, TPG), :],
                                                sq_qk[:, :, :].rearrange("p t (h d) -> p t h d", d=DH1),
                                                AX.X, ALU.add).then_inc(sums, 1)

            with nc.Block() as block:
                @block.vector
                def _(dve):
                    c = dve_chain.on(dve)
                    ss, y, t = norm[:, 0, :, :], norm[:, 1, :, :], norm[:, 2, :, :]
                    nc.vector.tensor_scalar(ss, ss, 1e-24, None, ALU.max).then_inc(setup, 1)
                    sq_ = scale[:, 0:HEADS1]
                    dve.wait_ge(setup, 1)
                    nc.vector.tensor_scalar(sq_, sq_, float(np.log(np.float32(1.0 / 0.01))), None, ALU.min).then_inc(setup, 1)
                    dve.wait_ge(rooted, 2)
                    c.link(nc.vector.tensor_scalar(sq_, sq_, -1.0, None, ALU.mult))
                    c.link(nc.vector.reciprocal(y, y))
                    c.link(nc.vector.tensor_tensor(t, y, y, ALU.mult))
                    c.link(nc.vector.tensor_tensor(t, t, ss, ALU.mult))
                    c.link(nc.vector.tensor_scalar(t, t, -0.5, 1.5, ALU.mult, ALU.add))
                    c.link(nc.vector.tensor_tensor(y, y, t, ALU.mult))
                    c.link(nc.vector.tensor_tensor(y, y, scale[:, :].unsqueeze(1).broadcast_to((P, NT, 2 * HEADS1)),
                                                   ALU.mult))

                @block.scalar
                def _(act):
                    act.wait_ge(setup, 1)
                    nc.scalar.activation(norm[:, 1, :, :], norm[:, 0, :, :], ACT.Sqrt).then_inc(rooted, 1)
                    act.wait_ge(setup, 2)
                    nc.scalar.activation(scale[:, 0:HEADS1], scale[:, 0:HEADS1], ACT.Exp).then_inc(rooted, 1)

            with nc.Block() as block:
                @block.vector
                def _(dve):
                    c = dve_chain.on(dve)
                    qk5 = low[:, :, :].rearrange("p t (w h d) -> p t w h d", w=2, d=DH1)
                    with dve.Fori(0, GROUPS) as g:
                        c.loop(g, 5)
                        c.link(nc.vector.tensor_tensor(
                            low[:, :, :].rearrange("p t (h d) -> p t h d", d=DH1),
                            qk[:, bass.ds(g * TPG, TPG), :].rearrange("p t (h d) -> p t h d", d=DH1),
                            norm[:, 1, bass.ds(g * TPG, TPG), :].unsqueeze(3).broadcast_to((P, TPG, 2 * HEADS1, DH1)),
                            ALU.mult))
                        dve.wait_ge(turned, g + 1)
                        for w in range(2):
                            src = qk5[:, :, w, :, :]
                            c.link(nc.vector.tensor_copy(parts[:, 0, :, w, :, 0, :], src))
                            hi, lo = (2, 1) if w == 0 else (1, 2)
                            nc.vector.tensor_copy(parts[:, 0, :, w, :, hi, :], parts[:, 0, :, w, :, 0, :])
                            c.link(nc.vector.tensor_tensor(parts[:, 0, :, w, :, lo, :], src,
                                                           parts[:, 0, :, w, :, 0, :], ALU.subtract))
                            last = nc.vector.tensor_copy(parts[:, 0, :, w, :, 3, :], parts[:, 0, :, w, :, lo, :])
                        last.then_inc(split, 1)
                    c.end(GROUPS)

                @block.tensor
                def _(pe):
                    pe.sem_inc(turned, 1)
                    with pe.Fori(0, GROUPS) as g:
                        pe.wait_ge(split, g + 1)
                        pe.wait_ge(t_copied, g + 1)
                        for b in range(2):
                            for w in range(2):
                                for s in range(2):
                                    for j in range(2):
                                        n = (w * 2 + s) * 2 + j
                                        last = nc.tensor.transpose(
                                            ps[:, b, n * (P // 2):(n + 1) * (P // 2)].bitcast(F16),
                                            parts[:, 0, 2 * b + j, w, 4 * s:4 * s + 4, :, :].rearrange("p h a d -> p (h a d)"),
                                            idn16[:, :])
                        last.then_inc(turned, 1)

                @block.scalar
                def _(act):
                    nc.scalar.copy(idn16[:, :], idn[:, :]).then_inc(t_copied, 1)
                    with act.Fori(0, GROUPS) as g:
                        act.wait_ge(turned, g + 2)
                        for b in range(2):
                            last = nc.scalar.copy(qk_t[:, bass.ds(2 * g + b, 1), :].rearrange("p a n -> p (a n)"),
                                                  ps[:, b, :].bitcast(F16))
                        last.then_inc(t_copied, 1)

            fetched = [sem("l1_fetched_even"), sem("l1_fetched_odd")]
            s_ps, shifted, exped = sem("l1_s_ps"), sem("l1_shifted"), sem("l1_exped")
            pt_ps, pt_dve, pt_act, o_ps = sem("l1_pt_ps"), sem("l1_pt_dve"), sem("l1_pt_act"), sem("l1_o_ps")
            o_ready, ot_ps, ot_copied, out_ps, out_added = (sem(f"l1_{n}") for n in ("o_ready", "ot_ps", "ot_copied", "out_ps", "out_added"))
            scores_seen, outputs_seen = sem("l1_scores_seen"), sem("l1_outputs_seen")
            UNITS = 2 * HEADS1 // 2
            o_view = ps[:, 4, 0:2 * HEADS1 * VW].rearrange("p (t h v) -> p t h v", t=2, v=VW)

            with nc.Block() as block:
                @block.sync
                def _(sp):
                    with sp.Fori(0, B // 2) as i:
                        for q in range(2):
                            sp.wait_ge(out_added, 2 * i + q + 1)
                            sp.dma_start(qk_b[:, q, :, :, :, :].rearrange("p w s j n -> p (w s j n)"),
                                         qk_t[:, bass.ds(2 * i + q, 1), :].rearrange("p a n -> p (a n)")).then_inc(fetched[q], 16)

                @block.tensor
                def _(pe):
                    with pe.Fori(0, B // 2) as i:
                        for q in range(2):
                            u0 = i * (2 * UNITS) + q * UNITS
                            pe.wait_ge(fetched[q], 16 * i + 16)
                            for k in range(UNITS + 2):
                                if k < UNITS:
                                    nt, hp = k // 4, k % 4
                                    for a in range(2):
                                        h = hp + 4 * a
                                        r = 32 * (h % 4)
                                        last = nc.tensor.matmul(
                                            ps[:, k % 2, a * N:(a + 1) * N],
                                            qk_b[r:r + 32, q, 0, h // 4, nt, :],
                                            qk_b[r:r + 32, q, 1, h // 4, :, :].rearrange("p j n -> p (j n)"),
                                            start=True, stop=True)
                                    last.then_inc(s_ps, 1)
                                if 1 <= k <= UNITS:
                                    u = k - 1
                                    pe.wait_ge(exped, u0 + k)
                                    for a in range(2):
                                        for m in range(2):
                                            last = nc.tensor.transpose(ps[:, 2 + u % 2, (2 * a + m) * P:(2 * a + m + 1) * P],
                                                                       prob[:, u % 2, a, m * P:(m + 1) * P], idn[:, :])
                                    last.then_inc(pt_ps, 1)
                                if k >= 2:
                                    u = k - 2
                                    nt, hp = u // 4, u % 4
                                    pe.wait_ge(pt_act if u % 2 else pt_dve, i * UNITS + (q * (UNITS // 2) + u // 2 + 1))
                                    for a in range(2):
                                        h = hp + 4 * a
                                        for m in range(2):
                                            v = vals[:, bass.ds(4 * i + 2 * q + m, 1), h, :].rearrange("p a v -> p (a v)")
                                            last = nc.tensor.matmul(o_view[:, nt, h, :],
                                                                    prob_t[:, u % 2, (2 * a + m) * P:(2 * a + m + 1) * P],
                                                                    v, start=(m == 0), stop=(m == 1))
                            last.then_inc(o_ps, 1)
                            pe.wait_ge(o_ready, 2 * i + q + 1)
                            pe.sem_inc(outputs_seen, 1)
                            for j in range(2):
                                last = nc.tensor.transpose(ps[0:C, 5, j * P:(j + 1) * P],
                                                           o_tok[:, j, :, :].rearrange("p h d -> p (h d)"), idn[:, :])
                            last.then_inc(ot_ps, 1)
                            pe.wait_ge(ot_copied, 2 * i + q + 1)
                            for j in range(2):
                                last = nc.tensor.matmul(ps[:, 6, j * C:(j + 1) * C], o_ch[:, j * P:(j + 1) * P],
                                                        proj_w[:, :], start=True, stop=True)
                            last.then_inc(out_ps, 1)

                @block.scalar
                def _(act):
                    with act.Fori(0, B // 2) as i:
                        for q in range(2):
                            u0 = i * (2 * UNITS) + q * UNITS
                            for k in range(UNITS + 1):
                                if k < UNITS:
                                    act.wait_ge(shifted, u0 + k + 1)
                                    for a in range(2):
                                        last = nc.scalar.activation(prob[:, k % 2, a, :], prob[:, k % 2, a, :], ACT.Exp,
                                                                    bias=nmax[:, k % 2, a:a + 1], scale=-1.0)
                                    last.then_inc(exped, 1)
                                if k >= 1 and (k - 1) % 2 == 1:
                                    u = k - 1
                                    act.wait_ge(pt_ps, u0 + k)
                                    nc.scalar.copy(prob_t[:, u % 2, :], ps[:, 2 + u % 2, :]).then_inc(pt_act, 1)
                            act.wait_ge(ot_ps, 2 * i + q + 1)
                            nc.scalar.copy(o_ch[0:C, :], ps[0:C, 5, 0:N]).then_inc(ot_copied, 1)

                @block.vector
                def _(dve):
                    c = dve_chain.on(dve)
                    dve.sem_inc(out_added, 2)
                    with dve.Fori(0, B // 2) as i:
                        c.loop(i, 2)
                        for q in range(2):
                            u0 = i * (2 * UNITS) + q * UNITS
                            for k in range(UNITS + 1):
                                if k < UNITS:
                                    nt, hp = k // 4, k % 4
                                    dve.wait_ge(s_ps, u0 + k + 1)
                                    dve.sem_inc(scores_seen, 1)
                                    for a in range(2):
                                        last = nc.vector.tensor_tensor_reduce(
                                            out=prob[:, k % 2, a, :], in0=ps[:, k % 2, a * N:(a + 1) * N],
                                            in1=rel_bias[:, nt, hp + 4 * a, :], scale=1.0, scalar=3e38,
                                            op0=ALU.add, op1=ALU.min, accum_out=nmax[:, k % 2, a:a + 1])
                                    last.then_inc(shifted, 1)
                                if k >= 1 and (k - 1) % 2 == 0:
                                    u = k - 1
                                    dve.wait_ge(pt_ps, u0 + k)
                                    nc.vector.tensor_copy(prob_t[:, u % 2, :], ps[:, 2 + u % 2, :]).then_inc(pt_dve, 1)
                            dve.wait_ge(o_ps, 2 * i + q + 1)
                            c.link(nc.vector.reciprocal(inv_sum[:, :, :], o_view[:, :, :, DH1]))
                            nc.vector.tensor_tensor(o_tok[:, :, :, :], o_view[:, :, :, 0:DH1],
                                                    inv_sum[:, :, :].unsqueeze(3).broadcast_to((P, 2, HEADS1, DH1)),
                                                    ALU.mult).then_inc(o_ready, 1)
                            dve.wait_ge(out_ps, 2 * i + q + 1)
                            xb = x_tok[:, bass.ds(4 * i + 2 * q, 2), :]
                            nc.vector.tensor_tensor(xb, xb, ps[:, 6, 0:2 * C].rearrange("p (t c) -> p t c", t=2),
                                                    ALU.add).then_inc(out_added, 1)
                    c.end(B // 2)

        def similarity():
            map_w = sbl("map_w", [KC, C])
            x_one = sbl("x2_one", [KC, GTOK])
            x_zero = sbl("x2_zero", [KC, GTOK])
            x_sq = sbl("x2_sq", [KC, GTOK])
            ones = sbl("x2_ones", [KC, P])
            tx = sbl("tx", [P, TPG, C])
            norm_p = sbl("norm_p", [P, TPG])
            dots = sbl("dots", [P, TPG, N])
            inv = sbl("inv_norm", [P, TPG, N])
            copied, tx_ps, nrm_ps, dot_ps, relu_d, tx_copied, sim, o_ps, ones_set = (
                sem(f"l2_{n}") for n in ("copied", "tx_ps", "nrm_ps", "dot_ps", "relu", "tx_copied", "sim", "o_ps", "ones_set"))
            with nc.Block() as block:
                @block.sync
                def _(sp):
                    load(sp, "l2", map_w[:, :], L2)

                @block.scalar
                def _(act):
                    nc.scalar.activation(x_zero[C:KC, :], xn_ch[C:KC, 0:GTOK], ACT.Copy, scale=0.0)
                    with act.Fori(0, GROUPS) as g:
                        xg = xn_ch[:, bass.ds(g * GTOK, GTOK)]
                        nc.scalar.copy(x_one[:, :], xg)
                        nc.scalar.copy(x_zero[0:C, :], xn_ch[0:C, bass.ds(g * GTOK, GTOK)])
                        nc.scalar.activation(x_sq[:, :], xg, ACT.Square).then_inc(copied, 1)
                        act.wait_ge(tx_ps, g + 1)
                        nc.scalar.copy(tx[:, :, :], ps[:, 6, 0:TPG * C].rearrange("p (t c) -> p t c", t=TPG)).then_inc(tx_copied, 1)
                        act.wait_ge(dot_ps, g + 1)
                        nc.scalar.activation(dots[:, :, :], ps[:, 0:2, :].rearrange("p b (t n) -> p (b t) n", n=N),
                                             ACT.Relu).then_inc(relu_d, 1)

                @block.tensor
                def _(pe):
                    pe.wait_ge(loaded["l2"], want["l2"])
                    pe.wait_ge(ones_set, 1)
                    with pe.Fori(0, GROUPS) as g:
                        pe.wait_ge(copied, g + 1)
                        nc.tensor.matmul(ps[:, 4, :], ones[:, :], x_sq[:, :], start=True, stop=True)
                        for t in range(TPG):
                            last = nc.tensor.matmul(ps[:, 5, t:t + 1], x_sq[:, t * P:(t + 1) * P], ones[:, 0:1],
                                                    start=True, stop=True)
                        last.then_inc(nrm_ps, 1)
                        for t in range(TPG):
                            b = t // 2
                            last = nc.tensor.matmul(ps[:, t // 2, (t % 2) * N:(t % 2 + 1) * N],
                                                    x_zero[:, t * P:(t + 1) * P], x_one[:, b * N:(b + 1) * N],
                                                    start=True, stop=True)
                        last.then_inc(dot_ps, 1)
                        for t in range(TPG):
                            last = nc.tensor.matmul(ps[:, 6, t * C:(t + 1) * C], x_one[:, t * P:(t + 1) * P],
                                                    map_w[:, :], start=True, stop=True)
                        last.then_inc(tx_ps, 1)
                        pe.wait_ge(tx_copied, g + 1)
                        pe.wait_ge(sim, g + 1)
                        for t in range(TPG):
                            for j in range(2):
                                q = 2 * (t // 2) + j
                                last = nc.tensor.matmul(ps[:, 7, t * C:(t + 1) * C],
                                                        dots[:, q, (t % 2) * P:(t % 2 + 1) * P], tx[:, q, :],
                                                        start=(j == 0), stop=(j == 1))
                        last.then_inc(o_ps, 1)

                @block.vector
                def _(dve):
                    c = dve_chain.on(dve)
                    c.link(nc.vector.memset(ones[:, :], 1.0))
                    nc.vector.memset(ones[C:KC, :], 0.0).then_inc(ones_set, 1)
                    with dve.Fori(0, GROUPS) as g:
                        c.loop(g, 5)
                        dve.wait_ge(nrm_ps, g + 1)
                        c.link(nc.vector.tensor_copy(norm_p[:, :], ps[:, 5, 0:TPG]))
                        for t in range(TPG):
                            last = nc.vector.tensor_scalar(inv[:, t, :], ps[:, 4, (t // 2) * N:(t // 2 + 1) * N],
                                                           norm_p[:, t:t + 1], 1e-16, ALU.mult, ALU.max)
                        c.link(last)
                        c.link(nc.vector.reciprocal(inv[:, :, :], inv[:, :, :]))
                        dve.wait_ge(relu_d, g + 1)
                        c.link(nc.vector.tensor_tensor(inv[:, :, :], inv[:, :, :], dots[:, :, :], ALU.mult))
                        nc.vector.tensor_tensor(dots[:, :, :], inv[:, :, :], dots[:, :, :], ALU.mult).then_inc(sim, 1)
                        dve.wait_ge(o_ps, g + 1)
                        xg = x_tok[:, bass.ds(g * TPG, TPG), :]
                        c.link(nc.vector.tensor_tensor(xg, xg, ps[:, 7, 0:TPG * C].rearrange("p (t c) -> p t c", t=TPG),
                                                       ALU.add))
                    c.end(GROUPS)

        def convolution():
            TAPS = 5
            cw = sbl("conv_w", [P, TAPS, C])
            clip = sbl("conv_clip", [P, TAPS, C])
            sign = sbl("conv_sign", [P, TAPS, C])
            img = sbl("conv_img", [P, 2, 2, PADS, SIDE])
            signed, filled, o_ps, w_ready, added = (
                sem(f"l3_{n}") for n in ("signed", "filled", "o_ps", "w_ready", "added"))
            with nc.Block() as block:
                @block.sync
                def _(sp):
                    load(sp, "l3", cw[:, :, :], L3)

                @block.scalar
                def _(act):
                    act.wait_ge(loaded["l3"], 16)
                    nc.scalar.activation(sign[:, :, :], cw[:, :, :], ACT.Sign).then_inc(signed, 1)
                    act.wait_ge(w_ready, 1)
                    with act.Fori(0, B // 2) as i:
                        for q in range(2):
                            act.wait_ge(o_ps, 2 * i + q + 1)
                            src = xn_ch[0:C, bass.ds(i * (2 * N) + q * N, N)].rearrange("c (i j) -> c i j", j=SIDE)
                            nc.scalar.copy(img[0:C, q, 0, 1:SIDE + 1, 1:], src[:, :, :SIDE - 1])
                            nc.scalar.copy(img[C:P, q, 0, 1:SIDE + 1, :], src)
                            nc.scalar.copy(img[0:C, q, 1, 1:SIDE + 1, :SIDE - 1], src[:, :, 1:])
                            nc.scalar.copy(img[C:P, q, 1, 0:SIDE, :SIDE - 1], src[:, :, 1:]).then_inc(filled, 1)

                @block.tensor
                def _(pe):
                    pe.sem_inc(o_ps, 2)
                    pe.wait_ge(w_ready, 1)
                    with pe.Fori(0, B // 2) as i:
                        for q in range(2):
                            pe.wait_ge(filled, 2 * i + q + 1)
                            pe.wait_ge(added, 2 * i + q + 1)
                            for t in range(2):
                                for tap, (side, dy) in enumerate(((0, 0), (0, 1), (0, 2), (1, 0), (1, 2))):
                                    y = dy + t * (SIDE // 2)
                                    last = nc.tensor.matmul(
                                        ps[:, q, t * C:(t + 1) * C],
                                        img[:, q, side, y:y + SIDE // 2, :].rearrange("c i j -> c (i j)"),
                                        cw[:, tap, :], start=(tap == 0), stop=(tap == TAPS - 1))
                            last.then_inc(o_ps, 1)

                @block.vector
                def _(dve):
                    c = dve_chain.on(dve)
                    dve.sem_inc(added, 2)
                    c.link(nc.vector.memset(img[:, :, :, :, :], 0.0))
                    dve.wait_ge(loaded["l3"], 16)
                    c.link(nc.vector.tensor_scalar(clip[:, :, :], cw[:, :, :], 1.0, -1.0, ALU.min, ALU.max))
                    dve.wait_ge(signed, 1)
                    c.link(nc.vector.tensor_tensor(sign[:, :, :], sign[:, :, :], clip[:, :, :], ALU.subtract))
                    nc.vector.tensor_tensor(cw[:, :, :], sign[:, :, :], clip[:, :, :], ALU.add).then_inc(w_ready, 1)
                    with dve.Fori(0, B // 2) as i:
                        for q in range(2):
                            dve.wait_ge(o_ps, 2 * i + q + 3)
                            xb = x_tok[:, bass.ds(4 * i + 2 * q, 2), :]
                            nc.vector.tensor_tensor(xb, xb, ps[:, q, 0:2 * C].rearrange("p (t c) -> p t c", t=2),
                                                    ALU.add).then_inc(added, 1)

        swiglu_tiles = []
        for pair in range(E // 2):
            col, col2 = pair * PAIR0 * P, pair * (PAIR0 + 1) * C
            swiglu_tiles.append((col, col2, pair * 2 * C, 2 * C, True, False))
            for n in range(2 * FULL0):
                e = 2 * pair + n // FULL0
                swiglu_tiles.append((col + (n + 1) * P, col2 + (n + 2) * C, e * C, C, False, n % FULL0 == FULL0 - 1))

        def gelu_tiles(hidden):
            per = hidden // P
            return [((e * per + n) * P, (e * per + n) * C, e * C, C, False, n == per - 1)
                    for e in range(E) for n in range(per)]

        pair_tiles = [(n * P, n * 2 * C, n * 2 * C, 2 * C, False, True) for n in range(E // 2)]

        local = []

        def sbl(name, shape, dt=F32):
            return local[-1].enter_context(nc.sbuf_tensor(name + "_sb", shape, dt))

        def stage(fn):
            with ExitStack() as s:
                local.append(s)
                fn()
                local.pop()

        sq_qk = sq[:, 0:8, :].rearrange("p (t a) c -> p t (a c)", a=2)

        norm_stage(1e-6)
        stage(linear_attention)
        if stop_after >= 2:
            stage(relative_bias)
            norm_stage(1e-5)
            experts(swiglu_tiles, ACT.Silu, True, "plus", next_loads=F1)
        if stop_after >= 3:
            norm_stage(1e-6)
            stage(attention)
        if stop_after >= 4:
            norm_stage(1e-5)
            experts(gelu_tiles(H_L1), ACT.Gelu, False, "all", next_loads=F2)
        if stop_after >= 5:
            norm_stage(1e-6)
            stage(similarity)
        if stop_after >= 6:
            norm_stage(1e-5)
            experts(gelu_tiles(H_L2), ACT.Gelu, False, "two", next_loads=F3)
        if stop_after >= 7:
            norm_stage(1e-6)
            stage(convolution)
        if stop_after >= 8:
            norm_stage(1e-5)
            experts(pair_tiles, ACT.Gelu, False, "floor", add_tokens=True)
        with nc.Block() as block:
            @block.sync
            def _(sp):
                sp.dma_start(out, x_tok[:, :, :]).then_inc(stored, 16)
                sp.wait_ge(stored, 16)
                for key, s in loaded.items():
                    if want[key]:
                        sp.wait_ge(s, want[key])


def layouts(a):
    f = np.float32

    def rows(w_t, bias=None):
        bias = np.zeros(w_t.shape[1], f) if bias is None else bias
        return np.concatenate([w_t, bias[None]], 0)

    def diag(a_, b_):
        z = np.zeros((2 * a_.shape[0], 2 * a_.shape[1]), f)
        z[:a_.shape[0], :a_.shape[1]], z[a_.shape[0]:, a_.shape[1]:] = a_, b_
        return z

    d = {}
    d["x"] = a["x"].reshape(B, C, 2, P).transpose(3, 0, 2, 1).reshape(P, NT, C)
    d["ident"] = np.eye(P, dtype=f)
    d["rank"] = np.tile(np.arange(E, 0, -1, dtype=f), (P, 1))
    wq = a["L0_conv_W_qkv"].T
    d["l0_qv"] = rows(np.concatenate([wq[:, 0:HID0], wq[:, 2 * HID0:]], 1))
    d["l0_k"] = rows(wq[:, HID0:2 * HID0])
    d["l0_out"] = a["L0_conv_W_out"].T
    d["l0_mem"] = rows(a["L0_conv_memory"].reshape(C, MEM))
    head = np.arange(HID0) // DH0
    d["l0_mask"] = (head[:, None] == head[None]).astype(f)
    d["l0_rows"] = np.stack([a["L0_conv_b_out"], a["L0_conv_ln_g"], a["L0_conv_ln_b"]])

    def up(w):
        out = np.zeros((KC, 4 * PAIR0 * P), f)
        for pair in range(E // 2):
            at = pair * PAIR0 * P
            for s in range(2):
                w_t = w[2 * pair + s].T
                out[:C, at + s * C:at + s * C + TAIL0] = w_t[:, FULL0 * P:]
                out[:C, at + (1 + s * FULL0) * P:at + (1 + (s + 1) * FULL0) * P] = w_t[:, :FULL0 * P]
        return out

    down = np.zeros((P, 4 * (PAIR0 + 1) * C), f)
    for pair in range(E // 2):
        at = pair * (PAIR0 + 1) * C
        for s in range(2):
            w_t = a["L0_ffn_w2"][2 * pair + s].T
            down[s * C:s * C + TAIL0, at + s * C:at + (s + 1) * C] = w_t[FULL0 * P:]
            for n in range(FULL0):
                c0 = at + (2 + s * FULL0 + n) * C
                down[:, c0:c0 + C] = w_t[n * P:(n + 1) * P]
    d["f0_w1"], d["f0_w3"], d["f0_w2"] = up(a["L0_ffn_w1"]), up(a["L0_ffn_w3"]), down
    d["f0_router"] = rows(a["L0_ffn_router_w"].T)

    def side_by_side(w):
        return w.transpose(1, 0, 2).reshape(w.shape[1], -1)

    def qkv(n):
        return rows(diag(a[f"L1_conv_{n}1_w"].T, a[f"L1_conv_{n}2_w"].T),
                    np.concatenate([a[f"L1_conv_{n}1_b"], a[f"L1_conv_{n}2_b"]]))

    d["l1_qkv"] = np.concatenate([qkv("q"), qkv("k"), qkv("v")], 1)
    d["l1_proj"] = qkv("proj")
    d["l1_scale"] = np.concatenate([a["L1_conv_logit_scale"].reshape(-1), np.ones(HEADS1, f)])
    r = np.arange(-(SIDE - 1), SIDE).astype(f) / f(SIDE - 1 + 1e-8)
    gh, gw = np.meshgrid(r, r, indexing="ij")
    tab = np.stack([gh, gw]) * f(3.2)
    tab = (np.sign(tab) * (f(1) - np.exp(-np.abs(tab)))).reshape(2, -1)
    d["l1_tab"] = np.concatenate([tab, np.ones((1, REL * REL), f)])[:, ::-1]
    d["l1_m1"] = rows(a["L1_conv_mlp_w1"].T, a["L1_conv_mlp_b1"])
    d["l1_m2"] = a["L1_conv_mlp_w2"].T
    d["f1_w1"] = rows(side_by_side(a["L1_ffn_W1"]), a["L1_ffn_b1"].reshape(-1))
    d["f1_w2"] = side_by_side(a["L1_ffn_W2"])
    d["f1_b2"] = a["L1_ffn_b2"].reshape(1, -1)
    d["f1_router"] = rows(a["L1_ffn_gate_w"], a["L1_ffn_gate_b"])
    d["f2_w1"] = rows(side_by_side(a["L2_ffn_W1"]), a["L2_ffn_b1"].reshape(-1))
    d["f2_w2"] = a["L2_ffn_W2"].reshape(E, H_L2 // P, P, C).transpose(2, 0, 1, 3).reshape(P, -1)
    d["f2_b2"] = a["L2_ffn_b2"].reshape(1, -1)
    d["f2_router"] = rows(a["L2_ffn_Wg"], a["L2_ffn_bg"])
    d["f3_w1"] = rows(side_by_side(a["L3_ffn_w1"]), a["L3_ffn_b1"].reshape(-1))
    d["f3_w2"] = np.concatenate([diag(a["L3_ffn_w2"][e], a["L3_ffn_w2"][e + 1]) for e in range(0, E, 2)], 1)
    d["f3_b2"] = a["L3_ffn_b2"].reshape(1, -1)
    d["f3_router"] = rows(a["L3_ffn_router_w"].T)
    d["l2_map"] = rows(a["L2_conv_W"].T, a["L2_conv_bias"])
    w = a["L3_conv_W"].transpose(1, 2, 3, 0)
    conv = np.zeros((P, 5, C), f)
    conv[:C, 0:3], conv[C:, 0:3] = w[:, :, 0], w[:, :, 1]
    conv[:C, 3], conv[C:, 3], conv[:C, 4] = w[:, 0, 2], w[:, 1, 2], w[:, 2, 2]
    d["l3_conv"] = conv
    return {k: np.ascontiguousarray(v) for k, v in d.items()}


def build(nc, d, out, scratch):
    metaformer(
        nc, d["x"], d["ident"], d["rank"],
        [d["l0_qv"], d["l0_k"], d["l0_out"], d["l0_mem"], d["l0_mask"], d["l0_rows"]],
        (d["f0_w1"], d["f0_w3"], d["f0_w2"], None, d["f0_router"]),
        dict(qkv_w=d["l1_qkv"], proj_w=d["l1_proj"], scale=d["l1_scale"], tab=d["l1_tab"],
             m1=d["l1_m1"], m2=d["l1_m2"], scratch=scratch),
        (d["f1_w1"], None, d["f1_w2"], d["f1_b2"], d["f1_router"]),
        d["l2_map"],
        (d["f2_w1"], None, d["f2_w2"], d["f2_b2"], d["f2_router"]),
        d["l3_conv"],
        (d["f3_w1"], None, d["f3_w2"], d["f3_b2"], d["f3_router"]),
        out)


def kernel(**inputs):
    import concourse.bacc as bacc
    from concourse.bass_utils import run_bass_kernel_spmd

    nc = bacc.Bacc("TRN2", target_bir_lowering=False, num_devices=1)
    arrays = layouts({k: np.asarray(v) for k, v in inputs.items()})
    d = {k: nc.dram_tensor(k, v.shape, mybir.dt.from_np(v.dtype), kind="ExternalInput").ap()
         for k, v in arrays.items()}
    out = nc.dram_tensor("out", (P, NT, C), F32, kind="ExternalOutput").ap()
    scratch = nc.dram_tensor("bias_bands", (SIDE, HEADS1, REL, SIDE), F32, kind="Internal").ap()
    build(nc, d, out, scratch)
    got = run_bass_kernel_spmd(nc, [arrays], core_ids=[0]).results[0]["out"]
    return got.reshape(P, B, 2, C).transpose(1, 3, 2, 0).reshape(B, C, SIDE, SIDE)
```

```python
from contextlib import ExitStack

import numpy as np

import concourse.bass as bass
from concourse import mybir

F32 = mybir.dt.float32
F16 = mybir.dt.float16
BF16 = mybir.dt.bfloat16
ALU = mybir.AluOpType
ACT = mybir.ActivationFunctionType
AX = mybir.AxisListType

P = 128
C = 64
KC = C + 1
B = 16
SIDE = 16
N = SIDE * SIDE
T = B * N
NT = T // P
TPG = 4
GROUPS = NT // TPG
GTOK = TPG * P
BANK = 512
E = 8
HEADS0, DH0, MEM = 8, 16, 16
HID0 = HEADS0 * DH0
HEADS1, DH1 = 8, 8
VW = DH1 + 1
VPAD = 32
H_L0, H_L1, H_L2, H_L3 = 682, 128, 256, 64
FULL0, TAIL0 = H_L0 // P, H_L0 % P
PAIR0 = 2 * FULL0 + 1
REL = 2 * SIDE - 1
PADS = SIDE + 2

TOKEN_SCALE, WEIGHT_SCALE = 1024.0, 64.0
UNSCALE = 1.0 / (TOKEN_SCALE * WEIGHT_SCALE)
STAGE = 512
KG = 72
PARTS_AT = (0, 32, 64)


class Chain:

    def __init__(self, sem):
        self.sem, self.eng, self.base, self.k, self.i, self.per = sem, None, 0, 0, None, 0

    def on(self, eng):
        self.eng = eng
        return self

    def loop(self, i, per):
        self.i, self.per = i, per

    def end(self, times):
        assert self.k == self.per, (self.k, self.per)
        self.base += times * self.per
        self.k, self.i, self.per = 0, None, 0

    def link(self, ins):
        ins.then_inc(self.sem, 1)
        self.k += 1
        at = self.base + self.k
        if self.i is None:
            self.base, self.k = at, 0
        self.eng.wait_ge(self.sem, at if self.i is None else self.i * self.per + at)


def metaformer(nc, x, ident, wt_rank, selector_d, L0, F0, L1, F1, L2, F2, L3, F3, out, stop_after=99):
    ctx = ExitStack()
    with ctx:
        def sb(name, shape, dt=F32):
            return ctx.enter_context(nc.sbuf_tensor(name + "_sb", shape, dt))

        def sem(name):
            return ctx.enter_context(nc.semaphore(name))

        ps = ctx.enter_context(nc.psum_tensor("ps", [P, 8, BANK], F32))

        x_tok = sb("x_tok", [P, NT, C])
        xn_tok = sb("xn_tok", [P, NT, C])
        xn_ch = sb("xn_ch", [KC, T])
        idn = sb("idn", [P, P])
        idn16 = sb("idn16", [P, P], F16)
        rank = sb("rank", [P, E])
        sq = sb("sq", [P, NT, C])
        st = sb("st", [P, 4, NT])
        neg_half = sb("neg_half", [P, 1])
        rt = sb("rt", [P, 6, NT, E])
        rs = sb("rs", [P, 6, NT])
        HIDDEN0 = 4 * PAIR0 * P
        w16 = sb("w16", [P, 2, 2 * HIDDEN0], F16)
        w_stage = sb("w_stage", [P, 4 * STAGE])
        w2 = sb("w2", [P, 4 * PAIR0 * C])
        x16 = sb("x16", [P, T], F16)
        b1_col = sb("b1_col", [P, E * H_L2 // P])
        b2_rows = sb("b2_rows", [KG, C])
        b2_rest = sb("b2_rest", [KG, C])
        b2_parts = sb("b2_parts", [KG, 3, C], BF16)
        router_w = sb("router_w", [P, E])
        router16 = sb("router16", [P, 2, E], F16)
        router_b = sb("router_b", [P, E])
        selector = sb("selector", [KG, E + E // 2, P], BF16)
        gate_parts = sb("gate_parts", [P, NT, KG], BF16)
        gate_t = sb("gate_t", [KG, T], BF16)
        idn_bf = sb("idn_bf", [P, P], BF16)
        rel_bias = sb("rel_bias", [P, 2, HEADS1, N])

        dve_chain = Chain(sem("dve_chain"))
        act_chain = Chain(sem("act_chain"))
        pool_chain = Chain(sem("pool_chain"))
        loaded = {k: sem(f"loaded_{k}") for k in ("x", "const", "l0", "f", "l1", "l2", "l3", "bias")}
        want = dict.fromkeys(loaded, 0)
        stored = sem("stored")

        def load(eng, key, dst, src):
            eng.dma_start(dst, src).then_inc(loaded[key], 16)
            want[key] += 16

        s_centred, s_squared = sem("norm_centred"), sem("norm_squared")
        s_var, s_rstd = sem("norm_var"), sem("norm_rstd")
        s_scaled, s_turned = sem("norm_scaled"), sem("norm_turned")
        norms = [0]

        s_high = sem("norm_high")
        highs = [0]

        def norm_stage(eps, stacked=False):
            hi0 = highs[0]
            if stacked:
                highs[0] += GROUPS
            n0 = norms[0]
            norms[0] += 1
            halves = [slice(h * NT // 2, (h + 1) * NT // 2) for h in range(2)]

            def wide(v, s):
                return v.unsqueeze(2).broadcast_to((P, s.stop - s.start, C))

            with nc.Block() as block:
                if n0 == 0:
                    @block.sync
                    def _(sp):
                        load(sp, "x", x_tok[:, :, :], x)
                        load(sp, "const", idn[:, :], ident)
                        load(sp, "const", rank[:, :], wt_rank)

                @block.vector
                def _(dve):
                    c = dve_chain.on(dve)
                    if n0 == 0:
                        nc.vector.memset(xn_ch[C:KC, :], 1.0)
                        dve.wait_ge(loaded["x"], want["x"])
                    for s in halves:
                        c.link(nc.vector.tensor_reduce(st[:, 0, s], x_tok[:, s, :], AX.X, ALU.add, negate=True))
                        c.link(nc.vector.tensor_scalar(st[:, 0, s], st[:, 0, s], 1.0 / C, None, ALU.mult))
                        nc.vector.tensor_tensor(xn_tok[:, s, :], x_tok[:, s, :], wide(st[:, 0, s], s),
                                                ALU.add).then_inc(s_centred, 1)
                    for h, s in enumerate(halves):
                        dve.wait_ge(s_squared, 2 * n0 + h + 1)
                        c.link(nc.vector.tensor_reduce(st[:, 1, s], sq[:, s, :], AX.X, ALU.add))
                        nc.vector.tensor_scalar(st[:, 2, s], st[:, 1, s], 1.0 / C, float(eps),
                                                ALU.mult, ALU.add).then_inc(s_var, 1)
                    for h, s in enumerate(halves):
                        dve.wait_ge(s_rstd, 2 * n0 + h + 1)
                        nc.vector.tensor_tensor(xn_tok[:, s, :], xn_tok[:, s, :], wide(st[:, 3, s], s),
                                                ALU.mult).then_inc(s_scaled, 1)
                    if stacked:
                        for k in range(GROUPS):
                            tok = slice(k * GTOK, (k + 1) * GTOK)
                            dve.wait_ge(s_high, hi0 + k + 1)
                            nc.vector.scalar_tensor_tensor(x16[C:P, tok], ps[0:C, k, :], TOKEN_SCALE,
                                                           x16[0:C, tok], ALU.mult, ALU.subtract)
                        return
                    for k in range(1, GROUPS, 2):
                        dve.wait_ge(s_turned, GROUPS * n0 + k + 1)
                        nc.vector.tensor_copy(xn_ch[0:C, k * GTOK:(k + 1) * GTOK], ps[0:C, k, :])

                @block.scalar
                def _(act):
                    for h, s in enumerate(halves):
                        act.wait_ge(s_centred, 2 * n0 + h + 1)
                        nc.scalar.activation(sq[:, s, :], xn_tok[:, s, :], ACT.Square).then_inc(s_squared, 1)
                    if stacked:
                        for k in range(GROUPS):
                            act.wait_ge(s_turned, GROUPS * n0 + k + 1)
                            nc.scalar.activation(x16[0:C, k * GTOK:(k + 1) * GTOK], ps[0:C, k, :], ACT.Copy,
                                                 scale=TOKEN_SCALE).then_inc(s_high, 1)
                        return
                    for k in range(0, GROUPS, 2):
                        act.wait_ge(s_turned, GROUPS * n0 + k + 1)
                        nc.scalar.copy(xn_ch[0:C, k * GTOK:(k + 1) * GTOK], ps[0:C, k, :])

                @block.gpsimd
                def _(pool):
                    if n0 == 0:
                        pool_chain.on(pool).link(nc.gpsimd.memset(neg_half[:, :], -0.5))
                    for h, s in enumerate(halves):
                        pool.wait_ge(s_var, 2 * n0 + h + 1)
                        nc.gpsimd.tensor_tensor(st[:, 3, s], st[:, 2, s],
                                                neg_half[:, :].broadcast_to((P, NT // 2)),
                                                ALU.pow).then_inc(s_rstd, 1)

                @block.tensor
                def _(pe):
                    if n0 == 0:
                        pe.wait_ge(loaded["const"], 32)
                    for k in range(GROUPS):
                        if k % (GROUPS // 2) == 0:
                            pe.wait_ge(s_scaled, 2 * n0 + k // (GROUPS // 2) + 1)
                        for t in range(TPG):
                            last = nc.tensor.transpose(ps[0:C, k, t * P:(t + 1) * P],
                                                       xn_tok[:, k * TPG + t, :], idn[:, :])
                        last.then_inc(s_turned, 1)

        def linear_attention():
            qv_w = sbl("qv_w", [KC, 2 * HID0])
            k_w = sbl("k_w", [KC, HID0])
            out_w = sbl("out_w", [HID0, C])
            memory = sbl("memory", [KC, MEM])
            head_mask = sbl("head_mask", [HID0, HID0])
            ln_rows = sbl("ln_rows", [P, 3, C])
            x_grp = sbl("x_grp", [KC, GTOK])
            k_mem = sbl("k_mem", [HID0, MEM])
            v_mem = sbl("v_mem", [MEM, HID0])
            nk_mem = sbl("nk_mem", [HID0, 1])
            nk_max = sbl("nk_max", [HID0, 2, 2])
            v_tok = sbl("v_tok", [P, TPG, HID0])
            k_exp = sbl("k_exp", [HID0, 2, N + MEM])
            k_sum = sbl("k_sum", [HID0, 2, 2])
            k_inv = sbl("k_inv", [HID0, 2])
            kt = sbl("kt", [P, TPG, HID0])
            kt_mem = sbl("kt_mem", [MEM, 2, HID0])
            ctx_t = sbl("ctx_t", [HID0, 2, HID0])
            mix = sbl("mix", [HID0, 2, C])
            q_tok = sbl("q_tok", [P, TPG, HEADS0, DH0])
            q_st = sbl("q_st", [P, 2, TPG, HEADS0])
            q_ch = sbl("q_ch", [HID0, GTOK])
            y_tok = sbl("y_tok", [P, 2, TPG, C])
            y_st = sbl("y_st", [P, 4, TPG])

            mem_ps, mem_kv = sem("l0_mem_ps"), sem("l0_mem_kv")
            x_copied, k_ps, qv_ps = sem("l0_x_copied"), sem("l0_k_ps"), sem("l0_qv_ps")
            k_max, k_exped, v_copied = sem("l0_k_max"), sem("l0_k_exped"), sem("l0_v_copied")
            q_shifted, q_exped, q_ready = sem("l0_q_shifted"), sem("l0_q_exped"), sem("l0_q_ready")
            kt_ps, kt_copied, ktm_copied = sem("l0_kt_ps"), sem("l0_kt_copied"), sem("l0_ktm_copied")
            ctx_ps, ctx_ready, mix_ps, mix_ready = sem("l0_ctx_ps"), sem("l0_ctx_ready"), sem("l0_mix_ps"), sem("l0_mix_ready")
            qt_ps, qt_copied, y_ps = sem("l0_qt_ps"), sem("l0_qt_copied"), sem("l0_y_ps")
            y_sq_in, y_sq, y_var, y_rstd = sem("l0_y_sq_in"), sem("l0_y_sq"), sem("l0_y_var"), sem("l0_y_rstd")

            qv = ps[:, 0:2, :].rearrange("p w (t c) -> p w t c", c=HID0)
            q_ps = qv[:, 0, :, :].rearrange("p t (h d) -> p t h d", d=DH0)
            v_ps = qv[:, 1, :, :]
            kp = ps[:, 2, :].rearrange("p (b n) -> p b n", b=2)

            with nc.Block() as block:
                @block.sync
                def _(sp):
                    for dst, src in ((qv_w, L0[0]), (k_w, L0[1]), (memory, L0[3]), (out_w, L0[2]),
                                     (head_mask, L0[4])):
                        load(sp, "l0", dst[:, :], src)
                    load(sp, "l0", ln_rows[:, :, :], L0[5].unsqueeze(0).broadcast_to((P, 3, C)))

                @block.scalar
                def _(act):
                    c = act_chain.on(act)
                    act.wait_ge(mem_ps, 1)
                    c.link(nc.scalar.copy(k_mem[:, :], ps[:, 4, 0:MEM]))
                    nc.scalar.copy(v_mem[:, :], ps[0:MEM, 4, 128:128 + HID0]).then_inc(mem_kv, 1)
                    with act.Fori(0, GROUPS) as g:
                        nc.scalar.copy(x_grp[:, :], xn_ch[:, bass.ds(g * GTOK, GTOK)]).then_inc(x_copied, 1)
                        act.wait_ge(qv_ps, g + 1)
                        nc.scalar.copy(v_tok[:, :, :], v_ps).then_inc(v_copied, 1)
                        act.wait_ge(k_max, g + 1)
                        for b in range(2):
                            nc.scalar.activation(k_exp[:, b, 0:N], kp[:, b, :], ACT.Exp,
                                                 bias=nk_max[:, b, 1:2], accum_out=k_sum[:, b, 0:1])
                            last = nc.scalar.activation(k_exp[:, b, N:], k_mem[:, :], ACT.Exp,
                                                        bias=nk_max[:, b, 1:2], accum_out=k_sum[:, b, 1:2])
                        last.then_inc(k_exped, 1)
                        act.wait_ge(q_shifted, g + 1)
                        nc.scalar.activation(q_tok[:, :, :, :], q_tok[:, :, :, :], ACT.Exp).then_inc(q_exped, 1)
                        act.wait_ge(kt_ps, g + 1)
                        nc.scalar.copy(kt_mem[:, :, :], ps[0:MEM, 4, 0:2 * HID0].rearrange(
                            "p (b d) -> p b d", b=2)).then_inc(ktm_copied, 1)
                        act.wait_ge(qt_ps, g + 1)
                        nc.scalar.copy(q_ch[:, :], ps[:, 7, :]).then_inc(qt_copied, 1)
                        act.wait_ge(y_sq_in, g + 1)
                        nc.scalar.activation(y_tok[:, 1, :, :], y_tok[:, 0, :, :], ACT.Square).then_inc(y_sq, 1)

                @block.tensor
                def _(pe):
                    pe.wait_ge(loaded["l0"], want["l0"])
                    nc.tensor.matmul(ps[:, 4, 0:MEM], k_w[:, :], memory[:, :], start=True, stop=True)
                    nc.tensor.matmul(ps[0:MEM, 4, 128:128 + HID0], memory[:, :], qv_w[:, HID0:],
                                     start=True, stop=True).then_inc(mem_ps, 1)
                    pe.wait_ge(mem_kv, 1)
                    with pe.Fori(0, GROUPS) as g:
                        pe.wait_ge(x_copied, g + 1)
                        nc.tensor.matmul(ps[:, 2, :], k_w[:, :], x_grp[:, :], start=True, stop=True).then_inc(k_ps, 1)
                        for t in range(TPG):
                            for w in range(2):
                                last = nc.tensor.matmul(qv[:, w, t, :], x_grp[:, t * P:(t + 1) * P],
                                                        qv_w[:, w * HID0:(w + 1) * HID0], start=True, stop=True)
                        last.then_inc(qv_ps, 1)
                        pe.wait_ge(k_exped, g + 1)
                        for b in range(2):
                            for j in range(2):
                                nc.tensor.transpose(ps[:, 3, (2 * b + j) * P:(2 * b + j + 1) * P],
                                                    k_exp[:, b, j * P:(j + 1) * P], idn[:, :])
                            last = nc.tensor.transpose(ps[0:MEM, 4, b * P:(b + 1) * P],
                                                       k_exp[:, b, N:], idn[:, :])
                        last.then_inc(kt_ps, 1)
                        pe.wait_ge(q_ready, g + 1)
                        for t in range(TPG):
                            last = nc.tensor.transpose(ps[:, 7, t * P:(t + 1) * P],
                                                       q_tok[:, t, :, :].rearrange("p h d -> p (h d)"), idn[:, :])
                        last.then_inc(qt_ps, 1)
                        pe.wait_ge(v_copied, g + 1)
                        pe.wait_ge(kt_copied, g + 1)
                        pe.wait_ge(ktm_copied, g + 1)
                        for b in range(2):
                            o = ps[:, 5, b * P:(b + 1) * P]
                            for j in range(2):
                                nc.tensor.matmul(o, v_tok[:, 2 * b + j, :], kt[:, 2 * b + j, :],
                                                 start=(j == 0), stop=False)
                            last = nc.tensor.matmul(o, v_mem[:, :], kt_mem[:, b, :], start=False, stop=True)
                        last.then_inc(ctx_ps, 1)
                        pe.wait_ge(ctx_ready, g + 1)
                        for b in range(2):
                            last = nc.tensor.matmul(ps[:, 6, b * C:(b + 1) * C], ctx_t[:, b, :], out_w[:, :],
                                                    start=True, stop=True)
                        last.then_inc(mix_ps, 1)
                        pe.wait_ge(mix_ready, g + 1)
                        pe.wait_ge(qt_copied, g + 1)
                        for t in range(TPG):
                            last = nc.tensor.matmul(ps[:, 6, 256 + t * C:256 + (t + 1) * C],
                                                    q_ch[:, t * P:(t + 1) * P], mix[:, t // 2, :],
                                                    start=True, stop=True)
                        last.then_inc(y_ps, 1)

                @block.gpsimd
                def _(pool):
                    with pool.Fori(0, GROUPS) as g:
                        pool.wait_ge(y_var, g + 1)
                        nc.gpsimd.tensor_tensor(y_st[:, 3, :], y_st[:, 2, :],
                                                neg_half[:, :].broadcast_to((P, TPG)), ALU.pow).then_inc(y_rstd, 1)

                @block.vector
                def _(dve):
                    c = dve_chain.on(dve)
                    dve.wait_ge(mem_kv, 1)
                    c.link(nc.vector.tensor_reduce(nk_mem[:, :], k_mem[:, :], AX.X, ALU.max, negate=True))
                    y, y2 = y_tok[:, 0, :, :], y_tok[:, 1, :, :]
                    with dve.Fori(0, GROUPS) as g:
                        c.loop(g, 15)

                        def wide4(v, n=C):
                            return v.unsqueeze(2).broadcast_to((P, TPG, n))

                        def rows(r):
                            return ln_rows[:, r, :].unsqueeze(1).broadcast_to((P, TPG, C))

                        dve.wait_ge(k_ps, g + 1)
                        c.link(nc.vector.tensor_reduce(nk_max[:, :, 0], kp, AX.X, ALU.max, negate=True))
                        nc.vector.tensor_tensor(nk_max[:, :, 1], nk_max[:, :, 0],
                                                nk_mem[:, :].broadcast_to((HID0, 2)), ALU.min).then_inc(k_max, 1)
                        dve.wait_ge(qv_ps, g + 1)
                        c.link(nc.vector.tensor_reduce(q_st[:, 0, :, :], q_ps, AX.X, ALU.max))
                        nc.vector.tensor_tensor(q_tok[:, :, :, :], q_ps,
                                                q_st[:, 0, :, :].unsqueeze(3).broadcast_to((P, TPG, HEADS0, DH0)),
                                                ALU.subtract).then_inc(q_shifted, 1)
                        dve.wait_ge(q_exped, g + 1)
                        c.link(nc.vector.tensor_reduce(q_st[:, 0, :, :], q_tok[:, :, :, :], AX.X, ALU.add))
                        c.link(nc.vector.reciprocal(q_st[:, 1, :, :], q_st[:, 0, :, :]))
                        nc.vector.tensor_tensor(q_tok[:, :, :, :], q_tok[:, :, :, :],
                                                q_st[:, 1, :, :].unsqueeze(3).broadcast_to((P, TPG, HEADS0, DH0)),
                                                ALU.mult).then_inc(q_ready, 1)
                        dve.wait_ge(kt_ps, g + 1)
                        nc.vector.tensor_copy(kt[:, :, :], ps[:, 3, :].rearrange(
                            "p (t d) -> p t d", t=TPG)).then_inc(kt_copied, 1)
                        c.link(nc.vector.tensor_tensor(k_inv[:, :], k_sum[:, :, 0], k_sum[:, :, 1], ALU.add))
                        c.link(nc.vector.reciprocal(k_inv[:, :], k_inv[:, :]))
                        c.link(nc.vector.tensor_scalar(k_inv[:, :], k_inv[:, :], DH0 ** -0.5, None, ALU.mult))
                        dve.wait_ge(ctx_ps, g + 1)
                        nc.vector.tensor_tensor(ctx_t[:, :, :],
                                                ps[:, 5, 0:2 * P].rearrange("p (b d) -> p b d", b=2),
                                                head_mask[:, :].unsqueeze(1).broadcast_to((P, 2, HID0)),
                                                ALU.mult).then_inc(ctx_ready, 1)
                        dve.wait_ge(mix_ps, g + 1)
                        for b in range(2):
                            last = nc.vector.tensor_scalar(mix[:, b, :], ps[:, 6, b * C:(b + 1) * C],
                                                           k_inv[:, b:b + 1], None, ALU.mult)
                        last.then_inc(mix_ready, 1)
                        dve.wait_ge(y_ps, g + 1)
                        c.link(nc.vector.tensor_tensor(y, ps[:, 6, 256:512].rearrange("p (t c) -> p t c", t=TPG),
                                                       rows(0), ALU.add))
                        c.link(nc.vector.tensor_reduce(y_st[:, 0, :], y, AX.X, ALU.add, negate=True))
                        c.link(nc.vector.tensor_scalar(y_st[:, 0, :], y_st[:, 0, :], 1.0 / C, None, ALU.mult))
                        nc.vector.tensor_tensor(y, y, wide4(y_st[:, 0, :]), ALU.add).then_inc(y_sq_in, 1)
                        dve.wait_ge(y_sq, g + 1)
                        c.link(nc.vector.tensor_reduce(y_st[:, 1, :], y2, AX.X, ALU.add))
                        nc.vector.tensor_scalar(y_st[:, 2, :], y_st[:, 1, :], 1.0 / C, 1e-5,
                                                ALU.mult, ALU.add).then_inc(y_var, 1)
                        dve.wait_ge(y_rstd, g + 1)
                        c.link(nc.vector.tensor_tensor(y, y, wide4(y_st[:, 3, :]), ALU.mult))
                        c.link(nc.vector.tensor_tensor(y, y, rows(1), ALU.mult))
                        c.link(nc.vector.tensor_tensor(y, y, rows(2), ALU.add))
                        xg = x_tok[:, bass.ds(g * TPG, TPG), :]
                        c.link(nc.vector.tensor_tensor(xg, xg, y, ALU.add))
                    c.end(GROUPS)

        router_ps, route_read, exp_in, exp_done = (sem(f"moe_{n}") for n in ("router_ps", "route_read", "exp_in", "exp_done"))
        parts_ready, gates_ps, gates_copied = (sem(f"moe_{n}") for n in ("parts_ready", "gates_ps", "gates_copied"))
        h_ps, h_act, h_mul, h_gated = sem("moe_h_ps"), sem("moe_h_act"), sem("moe_h_mul"), sem("moe_h_gated")
        gate_ps, gate_copied = sem("moe_gate_ps"), sem("moe_gate_copied")
        y_ps, y_copied, yt_ps = sem("moe_y_ps"), sem("moe_y_copied"), sem("moe_yt_ps")
        w_high, w_split = sem("moe_w_high"), sem("moe_w_split")
        w_loaded = [sem(f"moe_w_loaded{n}") for n in range(4)]
        s_cast = sem("moe_cast")
        at = dict.fromkeys(("phase", "tiles", "acts", "muls", "selects", "chunks", "small"), 0)

        def load_small(eng, F):
            _, _, w2_d, b1_d, b2_d, router_d, router_b_d = F
            load(eng, "f", w2[:, 0:w2_d.shape[1]], w2_d)
            for half in range(2):
                load(eng, "f", router_w[half * C:(half + 1) * C, :], router_d)
            load(eng, "f", router_b[:, :], router_b_d.broadcast_to((P, E)))
            if b1_d is not None:
                load(eng, "f", b1_col[:, 0:b1_d.shape[1]], b1_d)
                load(eng, "f", b2_rows[:, :], b2_d)

        def split_weights(chunks, engines):
            sp, act, dve = engines
            n0 = at["chunks"]
            if sp is not None:
                for n, (src, _) in enumerate(chunks):
                    m = n0 + n
                    width = src.shape[1]
                    if m >= 4:
                        sp.wait_ge(w_split, m - 3)
                    for half in range(2):
                        sp.dma_start(w_stage[half * C:(half + 1) * C, m % 4 * STAGE:m % 4 * STAGE + width],
                                     src).then_inc(w_loaded[m % 4], 16)
            if act is not None:
                for n, (src, col) in enumerate(chunks):
                    m = n0 + n
                    width = src.shape[1]
                    act.wait_ge(w_loaded[m % 4], 32 * (m // 4 + 1))
                    nc.scalar.activation(w16[:, 0, col:col + width], w_stage[:, m % 4 * STAGE:m % 4 * STAGE + width],
                                         ACT.Copy, scale=WEIGHT_SCALE).then_inc(w_high, 1)
            if dve is not None:
                for n, (src, col) in enumerate(chunks):
                    m = n0 + n
                    width = src.shape[1]
                    dve.wait_ge(w_high, m + 1)
                    nc.vector.scalar_tensor_tensor(w16[:, 1, col:col + width],
                                                   w_stage[:, m % 4 * STAGE:m % 4 * STAGE + width], WEIGHT_SCALE,
                                                   w16[:, 0, col:col + width], ALU.mult,
                                                   ALU.subtract).then_inc(w_split, 1)

        def chunks_of(F):
            out = []
            for base, w_d in ((0, F[0]), (HIDDEN0, F[1])):
                if w_d is not None:
                    for c in range(0, w_d.shape[1], STAGE):
                        out.append((w_d[:, c:c + STAGE], base + c))
            return out

        def experts(tiles, func, swiglu, gating, F, add_tokens=False):
            J = len(tiles)
            assert J % 4 == 0
            act_h = sbl("act_h", [P, 4, GTOK])
            mul_h = sbl("mul_h", [P, 2, GTOK])
            gate_sb = sbl("gate_sb", [P, 3, GTOK])
            hid = sbl("hid", [P, 4, GTOK])
            y_sb = sbl("y_sb", [P, GTOK])
            p0, v0, m0, g0 = at["phase"], at["tiles"], at["muls"], at["selects"]
            a0 = at["acts"]
            new_select = [j == 0 or tiles[j][2] != tiles[j - 1][2] for j in range(J)]
            select_no = [sum(new_select[:j + 1]) - 1 for j in range(J)]
            SPG = sum(new_select)
            at["phase"] += 1
            at["tiles"] += J * GROUPS
            at["acts"] += J * GROUPS
            at["muls"] += J * GROUPS if swiglu else 0
            at["selects"] += SPG * GROUPS if swiglu else 0
            H_BANKS, H3, GATE, YT, Y, LOGITS = 2, 2, (4 if swiglu else 2), 5, 6, 7
            Y_LAST, Y_COPY, Y_TURN, Y_ADD = J, J + 1, J + 2, J + 3

            def group_of(k, i, off):
                if (k - off) % J:
                    return None
                r = (k - off) // J
                if isinstance(i, int) and not 0 <= i + r < GROUPS:
                    return None
                return i + r

            def tile_of(k, i, lag):
                n = k + lag
                if isinstance(i, int) and not 0 <= i * J + n < J * GROUPS:
                    return None
                return n % J, i * J + (n + 1), i + n // J

            def stream(eng, step):
                for k in range(J):
                    step(0, k)
                with eng.Fori(1, GROUPS - 1) as i:
                    for k in range(J):
                        step(i, k)
                for k in range(J + Y_ADD + 1):
                    step(GROUPS - 1, k)

            with nc.Block() as block:
                @block.tensor
                def _(pe):
                    for t in range(NT):
                        for part in range(2):
                            last = nc.tensor.matmul(ps[:, LOGITS, t * E:(t + 1) * E], x16[:, t * P:(t + 1) * P],
                                                    router16[:, part, :], start=(part == 0), stop=(part == 1))
                    last.then_inc(router_ps, 1)
                    pe.wait_ge(parts_ready, p0 + 1)
                    for t in range(NT):
                        o = ps[0:KG, t // 8, :].bitcast(BF16)
                        last = nc.tensor.transpose(o[:, t % 8 * P:(t % 8 + 1) * P], gate_parts[:, t, :], idn_bf[:, :])
                        if t % 8 == 7:
                            last.then_inc(gates_ps, 1)
                    pe.wait_ge(gates_copied, 4 * (p0 + 1))

                    def hidden(i, k):
                        if (tile := tile_of(k, i, 1)) is None:
                            return
                        j, count, g = tile
                        col = tiles[j][0]
                        xg = x16[:, bass.ds(g * GTOK, GTOK)]
                        if not isinstance(i, int) or i * J + k + 1 >= H_BANKS:
                            if swiglu:
                                pe.wait_ge(h_mul, count + (m0 - H_BANKS))
                            else:
                                pe.wait_ge(h_act, count + (a0 - H_BANKS))
                        for part in range(2):
                            last = nc.tensor.matmul(ps[:, j % H_BANKS, :], w16[:, part, col:col + P], xg,
                                                    start=(part == 0), stop=(part == 1))
                        if swiglu:
                            for part in range(2):
                                last = nc.tensor.matmul(ps[:, H3 + j % H_BANKS, :],
                                                        w16[:, part, HIDDEN0 + col:HIDDEN0 + col + P], xg,
                                                        start=(part == 0), stop=(part == 1))
                        last.then_inc(h_ps, 1)

                    def gate(i, k):
                        if (tile := tile_of(k, i, 1)) is None or not new_select[tile[0]]:
                            return
                        j, _, g = tile
                        if swiglu and (not isinstance(i, int) or i * J + k + 1 > 0):
                            pe.wait_ge(gate_copied, g * SPG + (g0 + select_no[j]))
                        bank = GATE if swiglu else GATE + select_no[j] % 2
                        nc.tensor.matmul(ps[:, bank, :], selector[:, tiles[j][2], :],
                                         gate_t[:, bass.ds(g * GTOK, GTOK)], start=True, stop=True).then_inc(gate_ps, 1)

                    def step(i, k):
                        hidden(i, k)
                        if (tile := tile_of(k, i, -1)) is not None:
                            j, count, g = tile
                            if j == 0 and group_of(k, i, J + 1) is not None:
                                pe.wait_ge(y_copied, g + GROUPS * p0)
                                pe.sem_inc(y_bank_free, 1)
                            if j == 0 and not swiglu:
                                for part in range(3):
                                    nc.tensor.matmul(ps[0:C, Y, :], b2_parts[:, part, :],
                                                     gate_t[:, bass.ds(g * GTOK, GTOK)],
                                                     start=(part == 0), stop=False, skip_group_check=True)
                            pe.wait_ge(h_gated, count + v0)
                            half = (j + (0 if swiglu else 1)) % 2
                            last = nc.tensor.matmul(ps[half * C:(half + 1) * C, Y, :],
                                                    w2[:, tiles[j][1]:tiles[j][1] + C], hid[:, j % 4, :],
                                                    start=(j < (2 if swiglu else 1)), stop=(j >= J - 2),
                                                    skip_group_check=True)
                            if j == J - 1:
                                last.then_inc(y_ps, 1)
                        gate(i, k)
                        if (g := group_of(k, i, Y_TURN)) is not None:
                            pe.wait_ge(y_copied, g + (GROUPS * p0 + 1))
                            if not isinstance(g, int) or g > 0:
                                pe.wait_ge(added, g * 2 + 2 * GROUPS * p0)
                            for t in range(TPG):
                                last = nc.tensor.transpose(ps[:, YT, t * P:(t + 1) * P],
                                                           y_sb[:, t * P:(t + 1) * P], idn[:, :])
                            last.then_inc(yt_ps, 1)

                    hidden(0, -1)
                    gate(0, -1)
                    stream(pe, step)

                @block.scalar
                def _(act):
                    act.wait_ge(exp_in, p0 + 1)
                    nc.scalar.activation(rt[:, 1, :, :], rt[:, 1, :, :], ACT.Exp).then_inc(exp_done, 1)
                    for n in (0, 2):
                        act.wait_ge(gates_ps, 4 * p0 + n + 1)
                        nc.scalar.copy(gate_t[:, n * 2 * GTOK:(n + 1) * 2 * GTOK],
                                       ps[0:KG, n, :].bitcast(BF16)).then_inc(gates_copied, 1)

                    def step(i, k):
                        if (tile := tile_of(k, i, 0)) is not None:
                            j, count, g = tile
                            if swiglu and new_select[j]:
                                act.wait_ge(gate_ps, g * SPG + (gp0 + select_no[j] + 1))
                                nc.scalar.copy(gate_sb[:, select_no[j] % 3, :], ps[:, GATE, :]).then_inc(gate_copied, 1)
                            act.wait_ge(h_ps, count + v0)
                            bias = 0.0 if swiglu else b1_col[:, j:j + 1]
                            nc.scalar.activation(act_h[:, j % 4, :], ps[:, j % H_BANKS, :], func,
                                                 bias=bias, scale=UNSCALE).then_inc(h_act, 1)
                        if (g := group_of(k, i, Y_COPY)) is not None:
                            act.wait_ge(y_ps, g + (GROUPS * p0 + 1))
                            nc.scalar.copy(y_sb[:, :], ps[:, Y, :]).then_inc(y_copied, 1)

                    gp0 = at["small"]
                    stream(act, step)

                @block.vector
                def _(dve):
                    c = dve_chain.on(dve)
                    dve.wait_ge(router_ps, p0 + 1)
                    logits, ex = rt[:, 0, :, :], rt[:, 1, :, :]
                    hot1, hot2, tmp, rest = (rt[:, n, :, :] for n in (2, 3, 4, 5))
                    mx, r1, total, top, inv, inv2 = (rs[:, n, :] for n in range(6))

                    def wide(v):
                        return v.unsqueeze(2).broadcast_to((P, NT, E))

                    ranks = rank[:, :].unsqueeze(1).broadcast_to((P, NT, E))
                    c.link(nc.vector.tensor_scalar(logits, ps[:, LOGITS, 0:NT * E].rearrange(
                        "p (t e) -> p t e", e=E), UNSCALE, None, ALU.mult))
                    c.link(nc.vector.tensor_tensor(logits, logits, router_b[:, :].unsqueeze(1).broadcast_to((P, NT, E)),
                                                   ALU.add))
                    c.link(nc.vector.tensor_reduce(mx, logits, AX.X, ALU.max))
                    nc.vector.tensor_tensor(ex, logits, wide(mx), ALU.subtract).then_inc(exp_in, 1)

                    def one_hot(hot, values):
                        c.link(nc.vector.tensor_tensor(tmp, values, wide(mx), ALU.is_equal))
                        c.link(nc.vector.tensor_tensor(tmp, tmp, ranks, ALU.mult))
                        c.link(nc.vector.tensor_reduce(r1, tmp, AX.X, ALU.max))
                        c.link(nc.vector.tensor_tensor(hot, ranks, wide(r1), ALU.is_equal))

                    one_hot(hot1, logits)
                    c.link(nc.vector.scalar_tensor_tensor(rest, hot1, -3e38, logits, ALU.mult, ALU.add))
                    c.link(nc.vector.tensor_reduce(mx, rest, AX.X, ALU.max))
                    one_hot(hot2, rest)
                    c.link(nc.vector.tensor_tensor(hot1, hot1, hot2, ALU.add))
                    dve.wait_ge(exp_done, p0 + 1)
                    c.link(nc.vector.tensor_tensor(hot1, hot1, ex, ALU.mult))
                    c.link(nc.vector.tensor_reduce(total, ex, AX.X, ALU.add))
                    c.link(nc.vector.tensor_reduce(top, hot1, AX.X, ALU.add))
                    if gating == "two":
                        c.link(nc.vector.reciprocal(inv, top))
                    else:
                        c.link(nc.vector.reciprocal(inv, total))
                    if gating in ("plus", "floor"):
                        op, eps = (ALU.add, 1e-9) if gating == "plus" else (ALU.max, 1e-12)
                        c.link(nc.vector.tensor_tensor(top, top, inv, ALU.mult))
                        c.link(nc.vector.tensor_scalar(top, top, eps, None, op))
                        c.link(nc.vector.reciprocal(inv2, top))
                        c.link(nc.vector.tensor_tensor(inv, inv, inv2, ALU.mult))
                    c.link(nc.vector.tensor_tensor(hot1, hot1, wide(inv), ALU.mult))
                    for n, p_at in enumerate(PARTS_AT):
                        part = gate_parts[:, :, p_at:p_at + E]
                        if n == 2:
                            nc.vector.tensor_copy(part, hot1).then_inc(parts_ready, 1)
                            break
                        c.link(nc.vector.tensor_copy(part, hot1))
                        c.link(nc.vector.tensor_tensor(hot1, hot1, part, ALU.subtract))
                    if add_tokens:
                        c.link(nc.vector.tensor_tensor(x_tok[:, :, :], x_tok[:, :, :], xn_tok[:, :, :], ALU.add))
                    for n in (1, 3):
                        dve.wait_ge(gates_ps, 4 * p0 + n + 1)
                        nc.vector.tensor_copy(gate_t[:, n * 2 * GTOK:(n + 1) * 2 * GTOK],
                                              ps[0:KG, n, :].bitcast(BF16)).then_inc(gates_copied, 1)

                    gp0 = at["small"]

                    def step(i, k):
                        if (tile := tile_of(k, i, 0)) is not None:
                            j, count, g = tile
                            dve.wait_ge(h_act, count + a0)
                            if swiglu:
                                nc.vector.scalar_tensor_tensor(mul_h[:, j % 2, :], ps[:, H3 + j % H_BANKS, :], UNSCALE,
                                                               act_h[:, j % 4, :], ALU.mult, ALU.mult).then_inc(h_mul, 1)
                                dve.wait_ge(h_mul, count + m0)
                                values, gates_ = mul_h[:, j % 2, :], gate_sb[:, select_no[j] % 3, :]
                            else:
                                if new_select[j]:
                                    dve.wait_ge(gate_ps, g * SPG + (gp0 + select_no[j] + 1))
                                values, gates_ = act_h[:, j % 4, :], ps[:, GATE + select_no[j] % 2, :]
                            nc.vector.tensor_tensor(hid[:, j % 4, :], values, gates_, ALU.mult).then_inc(h_gated, 1)
                        if (g := group_of(k, i, Y_ADD)) is not None:
                            dve.wait_ge(yt_ps, g + (GROUPS * p0 + 1))
                            xg = x_tok[:, bass.ds(g * TPG, TPG), :]
                            yt = ps[:, YT, :].rearrange("p (t a c) -> p t a c", t=TPG, a=2)
                            for half in range(2):
                                nc.vector.tensor_tensor(xg, xg, yt[:, :, half, :], ALU.add).then_inc(added, 1)
                                dve.wait_ge(added, g * 2 + (2 * GROUPS * p0 + half + 1))

                    stream(dve, step)
                    at["small"] += SPG * GROUPS

        added, y_bank_free = sem("moe_added"), sem("moe_y_bank_free")

        def cast_small(act, dve, biases):
            n = at["cast"]
            if act is not None:
                act.wait_ge(loaded["f"], want["f"])
                nc.scalar.activation(router16[:, 0, :], router_w[:, :], ACT.Copy, scale=WEIGHT_SCALE).then_inc(s_cast, 1)
            if dve is not None:
                dve.wait_ge(s_cast, n + 1)
                nc.vector.scalar_tensor_tensor(router16[:, 1, :], router_w[:, :], WEIGHT_SCALE, router16[:, 0, :],
                                               ALU.mult, ALU.subtract)
                if biases:
                    c = dve_chain.on(dve)
                    c.link(nc.vector.tensor_copy(b2_parts[:, 0, :], b2_rows[:, :]))
                    c.link(nc.vector.tensor_tensor(b2_rest[:, :], b2_rows[:, :], b2_parts[:, 0, :], ALU.subtract))
                    c.link(nc.vector.tensor_copy(b2_parts[:, 1, :], b2_rest[:, :]))
                    c.link(nc.vector.tensor_tensor(b2_rest[:, :], b2_rest[:, :], b2_parts[:, 1, :], ALU.subtract))
                    nc.vector.tensor_copy(b2_parts[:, 2, :], b2_rest[:, :])

        at["cast"] = 0

        def prepare_experts(F):
            chunks = chunks_of(F)
            with nc.Block() as block:
                @block.sync
                def _(sp):
                    split_weights(chunks, (sp, None, None))

                @block.scalar
                def _(act):
                    split_weights(chunks, (None, act, None))
                    cast_small(act, None, F[4] is not None)

                @block.vector
                def _(dve):
                    split_weights(chunks, (None, None, dve))
                    cast_small(None, dve, F[4] is not None)
            at["chunks"] += len(chunks)
            at["cast"] += 1

        def start_loads(F):
            with nc.Block() as block:
                @block.sync
                def _(sp):
                    load_small(sp, F)

        def relative_bias():
            tab = sbl("tab", [3, REL * REL])
            m1 = sbl("m1", [3, 32])
            m2 = sbl("m2", [32, E])
            hid = sbl("bias_hid", [32, REL * REL])
            table = sbl("bias_table", [HEADS1, REL * REL])
            b_ps, b_hid, b_ps2, b_sig, b_tab, b_dram = (sem(f"bias_{n}") for n in ("ps", "hid", "ps2", "sig", "tab", "dram"))
            cuts = [(0, BANK), (BANK, REL * REL)]
            with nc.Block() as block:
                @block.sync
                def _(sp):
                    for dst, src in ((tab, L1["tab"]), (m1, L1["m1"]), (m2, L1["m2"])):
                        load(sp, "bias", dst[:, :], src)
                    sp.wait_ge(b_tab, 1)
                    bands = L1["scratch"]
                    for j in range(SIDE):
                        sp.dma_start(bands[j, :, :, :], table[:, :].rearrange("h (a b) -> h a b", b=REL)
                                     [:, :, SIDE - 1 - j:REL - j]).then_inc(b_dram, 16)
                    sp.wait_ge(b_dram, 16 * SIDE)
                    for i in range(SIDE):
                        r0 = i % (SIDE // 2) * SIDE
                        load(sp, "l1", rel_bias[r0:r0 + SIDE, i // (SIDE // 2), :, :],
                             bands[:, :, SIDE - 1 - i:REL - i, :].rearrange("j h k l -> j h (k l)"))

                @block.tensor
                def _(pe):
                    pe.wait_ge(loaded["bias"], 48)
                    for k, (a, b) in enumerate(cuts):
                        last = nc.tensor.matmul(ps[0:32, k, 0:b - a], m1[:, :], tab[:, a:b], start=True, stop=True)
                    last.then_inc(b_ps, 1)
                    pe.wait_ge(b_hid, 1)
                    for k, (a, b) in enumerate(cuts):
                        last = nc.tensor.matmul(ps[0:HEADS1, 2 + k, 0:b - a], m2[:, :], hid[:, a:b], start=True, stop=True)
                    last.then_inc(b_ps2, 1)

                @block.scalar
                def _(act):
                    act.wait_ge(b_ps, 1)
                    for k, (a, b) in enumerate(cuts):
                        last = nc.scalar.activation(hid[:, a:b], ps[0:32, k, 0:b - a], ACT.Relu)
                    last.then_inc(b_hid, 1)
                    act.wait_ge(b_ps2, 1)
                    for k, (a, b) in enumerate(cuts):
                        last = nc.scalar.activation(table[:, a:b], ps[0:HEADS1, 2 + k, 0:b - a], ACT.Sigmoid)
                    last.then_inc(b_sig, 1)

                @block.vector
                def _(dve):
                    dve.wait_ge(b_sig, 1)
                    nc.vector.tensor_scalar(table[:, :], table[:, :], -16.0, None, ALU.mult).then_inc(b_tab, 1)

        def attention():
            qkv_w = sbl("qkv_w", [KC, 3 * C])
            proj_w = sbl("proj_w", [KC, C])
            scale = sbl("scale", [P, 2 * HEADS1])
            x_grp = sbl("x1_grp", [KC, GTOK])
            qk = sbl("qk", [P, NT, 2 * C])
            vals = sbl("vals", [P, NT, HEADS1, VPAD])
            o_heads = sbl("o_heads", [P, GTOK])
            QK_T = B * 8 * P
            flat = w16[:, :, :].rearrange("p a n -> p (a n)")
            qk_t = flat[:, 0:QK_T].rearrange("p (b n) -> p b n", b=B)
            norm = flat[:, QK_T:QK_T + 12 * NT * HEADS1].bitcast(F32).rearrange(
                "p (k t h) -> p k t h", k=3, t=NT)
            parts = x16[:, 0:T // 2].rearrange("p (t w h a d) -> p t w h a d", t=TPG, w=2, h=HEADS1, a=4)
            qk_b = x16[:, T // 2:].rearrange("p (q w s j n) -> p q w s j n", q=2, w=2, s=2, j=2)
            prob = sq[:, :, :].rearrange("p t c -> p (t c)").rearrange("p (b a n) -> p b a n", b=4, a=2)
            prob_t = w_stage[:, :].rearrange("p (b n) -> p b n", b=4)
            low = o_heads[:, :].rearrange("p (t c) -> p t c", t=TPG)
            val_b = rt[:, 0:4, :, :].rearrange("p k t e -> p (k t e)").rearrange(
                "p (q m h v) -> p q m h v", q=2, m=2, v=VPAD)
            nmax = sbl("nmax", [P, 4, 2])
            inv_sum = sbl("inv_sum", [P, 2 * HEADS1])
            o_tok = sbl("o_tok", [P, 2, HEADS1, DH1])
            o_ch = sbl("o_ch", [KC, N])

            x_copied, qkv_ps, qkv_copied, qk_sq, sums = (sem(f"l1_{n}") for n in ("x_copied", "qkv_ps", "qkv_copied", "qk_sq", "sums"))
            setup, w_ready, sums_inverted = sem("l1_setup"), sem("l1_w_ready"), sem("l1_sums_inverted")
            rooted, inverted = sem("l1_rooted"), sem("l1_inverted")
            split, turned, t_copied = sem("l1_split"), sem("l1_turned"), sem("l1_t_copied")

            with nc.Block() as block:
                @block.sync
                def _(sp):
                    load(sp, "l1", qkv_w[:, :], L1["qkv_w"])
                    load(sp, "l1", proj_w[:, :], L1["proj_w"])
                    load(sp, "l1", scale[:, :], L1["scale"].unsqueeze(0).broadcast_to((P, 2 * HEADS1)))

                @block.gpsimd
                def _(pool):
                    nc.gpsimd.memset(vals[:, :, :, DH1:VW], 1.0)
                    pool_chain.on(pool).link(nc.gpsimd.memset(vals[:, :, :, VW:], 0.0))
                    nc.gpsimd.memset(o_ch[C:KC, :], 1.0)

                @block.scalar
                def _(act):
                    with act.Fori(0, GROUPS) as g:
                        nc.scalar.copy(x_grp[:, :], xn_ch[:, bass.ds(g * GTOK, GTOK)]).then_inc(x_copied, 1)
                        act.wait_ge(qkv_ps, g + 1)
                        nc.scalar.copy(qk[:, bass.ds(g * TPG, TPG), :], ps[:, 0:TPG, 0:2 * C])
                        nc.scalar.copy(vals[:, bass.ds(g * TPG, TPG), :, 0:DH1],
                                       ps[:, 0:TPG, 2 * C:3 * C].rearrange("p t (h d) -> p t h d", d=DH1))
                        nc.scalar.activation(sq_qk[:, :, :], ps[:, 0:TPG, 0:2 * C], ACT.Square).then_inc(qk_sq, 1)
                        act.wait_ge(sums, g + 1)

                @block.tensor
                def _(pe):
                    pe.wait_ge(w_ready, 3)
                    with pe.Fori(0, GROUPS) as g:
                        pe.wait_ge(x_copied, g + 1)
                        for t in range(TPG):
                            last = nc.tensor.matmul(ps[:, t, 0:3 * C], x_grp[:, t * P:(t + 1) * P], qkv_w[:, :],
                                                    start=True, stop=True)
                        last.then_inc(qkv_ps, 1)

                @block.vector
                def _(dve):
                    dve.wait_ge(loaded["l1"], want["l1"])
                    for n in range(3):
                        w = qkv_w[0:C, n * C:(n + 1) * C]
                        nc.vector.tensor_tensor(w, w, idn[0:C, 0:C], ALU.add).then_inc(w_ready, 1)
                    with dve.Fori(0, GROUPS) as g:
                        dve.wait_ge(qk_sq, g + 1)
                        nc.vector.tensor_reduce(norm[:, 0, bass.ds(g * TPG, TPG), :],
                                                sq_qk[:, :, :].rearrange("p t (h d) -> p t h d", d=DH1),
                                                AX.X, ALU.add).then_inc(sums, 1)

            with nc.Block() as block:
                @block.vector
                def _(dve):
                    c = dve_chain.on(dve)
                    ss, y, t = norm[:, 0, :, :], norm[:, 1, :, :], norm[:, 2, :, :]
                    nc.vector.tensor_scalar(ss, ss, 1e-24, None, ALU.max).then_inc(setup, 1)
                    sq_ = scale[:, 0:HEADS1]
                    dve.wait_ge(setup, 1)
                    nc.vector.tensor_scalar(sq_, sq_, float(np.log(np.float32(1.0 / 0.01))), None, ALU.min).then_inc(setup, 1)
                    dve.wait_ge(rooted, 2)
                    c.link(nc.vector.tensor_scalar(sq_, sq_, -1.0, None, ALU.mult))
                    c.link(nc.vector.reciprocal(y, y))
                    c.link(nc.vector.tensor_tensor(t, y, y, ALU.mult))
                    c.link(nc.vector.tensor_tensor(t, t, ss, ALU.mult))
                    c.link(nc.vector.tensor_scalar(t, t, -0.5, 1.5, ALU.mult, ALU.add))
                    c.link(nc.vector.tensor_tensor(y, y, t, ALU.mult))
                    c.link(nc.vector.tensor_tensor(y, y, scale[:, :].unsqueeze(1).broadcast_to((P, NT, 2 * HEADS1)),
                                                   ALU.mult))

                @block.scalar
                def _(act):
                    act.wait_ge(setup, 1)
                    nc.scalar.activation(norm[:, 1, :, :], norm[:, 0, :, :], ACT.Sqrt).then_inc(rooted, 1)
                    act.wait_ge(setup, 2)
                    nc.scalar.activation(scale[:, 0:HEADS1], scale[:, 0:HEADS1], ACT.Exp).then_inc(rooted, 1)

            with nc.Block() as block:
                @block.vector
                def _(dve):
                    c = dve_chain.on(dve)
                    qk5 = low[:, :, :].rearrange("p t (w h d) -> p t w h d", w=2, d=DH1)
                    with dve.Fori(0, GROUPS) as g:
                        c.loop(g, 5)
                        c.link(nc.vector.tensor_tensor(
                            low[:, :, :].rearrange("p t (h d) -> p t h d", d=DH1),
                            qk[:, bass.ds(g * TPG, TPG), :].rearrange("p t (h d) -> p t h d", d=DH1),
                            norm[:, 1, bass.ds(g * TPG, TPG), :].unsqueeze(3).broadcast_to((P, TPG, 2 * HEADS1, DH1)),
                            ALU.mult))
                        dve.wait_ge(turned, g + 1)
                        for w in range(2):
                            src = qk5[:, :, w, :, :]
                            c.link(nc.vector.tensor_copy(parts[:, :, w, :, 0, :], src))
                            hi, lo = (2, 1) if w == 0 else (1, 2)
                            nc.vector.tensor_copy(parts[:, :, w, :, hi, :], parts[:, :, w, :, 0, :])
                            c.link(nc.vector.tensor_tensor(parts[:, :, w, :, lo, :], src,
                                                           parts[:, :, w, :, 0, :], ALU.subtract))
                            last = nc.vector.tensor_copy(parts[:, :, w, :, 3, :], parts[:, :, w, :, lo, :])
                        last.then_inc(split, 1)
                    c.end(GROUPS)

                @block.tensor
                def _(pe):
                    pe.sem_inc(turned, 1)
                    with pe.Fori(0, GROUPS) as g:
                        pe.wait_ge(split, g + 1)
                        pe.wait_ge(t_copied, g + 1)
                        for b in range(2):
                            for w in range(2):
                                for s in range(2):
                                    for j in range(2):
                                        n = (w * 2 + s) * 2 + j
                                        last = nc.tensor.transpose(
                                            ps[:, b, n * (P // 2):(n + 1) * (P // 2)].bitcast(F16),
                                            parts[:, 2 * b + j, w, 4 * s:4 * s + 4, :, :].rearrange("p h a d -> p (h a d)"),
                                            idn16[:, :])
                        last.then_inc(turned, 1)

                @block.scalar
                def _(act):
                    nc.scalar.copy(idn16[:, :], idn[:, :]).then_inc(t_copied, 1)
                    with act.Fori(0, GROUPS) as g:
                        act.wait_ge(turned, g + 2)
                        for b in range(2):
                            last = nc.scalar.copy(qk_t[:, bass.ds(2 * g + b, 1), :].rearrange("p a n -> p (a n)"),
                                                  ps[:, b, :].bitcast(F16))
                        last.then_inc(t_copied, 1)

            fetched = [sem("l1_fetched_even"), sem("l1_fetched_odd")]
            s_ps, shifted, exped = sem("l1_s_ps"), sem("l1_shifted"), sem("l1_exped")
            pt_ps, pt_dve, pt_act, o_ps = sem("l1_pt_ps"), sem("l1_pt_dve"), sem("l1_pt_act"), sem("l1_o_ps")
            o_ready, ot_ps, ot_copied, out_ps = (sem(f"l1_{n}") for n in ("o_ready", "ot_ps", "ot_copied", "out_ps"))
            heads_copied, view_ps, out_added = sem("l1_heads_copied"), sem("l1_view_ps"), sem("l1_out_added")
            scores_seen, outputs_seen = sem("l1_scores_seen"), sem("l1_outputs_seen")
            UPI = HEADS1
            UNITS = B * UPI
            STEP = 2 * UPI
            AHEAD = 3
            SB = 4
            LAG = 2
            pick = idn[:, :].rearrange("p (s v) -> p s v", v=VPAD)[:, :, 0:VW]

            def o_view(q):
                return ps[:, 6 + q, 0:2 * HEADS1 * VW].rearrange("p (h v) -> p h v", v=VW)

            def o_turned(q):
                return ps[0:C, 6 + q, N:2 * N]

            def o_out(q):
                return ps[:, 6 + q, 0:2 * C].rearrange("p (t c) -> p t c", t=2)

            def units(k, i, lag):
                n = k + lag
                if isinstance(i, int) and not 0 <= STEP * i + n < UNITS:
                    return None
                return i * STEP + n if not isinstance(i, int) else STEP * i + n, n % UPI

            def image(k, i, off):
                if (k - off) % UPI:
                    return None
                r = (k - off) // UPI
                if isinstance(i, int) and not 0 <= 2 * i + r < B:
                    return None
                return i * 2 + r if not isinstance(i, int) else 2 * i + r

            O_HEADS, O_NORM, O_ADD = 13, 15, 19
            O_VIEW, O_TURN, O_PROJ = 12, 14, 16
            O_COPY = 17

            def stream(eng, step, start=0):
                last = B // 2 - 1
                for k in range(start, STEP):
                    step(0, k)
                with eng.Fori(1, last) as i:
                    for k in range(STEP):
                        step(i, k)
                for k in range(STEP + O_ADD):
                    step(last, k)

            with nc.Block() as block:
                @block.sync
                def _(sp):
                    def fetch(b, q):
                        sp.dma_start(val_b[:, q, :, :, :].rearrange("p m h v -> p (m h v)"),
                                     vals[:, bass.ds(b * 2, 2), :, :].rearrange("p m h v -> p (m h v)")
                                     ).then_inc(fetched[q], 16)
                        sp.dma_start(qk_b[:, q, :, :, :, :].rearrange("p w s j n -> p (w s j n)"),
                                     qk_t[:, bass.ds(b, 1), :].rearrange("p a n -> p (a n)")).then_inc(fetched[q], 16)

                    fetch(0, 0)
                    fetch(1, 1)
                    with sp.Fori(1, B // 2) as i:
                        for q in range(2):
                            sp.wait_ge(s_ps, i * STEP + (q * UPI - UPI))
                            sp.wait_ge(o_ps, 2 * i + (q - 1))
                            fetch(i * 2 + q, q)

                @block.tensor
                def _(pe):
                    def scores(k, i):
                        if (unit := units(k, i, AHEAD)) is None:
                            return
                        nt, hp = unit[1] // 4, unit[1] % 4
                        q = (k + AHEAD) // UPI % 2
                        if unit[1] == 0:
                            pe.wait_ge(fetched[q], (i + (k + AHEAD) // STEP) * 32 + 32)
                        for a in range(2):
                            r = 32 * hp
                            last = nc.tensor.matmul(
                                ps[:, (k + AHEAD) % SB, a * N:(a + 1) * N],
                                qk_b[r:r + 32, q, 0, a, nt, :],
                                qk_b[r:r + 32, q, 1, a, :, :].rearrange("p j n -> p (j n)"),
                                start=True, stop=True)
                        last.then_inc(s_ps, 1)

                    def step(i, k):
                        scores(k, i)
                        if units(k, i, -LAG) is not None:
                            pe.wait_ge(pt_act if k % 2 else pt_dve, i * (STEP // 2) + ((k - LAG) // 2 + 1))
                        if (unit := units(k, i, 0)) is not None:
                            pe.wait_ge(exped, unit[0] + 1)
                            for a in range(2):
                                for m in range(2):
                                    last = nc.tensor.transpose(ps[:, 4 + k % 2, (2 * a + m) * P:(2 * a + m + 1) * P],
                                                               prob[:, k % SB, a, m * P:(m + 1) * P], idn[:, :])
                            last.then_inc(pt_ps, 1)
                        if (unit := units(k, i, -LAG)) is not None:
                            n = k - LAG
                            nt, hp, q = unit[1] // 4, unit[1] % 4, n // UPI % 2
                            if unit[1] == 0 and (b := image(k, i, 2 * UPI + LAG)) is not None:
                                pe.wait_ge(out_added, b + 1)
                            for m in range(2):
                                for a in range(2):
                                    r = VPAD * (2 * (hp % 2) + a)
                                    col = (2 * nt + hp // 2) * P
                                    last = nc.tensor.matmul(ps[r:r + VPAD, 6 + q, col:col + P],
                                                            val_b[:, q, m, hp + 4 * a, :],
                                                            prob_t[:, n % 4, (2 * a + m) * P:(2 * a + m + 1) * P],
                                                            start=(m == 0), stop=(m == 1), skip_group_check=True)
                            if unit[1] == UPI - 1:
                                last.then_inc(o_ps, 1)
                        if (b := image(k, i, O_VIEW)) is not None:
                            q = (k - O_VIEW) // UPI % 2
                            pe.wait_ge(heads_copied, b + 1)
                            pe.sem_inc(outputs_seen, 1)
                            for n in range(4):
                                last = nc.tensor.matmul(ps[:, 6 + q, n * 4 * VW:(n + 1) * 4 * VW],
                                                        o_heads[:, n * P:(n + 1) * P], pick, start=True, stop=True)
                            last.then_inc(view_ps, 1)
                        if (b := image(k, i, O_TURN)) is not None:
                            q = (k - O_TURN) // UPI % 2
                            pe.wait_ge(o_ready, b + 1)
                            pe.sem_inc(outputs_seen, 1)
                            for j in range(2):
                                last = nc.tensor.transpose(o_turned(q)[:, j * P:(j + 1) * P],
                                                           o_tok[:, j, :, :].rearrange("p h d -> p (h d)"), idn[:, :])
                            last.then_inc(ot_ps, 1)
                        if (b := image(k, i, O_PROJ)) is not None:
                            q = (k - O_PROJ) // UPI % 2
                            pe.wait_ge(ot_copied, b + 1)
                            for j in range(2):
                                last = nc.tensor.matmul(o_out(q)[:, j, :], o_ch[:, j * P:(j + 1) * P],
                                                        proj_w[:, :], start=True, stop=True)
                            last.then_inc(out_ps, 1)

                    for k in range(-AHEAD, 0):
                        scores(k, 0)
                    stream(pe, step)

                @block.scalar
                def _(act):
                    def step(i, k):
                        if (unit := units(k, i, 0)) is not None:
                            act.wait_ge(shifted, unit[0] + 1)
                            for a in range(2):
                                last = nc.scalar.activation(prob[:, k % SB, a, :], prob[:, k % SB, a, :], ACT.Exp,
                                                            bias=nmax[:, k % SB, a:a + 1], scale=-1.0)
                            last.then_inc(exped, 1)
                        if (unit := units(k, i, -2)) is not None and k % 2:
                            act.wait_ge(pt_ps, unit[0] + 1)
                            nc.scalar.copy(prob_t[:, (k - 2) % 4, :], ps[:, 4 + k % 2, :]).then_inc(pt_act, 1)
                        if (b := image(k, i, O_COPY)) is not None:
                            act.wait_ge(ot_ps, b + 1)
                            nc.scalar.copy(o_ch[0:C, :], o_turned((k - O_COPY) // UPI % 2)).then_inc(ot_copied, 1)

                    stream(act, step)

                @block.vector
                def _(dve):
                    c = dve_chain.on(dve)

                    def step(i, k):
                        if (unit := units(k, i, 0)) is not None:
                            nt, hp = unit[1] // 4, unit[1] % 4
                            dve.wait_ge(s_ps, unit[0] + 1)
                            dve.sem_inc(scores_seen, 1)
                            for a in range(2):
                                last = nc.vector.tensor_tensor_reduce(
                                    out=prob[:, k % SB, a, :], in0=ps[:, k % SB, a * N:(a + 1) * N],
                                    in1=rel_bias[:, nt, hp + 4 * a, :], scale=1.0, scalar=3e38,
                                    op0=ALU.add, op1=ALU.min, accum_out=nmax[:, k % SB, a:a + 1])
                            last.then_inc(shifted, 1)
                        if (unit := units(k, i, -2)) is not None and k % 2 == 0:
                            dve.wait_ge(pt_ps, unit[0] + 1)
                            nc.vector.tensor_copy(prob_t[:, (k - 2) % 4, :], ps[:, 4 + k % 2, :]).then_inc(pt_dve, 1)
                        if (b := image(k, i, O_HEADS)) is not None:
                            dve.wait_ge(o_ps, b + 1)
                            nc.vector.tensor_copy(o_heads[:, :], ps[:, 6 + (k - O_HEADS) // UPI % 2, :]
                                                  ).then_inc(heads_copied, 1)
                        if (b := image(k, i, O_NORM)) is not None:
                            view = o_view((k - O_NORM) // UPI % 2)
                            dve.wait_ge(view_ps, b + 1)
                            nc.vector.reciprocal(inv_sum[:, :], view[:, :, DH1]).then_inc(sums_inverted, 1)
                            dve.wait_ge(sums_inverted, b + 1)
                            nc.vector.tensor_tensor(o_tok[:, :, :, :].rearrange("p t h d -> p (t h) d"), view[:, :, 0:DH1],
                                                    inv_sum[:, :].unsqueeze(2).broadcast_to((P, 2 * HEADS1, DH1)),
                                                    ALU.mult).then_inc(o_ready, 1)
                        if (b := image(k, i, O_ADD)) is not None:
                            dve.wait_ge(out_ps, b + 1)
                            xb = x_tok[:, bass.ds(b * 2, 2), :]
                            nc.vector.tensor_tensor(xb, xb, o_out((k - O_ADD) // UPI % 2), ALU.add).then_inc(out_added, 1)

                    stream(dve, step)

        def similarity():
            map_w = sbl("map_w", [KC, C])
            x_one = sbl("x2_one", [KC, GTOK])
            x_zero = sbl("x2_zero", [KC, GTOK])
            x_sq = sbl("x2_sq", [KC, GTOK])
            ones = sbl("x2_ones", [KC, P])
            tx = sbl("tx", [P, TPG, C])
            norm_p = sbl("norm_p", [P, TPG])
            dots = sbl("dots", [P, TPG, N])
            inv = sbl("inv_norm", [P, TPG, N])
            copied, tx_ps, nrm_ps, dot_ps, relu_d, tx_copied, sim, o_ps, ones_set = (
                sem(f"l2_{n}") for n in ("copied", "tx_ps", "nrm_ps", "dot_ps", "relu", "tx_copied", "sim", "o_ps", "ones_set"))
            with nc.Block() as block:
                @block.sync
                def _(sp):
                    load(sp, "l2", map_w[:, :], L2)

                @block.scalar
                def _(act):
                    nc.scalar.activation(x_zero[C:KC, :], xn_ch[C:KC, 0:GTOK], ACT.Copy, scale=0.0)
                    with act.Fori(0, GROUPS) as g:
                        xg = xn_ch[:, bass.ds(g * GTOK, GTOK)]
                        nc.scalar.copy(x_one[:, :], xg)
                        nc.scalar.copy(x_zero[0:C, :], xn_ch[0:C, bass.ds(g * GTOK, GTOK)])
                        nc.scalar.activation(x_sq[:, :], xg, ACT.Square).then_inc(copied, 1)
                        act.wait_ge(tx_ps, g + 1)
                        nc.scalar.copy(tx[:, :, :], ps[:, 6, 0:TPG * C].rearrange("p (t c) -> p t c", t=TPG)).then_inc(tx_copied, 1)
                        act.wait_ge(dot_ps, g + 1)
                        nc.scalar.activation(dots[:, :, :], ps[:, 0:2, :].rearrange("p b (t n) -> p (b t) n", n=N),
                                             ACT.Relu).then_inc(relu_d, 1)

                @block.tensor
                def _(pe):
                    pe.wait_ge(loaded["l2"], want["l2"])
                    pe.wait_ge(ones_set, 1)
                    with pe.Fori(0, GROUPS) as g:
                        pe.wait_ge(copied, g + 1)
                        nc.tensor.matmul(ps[:, 4, :], ones[:, :], x_sq[:, :], start=True, stop=True)
                        for t in range(TPG):
                            last = nc.tensor.matmul(ps[:, 5, t:t + 1], x_sq[:, t * P:(t + 1) * P], ones[:, 0:1],
                                                    start=True, stop=True)
                        last.then_inc(nrm_ps, 1)
                        for t in range(TPG):
                            b = t // 2
                            last = nc.tensor.matmul(ps[:, t // 2, (t % 2) * N:(t % 2 + 1) * N],
                                                    x_zero[:, t * P:(t + 1) * P], x_one[:, b * N:(b + 1) * N],
                                                    start=True, stop=True)
                        last.then_inc(dot_ps, 1)
                        for t in range(TPG):
                            last = nc.tensor.matmul(ps[:, 6, t * C:(t + 1) * C], x_one[:, t * P:(t + 1) * P],
                                                    map_w[:, :], start=True, stop=True)
                        last.then_inc(tx_ps, 1)
                        pe.wait_ge(tx_copied, g + 1)
                        pe.wait_ge(sim, g + 1)
                        for t in range(TPG):
                            for j in range(2):
                                q = 2 * (t // 2) + j
                                last = nc.tensor.matmul(ps[:, 7, t * C:(t + 1) * C],
                                                        dots[:, q, (t % 2) * P:(t % 2 + 1) * P], tx[:, q, :],
                                                        start=(j == 0), stop=(j == 1))
                        last.then_inc(o_ps, 1)

                @block.vector
                def _(dve):
                    c = dve_chain.on(dve)
                    c.link(nc.vector.memset(ones[:, :], 1.0))
                    nc.vector.memset(ones[C:KC, :], 0.0).then_inc(ones_set, 1)
                    with dve.Fori(0, GROUPS) as g:
                        c.loop(g, 5)
                        dve.wait_ge(nrm_ps, g + 1)
                        c.link(nc.vector.tensor_copy(norm_p[:, :], ps[:, 5, 0:TPG]))
                        for t in range(TPG):
                            last = nc.vector.tensor_scalar(inv[:, t, :], ps[:, 4, (t // 2) * N:(t // 2 + 1) * N],
                                                           norm_p[:, t:t + 1], 1e-16, ALU.mult, ALU.max)
                        c.link(last)
                        c.link(nc.vector.reciprocal(inv[:, :, :], inv[:, :, :]))
                        dve.wait_ge(relu_d, g + 1)
                        c.link(nc.vector.tensor_tensor(inv[:, :, :], inv[:, :, :], dots[:, :, :], ALU.mult))
                        nc.vector.tensor_tensor(dots[:, :, :], inv[:, :, :], dots[:, :, :], ALU.mult).then_inc(sim, 1)
                        dve.wait_ge(o_ps, g + 1)
                        xg = x_tok[:, bass.ds(g * TPG, TPG), :]
                        c.link(nc.vector.tensor_tensor(xg, xg, ps[:, 7, 0:TPG * C].rearrange("p (t c) -> p t c", t=TPG),
                                                       ALU.add))
                    c.end(GROUPS)

        def convolution():
            TAPS = 5
            cw = sbl("conv_w", [P, TAPS, C])
            clip = sbl("conv_clip", [P, TAPS, C])
            sign = sbl("conv_sign", [P, TAPS, C])
            img = sbl("conv_img", [P, 2, 2, PADS, SIDE])
            signed, filled, o_ps, w_ready, added = (
                sem(f"l3_{n}") for n in ("signed", "filled", "o_ps", "w_ready", "added"))
            with nc.Block() as block:
                @block.sync
                def _(sp):
                    load(sp, "l3", cw[:, :, :], L3)

                @block.scalar
                def _(act):
                    act.wait_ge(loaded["l3"], 16)
                    nc.scalar.activation(sign[:, :, :], cw[:, :, :], ACT.Sign).then_inc(signed, 1)
                    act.wait_ge(w_ready, 1)
                    with act.Fori(0, B // 2) as i:
                        for q in range(2):
                            act.wait_ge(o_ps, 2 * i + q + 1)
                            src = xn_ch[0:C, bass.ds(i * (2 * N) + q * N, N)].rearrange("c (i j) -> c i j", j=SIDE)
                            nc.scalar.copy(img[0:C, q, 0, 1:SIDE + 1, 1:], src[:, :, :SIDE - 1])
                            nc.scalar.copy(img[C:P, q, 0, 1:SIDE + 1, :], src)
                            nc.scalar.copy(img[0:C, q, 1, 1:SIDE + 1, :SIDE - 1], src[:, :, 1:])
                            nc.scalar.copy(img[C:P, q, 1, 0:SIDE, :SIDE - 1], src[:, :, 1:]).then_inc(filled, 1)

                @block.tensor
                def _(pe):
                    pe.sem_inc(o_ps, 2)
                    pe.wait_ge(w_ready, 1)
                    with pe.Fori(0, B // 2) as i:
                        for q in range(2):
                            pe.wait_ge(filled, 2 * i + q + 1)
                            pe.wait_ge(added, 2 * i + q + 1)
                            for t in range(2):
                                for tap, (side, dy) in enumerate(((0, 0), (0, 1), (0, 2), (1, 0), (1, 2))):
                                    y = dy + t * (SIDE // 2)
                                    last = nc.tensor.matmul(
                                        ps[:, q, t * C:(t + 1) * C],
                                        img[:, q, side, y:y + SIDE // 2, :].rearrange("c i j -> c (i j)"),
                                        cw[:, tap, :], start=(tap == 0), stop=(tap == TAPS - 1))
                            last.then_inc(o_ps, 1)

                @block.vector
                def _(dve):
                    c = dve_chain.on(dve)
                    dve.sem_inc(added, 2)
                    c.link(nc.vector.memset(img[:, :, :, :, :], 0.0))
                    dve.wait_ge(loaded["l3"], 16)
                    c.link(nc.vector.tensor_scalar(clip[:, :, :], cw[:, :, :], 1.0, -1.0, ALU.min, ALU.max))
                    dve.wait_ge(signed, 1)
                    c.link(nc.vector.tensor_tensor(sign[:, :, :], sign[:, :, :], clip[:, :, :], ALU.subtract))
                    nc.vector.tensor_tensor(cw[:, :, :], sign[:, :, :], clip[:, :, :], ALU.add).then_inc(w_ready, 1)
                    with dve.Fori(0, B // 2) as i:
                        for q in range(2):
                            dve.wait_ge(o_ps, 2 * i + q + 3)
                            xb = x_tok[:, bass.ds(4 * i + 2 * q, 2), :]
                            nc.vector.tensor_tensor(xb, xb, ps[:, q, 0:2 * C].rearrange("p (t c) -> p t c", t=2),
                                                    ALU.add).then_inc(added, 1)

        swiglu_tiles = []
        for pair in range(E // 2):
            for n in range(PAIR0):
                tile = pair * PAIR0 + n
                swiglu_tiles.append((tile * P, tile * C, E + pair if n == 0 else 2 * pair + (n - 1) // FULL0))

        def gelu_tiles(hidden):
            per = hidden // P
            return [(n * P, n * C, n // per) for n in range(E * per)]

        pair_tiles = [(n * P, n * C, E + n) for n in range(E // 2)]

        local = []

        def sbl(name, shape, dt=F32):
            return local[-1].enter_context(nc.sbuf_tensor(f"{name}_stage{len(local)}", shape, dt))

        def stage(fn):
            with ExitStack() as s:
                local.append(s)
                fn()

        def constants():
            sel32 = ones_.rearrange("k (s p) -> k s p", p=P)
            with nc.Block() as block:
                @block.sync
                def _(sp):
                    sp.dma_start(sel32, selector_d).then_inc(sel_loaded, 16)

                @block.scalar
                def _(act):
                    nc.scalar.copy(idn_bf[:, :], idn[:, :])
                    act.wait_ge(sel_loaded, 16)
                    nc.scalar.copy(selector[:, :, :], sel32)

                @block.gpsimd
                def _(pool):
                    nc.gpsimd.memset(gate_parts[:, :, :], 0.0)

        ones_ = w_stage[0:KG, 0:(E + E // 2) * P]
        sel_loaded = sem("selector_loaded")
        sq_qk = sq[:, 0:8, :].rearrange("p (t a) c -> p t (a c)", a=2)

        norm_stage(1e-6)
        stage(linear_attention)
        if stop_after >= 2:
            start_loads(F0)
            constants()
            stage(relative_bias)
            prepare_experts(F0)
            norm_stage(1e-5, stacked=True)
            stage(lambda: experts(swiglu_tiles, ACT.Silu, True, "plus", F0))
        if stop_after >= 3:
            norm_stage(1e-6)
            start_loads(F1)
            stage(attention)
        if stop_after >= 4:
            prepare_experts(F1)
            norm_stage(1e-5, stacked=True)
            stage(lambda: experts(gelu_tiles(H_L1), ACT.Gelu, False, "all", F1))
        if stop_after >= 5:
            norm_stage(1e-6)
            start_loads(F2)
            stage(similarity)
        if stop_after >= 6:
            prepare_experts(F2)
            norm_stage(1e-5, stacked=True)
            stage(lambda: experts(gelu_tiles(H_L2), ACT.Gelu, False, "two", F2))
        if stop_after >= 7:
            norm_stage(1e-6)
            start_loads(F3)
            stage(convolution)
        if stop_after >= 8:
            prepare_experts(F3)
            norm_stage(1e-5, stacked=True)
            stage(lambda: experts(pair_tiles, ACT.Gelu, False, "floor", F3, add_tokens=True))
        with nc.Block() as block:
            @block.sync
            def _(sp):
                sp.dma_start(out, x_tok[:, :, :]).then_inc(stored, 16)
                sp.wait_ge(stored, 16)
                for key, s in loaded.items():
                    if want[key]:
                        sp.wait_ge(s, want[key])


def layouts(a):
    f = np.float32

    def rows(w_t, bias=None):
        bias = np.zeros(w_t.shape[1], f) if bias is None else bias
        return np.concatenate([w_t, bias[None]], 0)

    def diag(a_, b_):
        z = np.zeros((2 * a_.shape[0], 2 * a_.shape[1]), f)
        z[:a_.shape[0], :a_.shape[1]], z[a_.shape[0]:, a_.shape[1]:] = a_, b_
        return z

    d = {}
    d["x"] = a["x"].reshape(B, C, 2, P).transpose(3, 0, 2, 1).reshape(P, NT, C)
    d["ident"] = np.eye(P, dtype=f)
    d["rank"] = np.tile(np.arange(E, 0, -1, dtype=f), (P, 1))
    wq = a["L0_conv_W_qkv"].T
    d["l0_qv"] = rows(np.concatenate([wq[:, 0:HID0], wq[:, 2 * HID0:]], 1))
    d["l0_k"] = rows(wq[:, HID0:2 * HID0])
    d["l0_out"] = a["L0_conv_W_out"].T
    d["l0_mem"] = rows(a["L0_conv_memory"].reshape(C, MEM))
    head = np.arange(HID0) // DH0
    d["l0_mask"] = (head[:, None] == head[None]).astype(f)
    d["l0_rows"] = np.stack([a["L0_conv_b_out"], a["L0_conv_ln_g"], a["L0_conv_ln_b"]])

    selector = np.zeros((KG, E + E // 2, P), f)
    for r in PARTS_AT:
        for e in range(E):
            selector[r + e, e] = 1
            selector[r + e, E + e // 2, e % 2 * C:(e % 2 + 1) * C] = 1
    d["selector"] = selector

    def up(w):
        out = np.zeros((C, 4 * PAIR0 * P), f)
        for pair in range(E // 2):
            at = pair * PAIR0 * P
            for s in range(2):
                w_t = w[2 * pair + s].T
                out[:, at + s * C:at + s * C + TAIL0] = w_t[:, FULL0 * P:]
                out[:, at + (1 + s * FULL0) * P:at + (1 + (s + 1) * FULL0) * P] = w_t[:, :FULL0 * P]
        return out

    down = np.zeros((P, 4 * PAIR0 * C), f)
    for pair in range(E // 2):
        at = pair * PAIR0 * C
        for s in range(2):
            w_t = a["L0_ffn_w2"][2 * pair + s].T
            down[s * C:s * C + TAIL0, at:at + C] = w_t[FULL0 * P:]
            for n in range(FULL0):
                c0 = at + (1 + s * FULL0 + n) * C
                down[:, c0:c0 + C] = w_t[n * P:(n + 1) * P]
    d["f0_w1"], d["f0_w3"], d["f0_w2"] = up(a["L0_ffn_w1"]), up(a["L0_ffn_w3"]), down
    d["f0_router"], d["f0_router_b"] = a["L0_ffn_router_w"].T, np.zeros((1, E), f)

    def side_by_side(w):
        return w.transpose(1, 0, 2).reshape(w.shape[1], -1)

    def qkv(n):
        return rows(diag(a[f"L1_conv_{n}1_w"].T, a[f"L1_conv_{n}2_w"].T),
                    np.concatenate([a[f"L1_conv_{n}1_b"], a[f"L1_conv_{n}2_b"]]))

    d["l1_qkv"] = np.concatenate([qkv("q"), qkv("k"), qkv("v")], 1)
    heads = [2 * c + s + 4 * a_ for c in range(2) for s in range(2) for a_ in range(2)]
    order = np.concatenate([np.arange(h * DH1, (h + 1) * DH1) for h in heads] + [[C]])
    d["l1_proj"] = qkv("proj")[order]
    d["l1_scale"] = np.concatenate([a["L1_conv_logit_scale"].reshape(-1), np.ones(HEADS1, f)])
    r = np.arange(-(SIDE - 1), SIDE).astype(f) / f(SIDE - 1 + 1e-8)
    gh, gw = np.meshgrid(r, r, indexing="ij")
    tab = np.stack([gh, gw]) * f(3.2)
    tab = (np.sign(tab) * (f(1) - np.exp(-np.abs(tab)))).reshape(2, -1)
    d["l1_tab"] = np.concatenate([tab, np.ones((1, REL * REL), f)])[:, ::-1]
    d["l1_m1"] = rows(a["L1_conv_mlp_w1"].T, a["L1_conv_mlp_b1"])
    d["l1_m2"] = a["L1_conv_mlp_w2"].T
    def gelu_experts(n, w1, b1, w2, b2, router, router_b):
        d[f"f{n}_w1"] = side_by_side(w1)
        d[f"f{n}_b1"] = b1.reshape(-1, P).T
        d[f"f{n}_w2"] = side_by_side(w2.reshape(-1, P, C))
        d[f"f{n}_b2"] = np.zeros((KG, C), f)
        for r in PARTS_AT:
            d[f"f{n}_b2"][r:r + E] = b2
        d[f"f{n}_router"], d[f"f{n}_router_b"] = router, router_b.reshape(1, E)

    gelu_experts(1, a["L1_ffn_W1"], a["L1_ffn_b1"], a["L1_ffn_W2"], a["L1_ffn_b2"], a["L1_ffn_gate_w"], a["L1_ffn_gate_b"])
    gelu_experts(2, a["L2_ffn_W1"], a["L2_ffn_b1"], a["L2_ffn_W2"], a["L2_ffn_b2"], a["L2_ffn_Wg"], a["L2_ffn_bg"])
    gelu_experts(3, a["L3_ffn_w1"], a["L3_ffn_b1"], a["L3_ffn_w2"], a["L3_ffn_b2"], a["L3_ffn_router_w"].T,
                 np.zeros(E, f))
    d["l2_map"] = rows(a["L2_conv_W"].T, a["L2_conv_bias"])
    w = a["L3_conv_W"].transpose(1, 2, 3, 0)
    conv = np.zeros((P, 5, C), f)
    conv[:C, 0:3], conv[C:, 0:3] = w[:, :, 0], w[:, :, 1]
    conv[:C, 3], conv[C:, 3], conv[:C, 4] = w[:, 0, 2], w[:, 1, 2], w[:, 2, 2]
    d["l3_conv"] = conv
    return {k: np.ascontiguousarray(v) for k, v in d.items()}


def build(nc, d, out, scratch):
    metaformer(
        nc, d["x"], d["ident"], d["rank"], d["selector"],
        [d["l0_qv"], d["l0_k"], d["l0_out"], d["l0_mem"], d["l0_mask"], d["l0_rows"]],
        (d["f0_w1"], d["f0_w3"], d["f0_w2"], None, None, d["f0_router"], d["f0_router_b"]),
        dict(qkv_w=d["l1_qkv"], proj_w=d["l1_proj"], scale=d["l1_scale"], tab=d["l1_tab"],
             m1=d["l1_m1"], m2=d["l1_m2"], scratch=scratch),
        (d["f1_w1"], None, d["f1_w2"], d["f1_b1"], d["f1_b2"], d["f1_router"], d["f1_router_b"]),
        d["l2_map"],
        (d["f2_w1"], None, d["f2_w2"], d["f2_b1"], d["f2_b2"], d["f2_router"], d["f2_router_b"]),
        d["l3_conv"],
        (d["f3_w1"], None, d["f3_w2"], d["f3_b1"], d["f3_b2"], d["f3_router"], d["f3_router_b"]),
        out)


def kernel(**inputs):
    import concourse.bacc as bacc
    from concourse.bass_utils import run_bass_kernel_spmd

    nc = bacc.Bacc("TRN2", target_bir_lowering=False, num_devices=1)
    arrays = layouts({k: np.asarray(v) for k, v in inputs.items()})
    d = {k: nc.dram_tensor(k, v.shape, mybir.dt.from_np(v.dtype), kind="ExternalInput").ap()
         for k, v in arrays.items()}
    out = nc.dram_tensor("out", (P, NT, C), F32, kind="ExternalOutput").ap()
    scratch = nc.dram_tensor("bias_bands", (SIDE, HEADS1, REL, SIDE), F32, kind="Internal").ap()
    build(nc, d, out, scratch)
    got = run_bass_kernel_spmd(nc, [arrays], core_ids=[0]).results[0]["out"]
    return got.reshape(P, B, 2, C).transpose(1, 3, 2, 0).reshape(B, C, SIDE, SIDE)
```

```python
from contextlib import ExitStack

import numpy as np

import concourse.bass as bass
from concourse import mybir

F32 = mybir.dt.float32
F16 = mybir.dt.float16
BF16 = mybir.dt.bfloat16
ALU = mybir.AluOpType
ACT = mybir.ActivationFunctionType
AX = mybir.AxisListType

P = 128
C = 64
KC = C + 1
B = 16
SIDE = 16
N = SIDE * SIDE
T = B * N
NT = T // P
TPG = 4
GROUPS = NT // TPG
GTOK = TPG * P
BANK = 512
E = 8
HEADS0, DH0, MEM = 8, 16, 16
HID0 = HEADS0 * DH0
HEADS1, DH1 = 8, 8
VW = DH1 + 1
VPAD = 32
H_L0, H_L1, H_L2 = 682, 128, 256
FULL0, TAIL0 = H_L0 // P, H_L0 % P
PAIR0 = 2 * FULL0 + 1
REL = 2 * SIDE - 1
PADS = SIDE + 2

TOKEN_SCALE, WEIGHT_SCALE = 1024.0, 64.0
UNSCALE = 1.0 / (TOKEN_SCALE * WEIGHT_SCALE)
STAGE = 512
KG = 72
PARTS_AT = (0, 32, 64)


class Chain:

    def __init__(self, sem):
        self.sem, self.eng, self.base, self.k, self.i, self.per, self.start = sem, None, 0, 0, None, 0, 0

    def on(self, eng):
        self.eng = eng
        return self

    def loop(self, i, per, start=0):
        self.i, self.per, self.start = i, per, start

    def end(self, times):
        assert self.k == self.per, (self.k, self.per)
        self.base += times * self.per
        self.k, self.i, self.per, self.start = 0, None, 0, 0

    def link(self, ins):
        ins.then_inc(self.sem, 1)
        self.k += 1
        at = self.base + self.k - self.start * self.per
        if self.i is None:
            self.base, self.k = at, 0
        self.eng.wait_ge(self.sem, at if self.i is None else self.i * self.per + at)


def metaformer(nc, x, ident, wt_rank, selector_d, L0, F0, L1, F1, L2, F2, L3, F3, out):
    ctx = ExitStack()
    with ctx:
        def sb(name, shape, dt=F32):
            return ctx.enter_context(nc.sbuf_tensor(name + "_sb", shape, dt))

        def sem(name):
            return ctx.enter_context(nc.semaphore(name))

        ps = ctx.enter_context(nc.psum_tensor("ps", [P, 8, BANK], F32))

        x_tok = sb("x_tok", [P, NT, C])
        xn_tok = sb("xn_tok", [P, NT, C])
        xn_ch = sb("xn_ch", [KC, T])
        idn = sb("idn", [P, P])
        idn16 = sb("idn16", [P, P], F16)
        rank = sb("rank", [P, E])
        sq = sb("sq", [P, NT, C])
        st = sb("st", [P, 4, NT])
        neg_half = sb("neg_half", [P, 1])
        xn_group = sb("xn_group", [P, TPG, C])
        rt = sb("rt", [P, 6, NT, E])
        rs = sb("rs", [P, 6, NT])
        HIDDEN0 = 4 * PAIR0 * P
        w16 = sb("w16", [P, 2, 2 * HIDDEN0], F16)
        w_stage = sb("w_stage", [P, 4 * STAGE])
        w2 = sb("w2", [P, 4 * PAIR0 * C])
        x16 = sb("x16", [P, T], F16)
        b1_col = sb("b1_col", [P, E * H_L2 // P])
        b2_rows = sb("b2_rows", [KG, C])
        b2_rest = sb("b2_rest", [KG, C])
        b2_parts = sb("b2_parts", [KG, 3, C], BF16)
        router_w = sb("router_w", [P, E])
        router16 = sb("router16", [P, 2, E], F16)
        router_b = sb("router_b", [P, E])
        selector = sb("selector", [KG, E + E // 2, P], BF16)
        gate_parts = sb("gate_parts", [P, NT, KG], BF16)
        gate_t = sb("gate_t", [KG, T], BF16)
        idn_bf = sb("idn_bf", [P, P], BF16)
        rel_bias = sb("rel_bias", [P, 2, HEADS1, N])
        tab = rel_bias[0:3, 0, 0:4, :].rearrange("p h n -> p (h n)")[:, 0:REL * REL]
        m1 = rel_bias[0:3, 0, 4, 0:32]
        m2 = rel_bias[0:32, 0, 5, 0:E]
        table = rel_bias[0:HEADS1, 1, 0:4, :].rearrange("p h n -> p (h n)")[:, 0:REL * REL]
        bias_hidden = xn_ch[0:32, 0:REL * REL]
        sel32 = w_stage[0:KG, 0:(E + E // 2) * P].rearrange("k (s p) -> k s p", p=P)
        b_ps, b_hidden, b_ps2, b_sig, b_dram = (sem(f"bias_{n}") for n in ("ps", "hidden", "ps2", "sig", "dram"))
        sel_loaded = sem("selector_loaded")
        bias_cuts = [(0, BANK), (BANK, REL * REL)]

        w_high, w_split = sem("moe_w_high"), sem("moe_w_split")
        w_loaded = [sem(f"moe_w_loaded{n}") for n in range(4)]
        dve_chain = Chain(sem("dve_chain"))
        act_chain = Chain(sem("act_chain"))
        pool_chain = Chain(sem("pool_chain"))
        loaded = {k: sem(f"loaded_{k}") for k in ("x", "const", "l0", "f", "l1", "l2", "l3", "bias")}
        want = dict.fromkeys(loaded, 0)
        stored = sem("stored")

        def load(eng, key, dst, src):
            eng.dma_start(dst, src).then_inc(loaded[key], 16)
            want[key] += 16

        def pairs(eng, step, c=None, links=0):
            last = GROUPS // 2 - 1
            for q in range(2):
                step(q, q)
            with eng.Fori(1, last) as i:
                if c is not None:
                    c.loop(i, 2 * links, start=1)
                for q in range(2):
                    step(i * 2 + q, q)
            if c is not None:
                c.end(last - 1)
            for q in range(2):
                step(2 * last + q, q)

        def is_group(g):
            return not isinstance(g, int) or 0 <= g < GROUPS

        def from_third(g):
            return not isinstance(g, int) or g >= 2

        s_centred, s_squared = sem("norm_centred"), sem("norm_squared")
        s_var, s_rstd = sem("norm_var"), sem("norm_rstd")
        s_scaled, s_turned = sem("norm_scaled"), sem("norm_turned")
        norms = [0]

        s_high = sem("norm_high")
        highs = [0]

        def norm_stage(eps, stacked=False, prepare=None):
            hi0 = highs[0]
            if stacked:
                highs[0] += GROUPS
            n0 = norms[0]
            norms[0] += 1
            halves = [slice(h * NT // 2, (h + 1) * NT // 2) for h in range(2)]

            def wide(v, s):
                return v.unsqueeze(2).broadcast_to((P, s.stop - s.start, C))

            with nc.Block() as block:
                if n0 == 0:
                    @block.sync
                    def _(sp):
                        load(sp, "x", x_tok[:, :, :], x)
                        for dst, src in ((tab, L1["tab"]), (m1, L1["m1"]), (m2, L1["m2"])):
                            load(sp, "bias", dst, src)
                        load(sp, "const", idn[:, :], ident)
                        load(sp, "const", rank[:, :], wt_rank)
                        sp.dma_start(sel32, selector_d).then_inc(sel_loaded, 16)
                        load_small(sp, F0)

                if prepare is not None:
                    @block.sync
                    def _(sp):
                        prepare_experts(prepare, sp=sp)

                @block.vector
                def _(dve):
                    c = dve_chain.on(dve)
                    if n0 == 0:
                        nc.vector.memset(xn_ch[C:KC, :], 1.0)
                        dve.wait_ge(loaded["x"], want["x"])
                    for s in halves:
                        c.link(nc.vector.tensor_reduce(st[:, 0, s], x_tok[:, s, :], AX.X, ALU.add, negate=True))
                        c.link(nc.vector.tensor_scalar(st[:, 0, s], st[:, 0, s], 1.0 / C, None, ALU.mult))
                        nc.vector.tensor_tensor(xn_tok[:, s, :], x_tok[:, s, :], wide(st[:, 0, s], s),
                                                ALU.add).then_inc(s_centred, 1)
                    for h, s in enumerate(halves):
                        dve.wait_ge(s_squared, 2 * n0 + h + 1)
                        c.link(nc.vector.tensor_reduce(st[:, 1, s], sq[:, s, :], AX.X, ALU.add))
                        nc.vector.tensor_scalar(st[:, 2, s], st[:, 1, s], 1.0 / C, float(eps),
                                                ALU.mult, ALU.add).then_inc(s_var, 1)
                    if prepare is not None:
                        prepare_experts(prepare, dve=dve)
                    for h, s in enumerate(halves):
                        dve.wait_ge(s_rstd, 2 * n0 + h + 1)
                        nc.vector.tensor_tensor(xn_tok[:, s, :], xn_tok[:, s, :], wide(st[:, 3, s], s),
                                                ALU.mult).then_inc(s_scaled, 1)
                    if stacked:
                        for k in range(GROUPS):
                            tok = slice(k * GTOK, (k + 1) * GTOK)
                            dve.wait_ge(s_high, hi0 + k + 1)
                            nc.vector.scalar_tensor_tensor(x16[C:P, tok], ps[0:C, k, :], TOKEN_SCALE,
                                                           x16[0:C, tok], ALU.mult, ALU.subtract)
                        if n0 == 0:
                            dve.wait_ge(b_sig, 1)
                            nc.vector.tensor_scalar(table, table, -16.0, None, ALU.mult)
                            cast_small(None, dve, False)
                        return
                    for k in range(1, GROUPS, 2):
                        dve.wait_ge(s_turned, GROUPS * n0 + k + 1)
                        nc.vector.tensor_copy(xn_ch[0:C, k * GTOK:(k + 1) * GTOK], ps[0:C, k, :])

                @block.scalar
                def _(act):
                    if n0 == 0:
                        act.wait_ge(b_ps, 1)
                        for k, (a, b) in enumerate(bias_cuts):
                            last = nc.scalar.activation(bias_hidden[:, a:b], ps[0:32, k, 0:b - a], ACT.Relu)
                        last.then_inc(b_hidden, 1)
                    for h, s in enumerate(halves):
                        act.wait_ge(s_centred, 2 * n0 + h + 1)
                        nc.scalar.activation(sq[:, s, :], xn_tok[:, s, :], ACT.Square).then_inc(s_squared, 1)
                    if n0 == 0:
                        act.wait_ge(b_ps2, 1)
                        for k, (a, b) in enumerate(bias_cuts):
                            last = nc.scalar.activation(table[:, a:b], ps[0:HEADS1, 2 + k, 0:b - a], ACT.Sigmoid)
                        last.then_inc(b_sig, 1)
                    if prepare is not None:
                        prepare_experts(prepare, act=act)
                    if stacked:
                        for k in range(GROUPS):
                            act.wait_ge(s_turned, GROUPS * n0 + k + 1)
                            nc.scalar.activation(x16[0:C, k * GTOK:(k + 1) * GTOK], ps[0:C, k, :], ACT.Copy,
                                                 scale=TOKEN_SCALE).then_inc(s_high, 1)
                        if n0 == 0:
                            nc.scalar.copy(idn_bf[:, :], idn[:, :])
                            act.wait_ge(sel_loaded, 16)
                            nc.scalar.copy(selector[:, :, :], sel32)
                            cast_small(act, None, False)
                        return
                    for k in range(0, GROUPS, 2):
                        act.wait_ge(s_turned, GROUPS * n0 + k + 1)
                        nc.scalar.copy(xn_ch[0:C, k * GTOK:(k + 1) * GTOK], ps[0:C, k, :])

                @block.gpsimd
                def _(pool):
                    if n0 == 0:
                        pool_chain.on(pool).link(nc.gpsimd.memset(neg_half[:, :], -0.5))
                    for h, s in enumerate(halves):
                        pool.wait_ge(s_var, 2 * n0 + h + 1)
                        nc.gpsimd.tensor_tensor(st[:, 3, s], st[:, 2, s],
                                                neg_half[:, :].broadcast_to((P, NT // 2)),
                                                ALU.pow).then_inc(s_rstd, 1)
                    if n0 == 0:
                        nc.gpsimd.memset(gate_parts[:, :, :], 0.0)

                @block.tensor
                def _(pe):
                    if n0 == 0:
                        pe.wait_ge(loaded["bias"], want["bias"])
                        for k, (a, b) in enumerate(bias_cuts):
                            last = nc.tensor.matmul(ps[0:32, k, 0:b - a], m1, tab[:, a:b], start=True, stop=True)
                        last.then_inc(b_ps, 1)
                        pe.wait_ge(b_hidden, 1)
                        for k, (a, b) in enumerate(bias_cuts):
                            last = nc.tensor.matmul(ps[0:HEADS1, 2 + k, 0:b - a], m2, bias_hidden[:, a:b],
                                                    start=True, stop=True)
                        last.then_inc(b_ps2, 1)
                        pe.wait_ge(loaded["const"], 32)
                        pe.wait_ge(b_sig, 1)
                    for k in range(GROUPS):
                        if k % (GROUPS // 2) == 0:
                            pe.wait_ge(s_scaled, 2 * n0 + k // (GROUPS // 2) + 1)
                        for t in range(TPG):
                            last = nc.tensor.transpose(ps[0:C, k, t * P:(t + 1) * P],
                                                       xn_tok[:, k * TPG + t, :], idn[:, :])
                        last.then_inc(s_turned, 1)
            if prepare is not None:
                at["chunks"] += len(chunks_of(prepare))
            if prepare is not None or n0 == 0:
                at["cast"] += 1

        g_centred, g_squared, g_var, g_rstd = (sem(f"group_norm_{n}") for n in ("centred", "squared", "var", "rstd"))
        g_scaled, g_turned, g_high, g_copied = (sem(f"group_norm_{n}") for n in ("scaled", "turned", "high", "copied"))
        g_link, g_scaled_seen = sem("group_norm_link"), sem("group_norm_scaled_seen")
        group_norms = dict(uses=0, highs=0)

        class GroupNorm:

            def __init__(self, eps, stacked, bank):
                self.eps, self.stacked, self.bank = float(eps), stacked, bank
                self.n0 = GROUPS * group_norms["uses"]
                self.h0 = group_norms["highs"]
                group_norms["uses"] += 1
                group_norms["highs"] += GROUPS if stacked else 0

            def tiles(self, g):
                return bass.ds(g * TPG, TPG)

            def wide(self, row, g):
                return st[:, row, self.tiles(g)].unsqueeze(2).broadcast_to((P, TPG, C))

            def follow(self, dve, g, n):
                dve.wait_ge(g_link, g * 3 + (3 * self.n0 + n))

            def sum(self, dve, g):
                nc.vector.tensor_reduce(st[:, 0, self.tiles(g)], x_tok[:, self.tiles(g), :], AX.X, ALU.add,
                                        negate=True).then_inc(g_link, 1)

            def mean(self, dve, g):
                self.follow(dve, g, 1)
                mean = st[:, 0, self.tiles(g)]
                nc.vector.tensor_scalar(mean, mean, 1.0 / C, None, ALU.mult).then_inc(g_link, 1)

            def centre(self, dve, g):
                self.follow(dve, g, 2)
                nc.vector.tensor_tensor(xn_tok[:, self.tiles(g), :], x_tok[:, self.tiles(g), :], self.wide(0, g),
                                        ALU.add).then_inc(g_centred, 1)

            def square(self, act, g):
                act.wait_ge(g_centred, g + (self.n0 + 1))
                nc.scalar.activation(sq[:, self.tiles(g), :], xn_tok[:, self.tiles(g), :],
                                     ACT.Square).then_inc(g_squared, 1)

            def sum_squares(self, dve, g):
                dve.wait_ge(g_squared, g + (self.n0 + 1))
                nc.vector.tensor_reduce(st[:, 1, self.tiles(g)], sq[:, self.tiles(g), :], AX.X,
                                        ALU.add).then_inc(g_link, 1)

            def variance(self, dve, g):
                self.follow(dve, g, 3)
                nc.vector.tensor_scalar(st[:, 2, self.tiles(g)], st[:, 1, self.tiles(g)], 1.0 / C, self.eps,
                                        ALU.mult, ALU.add).then_inc(g_var, 1)

            def power(self, pool, g):
                pool.wait_ge(g_var, g + (self.n0 + 1))
                nc.gpsimd.tensor_tensor(st[:, 3, self.tiles(g)], st[:, 2, self.tiles(g)],
                                        neg_half[:, :].broadcast_to((P, TPG)), ALU.pow).then_inc(g_rstd, 1)

            def scale(self, dve, g):
                dve.wait_ge(g_rstd, g + (self.n0 + 1))
                if self.n0 > 0:
                    dve.wait_ge(g_turned, g + self.n0)
                nc.vector.tensor_tensor(xn_group[:, :, :], xn_tok[:, self.tiles(g), :], self.wide(3, g),
                                        ALU.mult).then_inc(g_scaled, 1)

            def keep(self, pool, g):
                pool.wait_ge(g_scaled, g + (self.n0 + 1))
                nc.gpsimd.tensor_copy(xn_tok[:, self.tiles(g), :], xn_group[:, :, :])

            def turn(self, pe, g):
                if self.n0 > 0:
                    pe.wait_ge(g_copied, g + self.n0)
                pe.wait_ge(g_scaled, g + (self.n0 + 1))
                pe.sem_inc(g_scaled_seen, 1)
                for t in range(TPG):
                    last = nc.tensor.transpose(ps[0:C, self.bank, t * P:(t + 1) * P], xn_group[:, t, :], idn[:, :])
                last.then_inc(g_turned, 1)

            def columns(self, g):
                return bass.ds(g * GTOK, GTOK)

            def copy(self, act, g):
                act.wait_ge(g_turned, g + (self.n0 + 1))
                if self.stacked:
                    nc.scalar.activation(x16[0:C, self.columns(g)], ps[0:C, self.bank, :], ACT.Copy,
                                         scale=TOKEN_SCALE).then_inc(g_high, 1)
                else:
                    nc.scalar.copy(xn_ch[0:C, self.columns(g)], ps[0:C, self.bank, :]).then_inc(g_copied, 1)

            def low(self, dve, g):
                dve.wait_ge(g_high, g + (self.h0 + 1))
                nc.vector.scalar_tensor_tensor(x16[C:P, self.columns(g)], ps[0:C, self.bank, :], TOKEN_SCALE,
                                               x16[0:C, self.columns(g)], ALU.mult, ALU.subtract).then_inc(g_copied, 1)

        def linear_attention():
            qvk_w = sbl("qvk_w", [P, 3 * HID0])
            qvk16 = sbl("qvk16", [P, 2, 3 * HID0], F16)
            K_COL = 2 * HID0
            CHUNK0 = HIDDEN0 // GROUPS
            out_w = sbl("out_w", [HID0, C])
            memory = sbl("memory", [C, MEM])
            head_mask = sbl("head_mask", [HID0, HID0])
            ln_rows = sbl("ln_rows", [P, 3, C])
            x_grp = sbl("x_grp", [P, GTOK], F16)
            k_mem = sbl("k_mem", [HID0, MEM])
            v_mem = sbl("v_mem", [MEM, HID0])
            nk_mem = sbl("nk_mem", [HID0, 1])
            nk_max = sbl("nk_max", [HID0, 2, 2])
            v_tok = sbl("v_tok", [P, TPG, HID0])
            k_exp = sbl("k_exp", [HID0, 2, N + MEM])
            k_sum = sbl("k_sum", [HID0, 2, 2])
            k_inv = sbl("k_inv", [HID0, 2])
            kt = sbl("kt", [P, TPG, HID0])
            kt_mem = sbl("kt_mem", [MEM, 2, HID0])
            ctx_t = sbl("ctx_t", [HID0, 2, HID0])
            mix = sbl("mix", [HID0, 2, C])
            q_tok = sbl("q_tok", [P, TPG, HEADS0, DH0])
            q_st = sbl("q_st", [P, 2, TPG, HEADS0])
            q_ch = sbl("q_ch", [HID0, GTOK])
            y_tok = sbl("y_tok", [P, 2, TPG, C])
            y_st = sbl("y_st", [P, 4, TPG])

            mem_ps, mem_kv = sem("l0_mem_ps"), sem("l0_mem_kv")
            qvk_high, qvk_low = sem("l0_qvk_high"), sem("l0_qvk_low")
            w_high_e = sem("l0_experts_w_high")
            x_copied, k_ps, qv_ps = sem("l0_x_copied"), sem("l0_k_ps"), sem("l0_qv_ps")
            k_max, k_exped, v_copied = sem("l0_k_max"), sem("l0_k_exped"), sem("l0_v_copied")
            q_shifted, q_exped, q_ready = sem("l0_q_shifted"), sem("l0_q_exped"), sem("l0_q_ready")
            kt_ps, kt_copied, ktm_copied = sem("l0_kt_ps"), sem("l0_kt_copied"), sem("l0_ktm_copied")
            ctx_ps, ctx_ready, mix_ps, mix_ready = (sem(f"l0_{n}") for n in ("ctx_ps", "ctx_ready", "mix_ps", "mix_ready"))
            qt_ps, qt_copied, y_ps = sem("l0_qt_ps"), sem("l0_qt_copied"), sem("l0_y_ps")
            y_sq_in, y_sq, y_var, y_rstd = sem("l0_y_sq_in"), sem("l0_y_sq"), sem("l0_y_var"), sem("l0_y_rstd")

            qv = ps[:, 0:2, :].rearrange("p w (t c) -> p w t c", c=HID0)
            q_ps = qv[:, 0, :, :].rearrange("p t (h d) -> p t h d", d=DH0)
            v_ps = qv[:, 1, :, :]
            kp = ps[:, 2, :].rearrange("p (b n) -> p b n", b=2)

            with nc.Block() as block:
                @block.sync
                def _(sp):
                    for half in range(2):
                        load(sp, "l0", qvk_w[half * C:(half + 1) * C, :], L0[0])
                    for dst, src in ((memory, L0[2]), (out_w, L0[1]), (head_mask, L0[3])):
                        load(sp, "l0", dst[:, :], src)
                    load(sp, "l0", ln_rows[:, :, :], L0[4].unsqueeze(0).broadcast_to((P, 3, C)))
                    for n in range(2 * GROUPS):
                        if n >= 2:
                            sp.wait_ge(w_split, n - 1)
                        src = F0[n // GROUPS][:, n % GROUPS * CHUNK0:(n % GROUPS + 1) * CHUNK0]
                        for half in range(2):
                            sp.dma_start(w_stage[half * C:(half + 1) * C, n % 2 * CHUNK0:(n % 2 + 1) * CHUNK0],
                                         src).then_inc(w_loaded[n % 2], 16)

                @block.scalar
                def _(act):
                    c = act_chain.on(act)
                    act.wait_ge(loaded["l0"], want["l0"])
                    nc.scalar.activation(qvk16[:, 0, :], qvk_w[:, :], ACT.Copy, scale=WEIGHT_SCALE).then_inc(qvk_high, 1)
                    nc.scalar.copy(x_grp[:, :], x16[:, 0:GTOK]).then_inc(x_copied, 1)
                    act.wait_ge(mem_ps, 1)
                    c.link(nc.scalar.copy(k_mem[:, :], ps[:, 4, 0:MEM]))
                    nc.scalar.copy(v_mem[:, :], ps[0:MEM, 4, 128:128 + HID0]).then_inc(mem_kv, 1)

                    def square(g):
                        act.wait_ge(y_sq_in, g + 1)
                        nc.scalar.activation(y_tok[:, 1, :, :], y_tok[:, 0, :, :], ACT.Square).then_inc(y_sq, 1)

                    def split_high(g, n):
                        act.wait_ge(w_loaded[n], g * 32 + 32)
                        nc.scalar.activation(w16[:, 0, bass.ds(g * (2 * CHUNK0) + n * CHUNK0, CHUNK0)],
                                             w_stage[:, n * CHUNK0:(n + 1) * CHUNK0], ACT.Copy,
                                             scale=WEIGHT_SCALE).then_inc(w_high_e, 1)

                    def group(g, first=False, last_group=False):
                        act.wait_ge(k_max, g + 1)
                        for b in range(2):
                            nc.scalar.activation(k_exp[:, b, 0:N], kp[:, b, :], ACT.Exp, scale=UNSCALE,
                                                 bias=nk_max[:, b, 1:2], accum_out=k_sum[:, b, 0:1])
                            last = nc.scalar.activation(k_exp[:, b, N:], k_mem[:, :], ACT.Exp,
                                                        bias=nk_max[:, b, 1:2], accum_out=k_sum[:, b, 1:2])
                        last.then_inc(k_exped, 1)
                        act.wait_ge(q_shifted, g + 1)
                        nc.scalar.activation(q_tok[:, :, :, :], q_tok[:, :, :, :], ACT.Exp,
                                             scale=UNSCALE).then_inc(q_exped, 1)
                        act.wait_ge(qv_ps, g + 1)
                        nc.scalar.activation(v_tok[:, :, :], v_ps, ACT.Copy, scale=UNSCALE).then_inc(v_copied, 1)
                        if not last_group:
                            nc.scalar.copy(x_grp[:, :], x16[:, bass.ds((g + 1) * GTOK, GTOK)]).then_inc(x_copied, 1)
                        split_high(g, 0)
                        act.wait_ge(kt_ps, g + 1)
                        nc.scalar.copy(kt_mem[:, :, :], ps[0:MEM, 4, 0:2 * HID0].rearrange(
                            "p (b d) -> p b d", b=2)).then_inc(ktm_copied, 1)
                        if not first:
                            square(g - 1)
                        act.wait_ge(qt_ps, g + 1)
                        nc.scalar.copy(q_ch[:, :], ps[:, 7, :]).then_inc(qt_copied, 1)
                        split_high(g, 1)

                    group(0, first=True)
                    with act.Fori(1, GROUPS - 1) as g:
                        group(g)
                    group(GROUPS - 1, last_group=True)
                    square(GROUPS - 1)

                @block.tensor
                def _(pe):
                    pe.wait_ge(loaded["l0"], want["l0"])
                    nc.tensor.matmul(ps[:, 4, 0:MEM], qvk_w[0:C, K_COL:], memory[:, :], start=True, stop=True)
                    nc.tensor.matmul(ps[0:MEM, 4, 128:128 + HID0], memory[:, :], qvk_w[0:C, HID0:2 * HID0],
                                     start=True, stop=True).then_inc(mem_ps, 1)
                    pe.wait_ge(mem_kv, 1)

                    def keys(g):
                        pe.wait_ge(x_copied, g + 1)
                        for part in range(2):
                            last = nc.tensor.matmul(ps[:, 2, :], qvk16[:, part, K_COL:], x_grp[:, :],
                                                    start=(part == 0), stop=(part == 1))
                        last.then_inc(k_ps, 1)

                    def queries_values(tiles):
                        for t in tiles:
                            for w in range(2):
                                for part in range(2):
                                    last = nc.tensor.matmul(qv[:, w, t, :], x_grp[:, t * P:(t + 1) * P],
                                                            qvk16[:, part, w * HID0:(w + 1) * HID0],
                                                            start=(part == 0), stop=(part == 1))
                        return last

                    def group(g, last_group=False):
                        pe.wait_ge(k_exped, g + 1)
                        for b in range(2):
                            for j in range(2):
                                nc.tensor.transpose(ps[:, 3, (2 * b + j) * P:(2 * b + j + 1) * P],
                                                    k_exp[:, b, j * P:(j + 1) * P], idn[:, :])
                            last = nc.tensor.transpose(ps[0:MEM, 4, b * P:(b + 1) * P],
                                                       k_exp[:, b, N:], idn[:, :])
                        last.then_inc(kt_ps, 1)
                        pe.wait_ge(q_ready, g + 1)
                        for t in range(TPG):
                            last = nc.tensor.transpose(ps[:, 7, t * P:(t + 1) * P],
                                                       q_tok[:, t, :, :].rearrange("p h d -> p (h d)"), idn[:, :])
                        last.then_inc(qt_ps, 1)
                        if not last_group:
                            keys(g + 1)
                        pe.wait_ge(v_copied, g + 1)
                        pe.wait_ge(kt_copied, g + 1)
                        pe.wait_ge(ktm_copied, g + 1)
                        for b in range(2):
                            o = ps[:, 5, b * P:(b + 1) * P]
                            for j in range(2):
                                nc.tensor.matmul(o, v_tok[:, 2 * b + j, :], kt[:, 2 * b + j, :],
                                                 start=(j == 0), stop=False)
                            last = nc.tensor.matmul(o, v_mem[:, :], kt_mem[:, b, :], start=False, stop=True)
                        last.then_inc(ctx_ps, 1)
                        if not last_group:
                            queries_values((0, 1))
                        pe.wait_ge(ctx_ready, g + 1)
                        for b in range(2):
                            last = nc.tensor.matmul(ps[:, 6, b * C:(b + 1) * C], ctx_t[:, b, :], out_w[:, :],
                                                    start=True, stop=True)
                        last.then_inc(mix_ps, 1)
                        if not last_group:
                            queries_values((2, 3)).then_inc(qv_ps, 1)
                        pe.wait_ge(mix_ready, g + 1)
                        pe.wait_ge(qt_copied, g + 1)
                        for t in range(TPG):
                            last = nc.tensor.matmul(ps[:, 6, 256 + t * C:256 + (t + 1) * C],
                                                    q_ch[:, t * P:(t + 1) * P], mix[:, t // 2, :],
                                                    start=True, stop=True)
                        last.then_inc(y_ps, 1)

                    pe.wait_ge(qvk_low, 1)
                    keys(0)
                    queries_values(range(TPG)).then_inc(qv_ps, 1)
                    with pe.Fori(0, GROUPS - 1) as g:
                        group(g)
                    group(GROUPS - 1, last_group=True)

                @block.gpsimd
                def _(pool):
                    with pool.Fori(0, GROUPS) as g:
                        pool.wait_ge(y_var, g + 1)
                        nc.gpsimd.tensor_tensor(y_st[:, 3, :], y_st[:, 2, :],
                                                neg_half[:, :].broadcast_to((P, TPG)), ALU.pow).then_inc(y_rstd, 1)

                @block.vector
                def _(dve):
                    c = dve_chain.on(dve)
                    dve.wait_ge(qvk_high, 1)
                    nc.vector.scalar_tensor_tensor(qvk16[:, 1, :], qvk_w[:, :], WEIGHT_SCALE, qvk16[:, 0, :],
                                                   ALU.mult, ALU.subtract).then_inc(qvk_low, 1)
                    dve.wait_ge(mem_kv, 1)
                    c.link(nc.vector.tensor_reduce(nk_mem[:, :], k_mem[:, :], AX.X, ALU.max, negate=True))
                    y, y2 = y_tok[:, 0, :, :], y_tok[:, 1, :, :]

                    def wide4(v, n=C):
                        return v.unsqueeze(2).broadcast_to((P, TPG, n))

                    def rows(r):
                        return ln_rows[:, r, :].unsqueeze(1).broadcast_to((P, TPG, C))

                    def centre(g):
                        dve.wait_ge(y_ps, g + 1)
                        c.link(nc.vector.tensor_tensor(y, ps[:, 6, 256:512].rearrange("p (t c) -> p t c", t=TPG),
                                                       rows(0), ALU.add))
                        c.link(nc.vector.tensor_reduce(y_st[:, 0, :], y, AX.X, ALU.add, negate=True))
                        c.link(nc.vector.tensor_scalar(y_st[:, 0, :], y_st[:, 0, :], 1.0 / C, None, ALU.mult))
                        nc.vector.tensor_tensor(y, y, wide4(y_st[:, 0, :]), ALU.add).then_inc(y_sq_in, 1)

                    def variance(g):
                        dve.wait_ge(y_sq, g + 1)
                        c.link(nc.vector.tensor_reduce(y_st[:, 1, :], y2, AX.X, ALU.add))
                        nc.vector.tensor_scalar(y_st[:, 2, :], y_st[:, 1, :], 1.0 / C, 1e-5,
                                                ALU.mult, ALU.add).then_inc(y_var, 1)

                    def finish(g):
                        dve.wait_ge(y_rstd, g + 1)
                        c.link(nc.vector.tensor_tensor(y, y, wide4(y_st[:, 3, :]), ALU.mult))
                        c.link(nc.vector.tensor_tensor(y, y, rows(1), ALU.mult))
                        c.link(nc.vector.tensor_tensor(y, y, rows(2), ALU.add))
                        xg = x_tok[:, bass.ds(g * TPG, TPG), :]
                        c.link(nc.vector.tensor_tensor(xg, xg, y, ALU.add))

                    def split_low(g, n):
                        dve.wait_ge(w_high_e, 2 * g + (n + 1))
                        col = g * (2 * CHUNK0) + n * CHUNK0
                        nc.vector.scalar_tensor_tensor(w16[:, 1, bass.ds(col, CHUNK0)],
                                                       w_stage[:, n * CHUNK0:(n + 1) * CHUNK0], WEIGHT_SCALE,
                                                       w16[:, 0, bass.ds(col, CHUNK0)], ALU.mult,
                                                       ALU.subtract).then_inc(w_split, 1)

                    def group(g, first=False):
                        dve.wait_ge(k_ps, g + 1)
                        c.link(nc.vector.tensor_reduce(nk_max[:, :, 0], kp, AX.X, ALU.max, negate=True))
                        nc.vector.scalar_tensor_tensor(nk_max[:, :, 1], nk_max[:, :, 0], UNSCALE,
                                                       nk_mem[:, :].broadcast_to((HID0, 2)),
                                                       ALU.mult, ALU.min).then_inc(k_max, 1)
                        dve.wait_ge(qv_ps, g + 1)
                        c.link(nc.vector.tensor_reduce(q_st[:, 0, :, :], q_ps, AX.X, ALU.max))
                        nc.vector.tensor_tensor(q_tok[:, :, :, :], q_ps,
                                                q_st[:, 0, :, :].unsqueeze(3).broadcast_to((P, TPG, HEADS0, DH0)),
                                                ALU.subtract).then_inc(q_shifted, 1)
                        if not first:
                            centre(g - 1)
                        dve.wait_ge(q_exped, g + 1)
                        c.link(nc.vector.tensor_reduce(q_st[:, 0, :, :], q_tok[:, :, :, :], AX.X, ALU.add))
                        c.link(nc.vector.reciprocal(q_st[:, 1, :, :], q_st[:, 0, :, :]))
                        nc.vector.tensor_tensor(q_tok[:, :, :, :], q_tok[:, :, :, :],
                                                q_st[:, 1, :, :].unsqueeze(3).broadcast_to((P, TPG, HEADS0, DH0)),
                                                ALU.mult).then_inc(q_ready, 1)
                        dve.wait_ge(kt_ps, g + 1)
                        nc.vector.tensor_copy(kt[:, :, :], ps[:, 3, :].rearrange(
                            "p (t d) -> p t d", t=TPG)).then_inc(kt_copied, 1)
                        c.link(nc.vector.tensor_tensor(k_inv[:, :], k_sum[:, :, 0], k_sum[:, :, 1], ALU.add))
                        c.link(nc.vector.reciprocal(k_inv[:, :], k_inv[:, :]))
                        c.link(nc.vector.tensor_scalar(k_inv[:, :], k_inv[:, :], DH0 ** -0.5, None, ALU.mult))
                        if not first:
                            variance(g - 1)
                        split_low(g, 0)
                        if not first:
                            finish(g - 1)
                        dve.wait_ge(ctx_ps, g + 1)
                        nc.vector.tensor_tensor(ctx_t[:, :, :],
                                                ps[:, 5, 0:2 * P].rearrange("p (b d) -> p b d", b=2),
                                                head_mask[:, :].unsqueeze(1).broadcast_to((P, 2, HID0)),
                                                ALU.mult).then_inc(ctx_ready, 1)
                        split_low(g, 1)
                        dve.wait_ge(mix_ps, g + 1)
                        for b in range(2):
                            last = nc.vector.tensor_scalar(mix[:, b, :], ps[:, 6, b * C:(b + 1) * C],
                                                           k_inv[:, b:b + 1], None, ALU.mult)
                        last.then_inc(mix_ready, 1)

                    group(0, first=True)
                    with dve.Fori(1, GROUPS) as g:
                        c.loop(g, 15, start=1)
                        group(g)
                    c.end(GROUPS - 1)
                    for part in (centre, variance, finish):
                        part(GROUPS - 1)

        router_ps, exp_in, exp_done = (sem(f"moe_{n}") for n in ("router_ps", "exp_in", "exp_done"))
        parts_ready, gates_ps, gates_copied = (sem(f"moe_{n}") for n in ("parts_ready", "gates_ps", "gates_copied"))
        h_ps, h_act, h_mul, h_gated = sem("moe_h_ps"), sem("moe_h_act"), sem("moe_h_mul"), sem("moe_h_gated")
        gate_ps, gate_copied = sem("moe_gate_ps"), sem("moe_gate_copied")
        y_ps, y_copied, yt_ps = sem("moe_y_ps"), sem("moe_y_copied"), sem("moe_yt_ps")
        s_cast = sem("moe_cast")
        at = dict.fromkeys(("phase", "tiles", "acts", "muls", "selects", "chunks", "small"), 0)

        def load_small(eng, F):
            _, _, w2_d, b1_d, b2_d, router_d, router_b_d = F
            load(eng, "f", w2[:, 0:w2_d.shape[1]], w2_d)
            for half in range(2):
                load(eng, "f", router_w[half * C:(half + 1) * C, :], router_d)
            load(eng, "f", router_b[:, :], router_b_d.broadcast_to((P, E)))
            if b1_d is not None:
                load(eng, "f", b1_col[:, 0:b1_d.shape[1]], b1_d)
                load(eng, "f", b2_rows[:, :], b2_d)

        def split_weights(chunks, engines):
            sp, act, dve = engines
            n0 = at["chunks"]
            if sp is not None:
                for n, (src, _) in enumerate(chunks):
                    m = n0 + n
                    width = src.shape[1]
                    if m >= 4:
                        sp.wait_ge(w_split, 2 * GROUPS + m - 3)
                    for half in range(2):
                        sp.dma_start(w_stage[half * C:(half + 1) * C, m % 4 * STAGE:m % 4 * STAGE + width],
                                     src).then_inc(w_loaded[m % 4], 16)
            if act is not None:
                for n, (src, col) in enumerate(chunks):
                    m = n0 + n
                    width = src.shape[1]
                    act.wait_ge(w_loaded[m % 4], 32 * (m // 4 + 1 + (GROUPS if m % 4 < 2 else 0)))
                    nc.scalar.activation(w16[:, 0, col:col + width], w_stage[:, m % 4 * STAGE:m % 4 * STAGE + width],
                                         ACT.Copy, scale=WEIGHT_SCALE).then_inc(w_high, 1)
            if dve is not None:
                for n, (src, col) in enumerate(chunks):
                    m = n0 + n
                    width = src.shape[1]
                    dve.wait_ge(w_high, m + 1)
                    nc.vector.scalar_tensor_tensor(w16[:, 1, col:col + width],
                                                   w_stage[:, m % 4 * STAGE:m % 4 * STAGE + width], WEIGHT_SCALE,
                                                   w16[:, 0, col:col + width], ALU.mult,
                                                   ALU.subtract).then_inc(w_split, 1)

        def chunks_of(F):
            out = []
            for base, w_d in ((0, F[0]), (HIDDEN0, F[1])):
                if w_d is not None:
                    for c in range(0, w_d.shape[1], STAGE):
                        out.append((w_d[:, c:c + STAGE], base + c))
            return out

        def experts(tiles, func, swiglu, gating, F, add_tokens=False, also=None, norm=None):
            J = len(tiles)
            assert J % 4 == 0
            act_h = sbl("act_h", [P, 4, GTOK])
            mul_h = sbl("mul_h", [P, 4, GTOK])
            gate_sb = sbl("gate_sb", [P, 3, GTOK])
            hid = sbl("hid", [P, 4, GTOK])
            y_sb = sbl("y_sb", [P, GTOK])
            p0, v0, m0, g0 = at["phase"], at["tiles"], at["muls"], at["selects"]
            a0 = at["acts"]
            new_select = [j == 0 or tiles[j][2] != tiles[j - 1][2] for j in range(J)]
            select_no = [sum(new_select[:j + 1]) - 1 for j in range(J)]
            SPG = sum(new_select)
            at["phase"] += 1
            at["tiles"] += J * GROUPS
            at["acts"] += J * GROUPS
            at["muls"] += J * GROUPS if swiglu else 0
            at["selects"] += SPG * GROUPS if swiglu else 0
            H_BANKS, H3, GATE, YT, Y, LOGITS = 2, 2, (4 if swiglu else 2), 5, 6, 7
            LAG = 2 if swiglu else 1
            Y_COPY, Y_TURN, Y_ADD = J + LAG, J + LAG + 1, J + LAG + 2
            N_SQUARE, N_TURN, N_COPY = Y_ADD + 4, Y_ADD + 10, Y_ADD + 12
            END = Y_ADD if norm is None else N_COPY
            DEPTH = END // J

            def group_of(k, i, off):
                if (k - off) % J:
                    return None
                r = (k - off) // J
                if isinstance(i, int) and not 0 <= i + r < GROUPS:
                    return None
                return i + r

            def tile_of(k, i, lag):
                n = k + lag
                if isinstance(i, int) and not 0 <= i * J + n < J * GROUPS:
                    return None
                return n % J, i * J + (n + 1), i + n // J

            def stream(eng, step):
                for i in range(DEPTH):
                    for k in range(J):
                        step(i, k)
                with eng.Fori(DEPTH, GROUPS - 1) as i:
                    for k in range(J):
                        step(i, k)
                for k in range(END + 1):
                    step(GROUPS - 1, k)

            with nc.Block() as block:
                if also is not None:
                    block.sync(also)

                if norm is not None:
                    @block.gpsimd
                    def _(pool):
                        with pool.Fori(0, GROUPS) as g:
                            norm.power(pool, g)
                            norm.keep(pool, g)

                @block.tensor
                def _(pe):
                    for t in range(NT):
                        for part in range(2):
                            last = nc.tensor.matmul(ps[:, LOGITS, t * E:(t + 1) * E], x16[:, t * P:(t + 1) * P],
                                                    router16[:, part, :], start=(part == 0), stop=(part == 1))
                    last.then_inc(router_ps, 1)
                    pe.wait_ge(parts_ready, p0 + 1)
                    for t in range(NT):
                        o = ps[0:KG, t // 8, :].bitcast(BF16)
                        last = nc.tensor.transpose(o[:, t % 8 * P:(t % 8 + 1) * P], gate_parts[:, t, :], idn_bf[:, :])
                        if t % 8 == 7:
                            last.then_inc(gates_ps, 1)
                    pe.wait_ge(gates_copied, 4 * (p0 + 1))

                    def hidden(i, k):
                        if (tile := tile_of(k, i, 1)) is None:
                            return
                        j, count, g = tile
                        col = tiles[j][0]
                        xg = x16[:, bass.ds(g * GTOK, GTOK)]
                        reused = not isinstance(i, int) or i * J + k + 1 >= H_BANKS
                        if reused:
                            pe.wait_ge(h_act, count + (a0 - H_BANKS))
                        for part in range(2):
                            last = nc.tensor.matmul(ps[:, j % H_BANKS, :], w16[:, part, col:col + P], xg,
                                                    start=(part == 0), stop=(part == 1))
                        if swiglu:
                            if reused:
                                pe.wait_ge(h_mul, count + (m0 - H_BANKS))
                            for part in range(2):
                                last = nc.tensor.matmul(ps[:, H3 + j % H_BANKS, :],
                                                        w16[:, part, HIDDEN0 + col:HIDDEN0 + col + P], xg,
                                                        start=(part == 0), stop=(part == 1))
                        last.then_inc(h_ps, 1)

                    def gate(i, k):
                        if (tile := tile_of(k, i, 1)) is None or not new_select[tile[0]]:
                            return
                        j, _, g = tile
                        if swiglu and (not isinstance(i, int) or i * J + k + 1 > 0):
                            pe.wait_ge(gate_copied, g * SPG + (g0 + select_no[j]))
                        bank = GATE if swiglu else GATE + select_no[j] % 2
                        nc.tensor.matmul(ps[:, bank, :], selector[:, tiles[j][2], :],
                                         gate_t[:, bass.ds(g * GTOK, GTOK)], start=True, stop=True).then_inc(gate_ps, 1)

                    def step(i, k):
                        hidden(i, k)
                        if (tile := tile_of(k, i, -LAG)) is not None:
                            j, count, g = tile
                            if j == 0 and group_of(k, i, J + LAG) is not None:
                                pe.wait_ge(y_copied, g + GROUPS * p0)
                                pe.sem_inc(y_bank_free, 1)
                            if j == 0 and not swiglu:
                                for part in range(3):
                                    nc.tensor.matmul(ps[0:C, Y, :], b2_parts[:, part, :],
                                                     gate_t[:, bass.ds(g * GTOK, GTOK)],
                                                     start=(part == 0), stop=False, skip_group_check=True)
                            pe.wait_ge(h_gated, count + v0)
                            half = (j + (0 if swiglu else 1)) % 2
                            last = nc.tensor.matmul(ps[half * C:(half + 1) * C, Y, :],
                                                    w2[:, tiles[j][1]:tiles[j][1] + C], hid[:, j % 4, :],
                                                    start=(j < (2 if swiglu else 1)), stop=(j >= J - 2),
                                                    skip_group_check=True)
                            if j == J - 1:
                                last.then_inc(y_ps, 1)
                        gate(i, k)
                        if (g := group_of(k, i, Y_TURN)) is not None:
                            pe.wait_ge(y_copied, g + (GROUPS * p0 + 1))
                            if p0 > 0 and (not isinstance(g, int) or g > 0):
                                pe.wait_ge(added, g * 2 + 2 * GROUPS * p0)
                            for t in range(TPG):
                                last = nc.tensor.transpose(ps[:, YT, t * P:(t + 1) * P],
                                                           y_sb[:, t * P:(t + 1) * P], idn[:, :])
                            last.then_inc(yt_ps, 1)
                        if norm is not None and (g := group_of(k, i, N_TURN)) is not None:
                            norm.turn(pe, g)

                    hidden(0, -1)
                    gate(0, -1)
                    stream(pe, step)

                @block.scalar
                def _(act):
                    act.wait_ge(exp_in, p0 + 1)
                    nc.scalar.activation(rt[:, 1, :, :], rt[:, 1, :, :], ACT.Exp).then_inc(exp_done, 1)
                    for n in (0, 2):
                        act.wait_ge(gates_ps, 4 * p0 + n + 1)
                        nc.scalar.copy(gate_t[:, n * 2 * GTOK:(n + 1) * 2 * GTOK],
                                       ps[0:KG, n, :].bitcast(BF16)).then_inc(gates_copied, 1)

                    def step(i, k):
                        if (tile := tile_of(k, i, 0)) is not None:
                            j, count, g = tile
                            act.wait_ge(h_ps, count + v0)
                            bias = 0.0 if swiglu else b1_col[:, j:j + 1]
                            nc.scalar.activation(act_h[:, j % 4, :], ps[:, j % H_BANKS, :], func,
                                                 bias=bias, scale=UNSCALE).then_inc(h_act, 1)
                            if swiglu and new_select[j]:
                                act.wait_ge(gate_ps, g * SPG + (gp0 + select_no[j] + 1))
                                nc.scalar.copy(gate_sb[:, select_no[j] % 3, :], ps[:, GATE, :]).then_inc(gate_copied, 1)
                        if (g := group_of(k, i, Y_COPY)) is not None:
                            act.wait_ge(y_ps, g + (GROUPS * p0 + 1))
                            nc.scalar.copy(y_sb[:, :], ps[:, Y, :]).then_inc(y_copied, 1)
                        if norm is not None:
                            if (g := group_of(k, i, N_SQUARE)) is not None:
                                norm.square(act, g)
                            if (g := group_of(k, i, N_COPY)) is not None:
                                norm.copy(act, g)

                    gp0 = at["small"]
                    stream(act, step)

                @block.vector
                def _(dve):
                    c = dve_chain.on(dve)
                    dve.wait_ge(router_ps, p0 + 1)
                    logits, ex = rt[:, 0, :, :], rt[:, 1, :, :]
                    hot1, hot2, tmp, rest = (rt[:, n, :, :] for n in (2, 3, 4, 5))
                    mx, r1, total, top, inv, inv2 = (rs[:, n, :] for n in range(6))

                    def wide(v):
                        return v.unsqueeze(2).broadcast_to((P, NT, E))

                    ranks = rank[:, :].unsqueeze(1).broadcast_to((P, NT, E))
                    c.link(nc.vector.tensor_scalar(logits, ps[:, LOGITS, 0:NT * E].rearrange(
                        "p (t e) -> p t e", e=E), UNSCALE, None, ALU.mult))
                    c.link(nc.vector.tensor_tensor(logits, logits, router_b[:, :].unsqueeze(1).broadcast_to((P, NT, E)),
                                                   ALU.add))
                    c.link(nc.vector.tensor_reduce(mx, logits, AX.X, ALU.max))
                    nc.vector.tensor_tensor(ex, logits, wide(mx), ALU.subtract).then_inc(exp_in, 1)

                    def one_hot(hot, values):
                        c.link(nc.vector.tensor_tensor(tmp, values, wide(mx), ALU.is_equal))
                        c.link(nc.vector.tensor_tensor(tmp, tmp, ranks, ALU.mult))
                        c.link(nc.vector.tensor_reduce(r1, tmp, AX.X, ALU.max))
                        c.link(nc.vector.tensor_tensor(hot, ranks, wide(r1), ALU.is_equal))

                    one_hot(hot1, logits)
                    c.link(nc.vector.scalar_tensor_tensor(rest, hot1, -3e38, logits, ALU.mult, ALU.add))
                    c.link(nc.vector.tensor_reduce(mx, rest, AX.X, ALU.max))
                    one_hot(hot2, rest)
                    c.link(nc.vector.tensor_tensor(hot1, hot1, hot2, ALU.add))
                    dve.wait_ge(exp_done, p0 + 1)
                    c.link(nc.vector.tensor_tensor(hot1, hot1, ex, ALU.mult))
                    c.link(nc.vector.tensor_reduce(total, ex, AX.X, ALU.add))
                    c.link(nc.vector.tensor_reduce(top, hot1, AX.X, ALU.add))
                    if gating == "two":
                        c.link(nc.vector.reciprocal(inv, top))
                    else:
                        c.link(nc.vector.reciprocal(inv, total))
                    if gating in ("plus", "floor"):
                        op, eps = (ALU.add, 1e-9) if gating == "plus" else (ALU.max, 1e-12)
                        c.link(nc.vector.tensor_tensor(top, top, inv, ALU.mult))
                        c.link(nc.vector.tensor_scalar(top, top, eps, None, op))
                        c.link(nc.vector.reciprocal(inv2, top))
                        c.link(nc.vector.tensor_tensor(inv, inv, inv2, ALU.mult))
                    c.link(nc.vector.tensor_tensor(hot1, hot1, wide(inv), ALU.mult))
                    for n, p_at in enumerate(PARTS_AT):
                        part = gate_parts[:, :, p_at:p_at + E]
                        if n == 2:
                            nc.vector.tensor_copy(part, hot1).then_inc(parts_ready, 1)
                            break
                        c.link(nc.vector.tensor_copy(part, hot1))
                        c.link(nc.vector.tensor_tensor(hot1, hot1, part, ALU.subtract))
                    if add_tokens:
                        c.link(nc.vector.tensor_tensor(x_tok[:, :, :], x_tok[:, :, :], xn_tok[:, :, :], ALU.add))
                    for n in (1, 3):
                        dve.wait_ge(gates_ps, 4 * p0 + n + 1)
                        nc.vector.tensor_copy(gate_t[:, n * 2 * GTOK:(n + 1) * 2 * GTOK],
                                              ps[0:KG, n, :].bitcast(BF16)).then_inc(gates_copied, 1)

                    gp0 = at["small"]

                    def step(i, k):
                        if swiglu and (tile := tile_of(k, i, 0)) is not None:
                            j, count, _ = tile
                            dve.wait_ge(h_act, count + a0)
                            nc.vector.scalar_tensor_tensor(mul_h[:, j % 4, :], ps[:, H3 + j % H_BANKS, :], UNSCALE,
                                                           act_h[:, j % 4, :], ALU.mult, ALU.mult).then_inc(h_mul, 1)
                        if (tile := tile_of(k, i, 1 - LAG)) is not None:
                            j, count, g = tile
                            if swiglu:
                                dve.wait_ge(h_mul, count + m0)
                                if new_select[j]:
                                    dve.wait_ge(gate_copied, g * SPG + (g0 + select_no[j] + 1))
                                values, gates_ = mul_h[:, j % 4, :], gate_sb[:, select_no[j] % 3, :]
                            else:
                                dve.wait_ge(h_act, count + a0)
                                if new_select[j]:
                                    dve.wait_ge(gate_ps, g * SPG + (gp0 + select_no[j] + 1))
                                values, gates_ = act_h[:, j % 4, :], ps[:, GATE + select_no[j] % 2, :]
                            nc.vector.tensor_tensor(hid[:, j % 4, :], values, gates_, ALU.mult).then_inc(h_gated, 1)
                        if (g := group_of(k, i, Y_ADD)) is not None:
                            dve.wait_ge(yt_ps, g + (GROUPS * p0 + 1))
                            xg = x_tok[:, bass.ds(g * TPG, TPG), :]
                            yt = ps[:, YT, :].rearrange("p (t a c) -> p t a c", t=TPG, a=2)
                            for half in range(2):
                                nc.vector.tensor_tensor(xg, xg, yt[:, :, half, :], ALU.add).then_inc(added, 1)
                                dve.wait_ge(added, g * 2 + (2 * GROUPS * p0 + half + 1))
                        if norm is not None:
                            for part, at_step in ((norm.sum, 1), (norm.mean, 2), (norm.centre, 3),
                                                  (norm.sum_squares, 6), (norm.variance, 7), (norm.scale, 9)):
                                if (g := group_of(k, i, Y_ADD + at_step)) is not None:
                                    part(dve, g)

                    stream(dve, step)
                    at["small"] += SPG * GROUPS

        added, y_bank_free = sem("moe_added"), sem("moe_y_bank_free")

        def cast_small(act, dve, biases):
            n = at["cast"]
            if act is not None:
                act.wait_ge(loaded["f"], want["f"])
                nc.scalar.activation(router16[:, 0, :], router_w[:, :], ACT.Copy, scale=WEIGHT_SCALE).then_inc(s_cast, 1)
            if dve is not None:
                dve.wait_ge(s_cast, n + 1)
                nc.vector.scalar_tensor_tensor(router16[:, 1, :], router_w[:, :], WEIGHT_SCALE, router16[:, 0, :],
                                               ALU.mult, ALU.subtract)
                if biases:
                    c = dve_chain.on(dve)
                    c.link(nc.vector.tensor_copy(b2_parts[:, 0, :], b2_rows[:, :]))
                    c.link(nc.vector.tensor_tensor(b2_rest[:, :], b2_rows[:, :], b2_parts[:, 0, :], ALU.subtract))
                    c.link(nc.vector.tensor_copy(b2_parts[:, 1, :], b2_rest[:, :]))
                    c.link(nc.vector.tensor_tensor(b2_rest[:, :], b2_rest[:, :], b2_parts[:, 1, :], ALU.subtract))
                    nc.vector.tensor_copy(b2_parts[:, 2, :], b2_rest[:, :])

        at["cast"] = 0

        def prepare_experts(F, sp=None, act=None, dve=None):
            split_weights(chunks_of(F), (sp, act, dve))
            cast_small(act, dve, F[4] is not None)

        def start_loads(F):
            with nc.Block() as block:
                @block.sync
                def _(sp):
                    load_small(sp, F)

        def bias_bands(sp):
            bands = L1["scratch"]
            for j in range(SIDE):
                sp.dma_start(bands[j, :, :, :], table.rearrange("h (a b) -> h a b", b=REL)
                             [:, :, SIDE - 1 - j:REL - j]).then_inc(b_dram, 16)
            sp.wait_ge(b_dram, 16 * SIDE)
            for i in range(SIDE):
                r0 = i % (SIDE // 2) * SIDE
                load(sp, "l1", rel_bias[r0:r0 + SIDE, i // (SIDE // 2), :, :],
                     bands[:, :, SIDE - 1 - i:REL - i, :].rearrange("j h k l -> j h (k l)"))

        def attention():
            qkv_w = sbl("qkv_w", [KC, 3 * C])
            proj_w = sbl("proj_w", [KC, C])
            scale = sbl("scale", [P, 2 * HEADS1])
            qk = sbl("qk", [P, NT, 2 * C])
            vals = sbl("vals", [P, NT, HEADS1, VPAD])
            o_heads = sbl("o_heads", [P, GTOK])
            QK_T = B * 8 * P
            flat = w16[:, :, :].rearrange("p a n -> p (a n)")
            qk_t = flat[:, 0:QK_T].rearrange("p (b n) -> p b n", b=B)
            norm = flat[:, QK_T:QK_T + 12 * NT * HEADS1].bitcast(F32).rearrange(
                "p (k t h) -> p k t h", k=3, t=NT)
            parts = x16[:, :].rearrange("p (q t w h a d) -> p q t w h a d", q=2, t=TPG, w=2, h=HEADS1, a=4)
            qk_b = x16[:, T // 2:].rearrange("p (q w s j n) -> p q w s j n", q=2, w=2, s=2, j=2)
            prob = sq[:, :, :].rearrange("p t c -> p (t c)").rearrange("p (b a n) -> p b a n", b=4, a=2)
            prob_t = w_stage[:, :].rearrange("p (b n) -> p b n", b=4)
            x_grp = gate_t[0:KC, 0:T // 2].bitcast(F32).rearrange("k (q n) -> k q n", q=2)
            squares = sq[:, 0:16, :].rearrange("p t c -> p (t c)").rearrange("p (q t c) -> p q t c", q=2, t=TPG)
            lows = w_stage[:, 0:2 * GTOK].rearrange("p (q t c) -> p q t c", q=2, t=TPG)
            banks_free = sem("l1_banks_free")
            val_b = rt[:, 0:4, :, :].rearrange("p k t e -> p (k t e)").rearrange(
                "p (q m h v) -> p q m h v", q=2, m=2, v=VPAD)
            nmax = sbl("nmax", [P, 4, 2])
            inv_sum = sbl("inv_sum", [P, 2 * HEADS1])
            o_tok = sbl("o_tok", [P, 2, HEADS1, DH1])
            o_ch = sbl("o_ch", [KC, N])

            x_copied, qkv_ps, qk_sq, sums = (sem(f"l1_{n}") for n in ("x_copied", "qkv_ps", "qk_sq", "sums"))
            setup, w_ready, sums_inverted = sem("l1_setup"), sem("l1_w_ready"), sem("l1_sums_inverted")
            rooted = sem("l1_rooted")
            split, turned, t_copied = sem("l1_split"), sem("l1_turned"), sem("l1_t_copied")

            with nc.Block() as block:
                @block.sync
                def _(sp):
                    load(sp, "l1", qkv_w[:, :], L1["qkv_w"])
                    load(sp, "l1", proj_w[:, :], L1["proj_w"])
                    load(sp, "l1", scale[:, :], L1["scale"].unsqueeze(0).broadcast_to((P, 2 * HEADS1)))

                @block.gpsimd
                def _(pool):
                    nc.gpsimd.memset(vals[:, :, :, DH1:VW], 1.0)
                    pool_chain.on(pool).link(nc.gpsimd.memset(vals[:, :, :, VW:], 0.0))
                    nc.gpsimd.memset(o_ch[C:KC, :], 1.0)

                @block.scalar
                def _(act):
                    def copy_tokens(g, q):
                        if is_group(g):
                            nc.scalar.copy(x_grp[:, q, :], xn_ch[:, bass.ds(g * GTOK, GTOK)]).then_inc(x_copied, 1)

                    def step(g, q):
                        copy_tokens(g + 1, 1 - q)
                        act.wait_ge(qkv_ps, g + 1)
                        banks = slice(TPG * q, TPG * (q + 1))
                        nc.scalar.copy(qk[:, bass.ds(g * TPG, TPG), :], ps[:, banks, 0:2 * C])
                        nc.scalar.copy(vals[:, bass.ds(g * TPG, TPG), :, 0:DH1],
                                       ps[:, banks, 2 * C:3 * C].rearrange("p t (h d) -> p t h d", d=DH1))
                        if from_third(g):
                            act.wait_ge(sums, g - 1)
                        nc.scalar.activation(squares[:, q, :, :], ps[:, banks, 0:2 * C], ACT.Square).then_inc(qk_sq, 1)

                    copy_tokens(0, 0)
                    pairs(act, step)

                @block.tensor
                def _(pe):
                    def step(g, q):
                        pe.wait_ge(x_copied, g + 1)
                        for t in range(TPG):
                            last = nc.tensor.matmul(ps[:, TPG * q + t, 0:3 * C], x_grp[:, q, t * P:(t + 1) * P],
                                                    qkv_w[:, :], start=True, stop=True)
                        last.then_inc(qkv_ps, 1)

                    pe.wait_ge(w_ready, 3)
                    pairs(pe, step)

                @block.vector
                def _(dve):
                    def step(g, q):
                        dve.wait_ge(qk_sq, g + 1)
                        nc.vector.tensor_reduce(norm[:, 0, bass.ds(g * TPG, TPG), :],
                                                squares[:, q, :, :].rearrange("p t (h d) -> p t h d", d=DH1),
                                                AX.X, ALU.add).then_inc(sums, 1)

                    dve.wait_ge(loaded["l1"], want["l1"])
                    for n in range(3):
                        w = qkv_w[0:C, n * C:(n + 1) * C]
                        nc.vector.tensor_tensor(w, w, idn[0:C, 0:C], ALU.add).then_inc(w_ready, 1)
                    pairs(dve, step)

            with nc.Block() as block:
                @block.vector
                def _(dve):
                    c = dve_chain.on(dve)
                    ss, y, t = norm[:, 0, :, :], norm[:, 1, :, :], norm[:, 2, :, :]
                    nc.vector.tensor_scalar(ss, ss, 1e-24, None, ALU.max).then_inc(setup, 1)
                    sq_ = scale[:, 0:HEADS1]
                    dve.wait_ge(setup, 1)
                    nc.vector.tensor_scalar(sq_, sq_, float(np.log(np.float32(1.0 / 0.01))), None, ALU.min).then_inc(setup, 1)
                    dve.wait_ge(rooted, 2)
                    c.link(nc.vector.tensor_scalar(sq_, sq_, -1.0, None, ALU.mult))
                    c.link(nc.vector.reciprocal(y, y))
                    c.link(nc.vector.tensor_tensor(t, y, y, ALU.mult))
                    c.link(nc.vector.tensor_tensor(t, t, ss, ALU.mult))
                    c.link(nc.vector.tensor_scalar(t, t, -0.5, 1.5, ALU.mult, ALU.add))
                    c.link(nc.vector.tensor_tensor(y, y, t, ALU.mult))
                    c.link(nc.vector.tensor_tensor(y, y, scale[:, :].unsqueeze(1).broadcast_to((P, NT, 2 * HEADS1)),
                                                   ALU.mult))

                @block.scalar
                def _(act):
                    act.wait_ge(setup, 1)
                    nc.scalar.activation(norm[:, 1, :, :], norm[:, 0, :, :], ACT.Sqrt).then_inc(rooted, 1)
                    act.wait_ge(setup, 2)
                    nc.scalar.activation(scale[:, 0:HEADS1], scale[:, 0:HEADS1], ACT.Exp).then_inc(rooted, 1)

            with nc.Block() as block:
                @block.vector
                def _(dve):
                    c = dve_chain.on(dve)

                    def step(g, q):
                        low = lows[:, q, :, :]
                        part = parts[:, q, :, :, :, :, :]
                        c.link(nc.vector.tensor_tensor(
                            low.rearrange("p t (h d) -> p t h d", d=DH1),
                            qk[:, bass.ds(g * TPG, TPG), :].rearrange("p t (h d) -> p t h d", d=DH1),
                            norm[:, 1, bass.ds(g * TPG, TPG), :].unsqueeze(3).broadcast_to((P, TPG, 2 * HEADS1, DH1)),
                            ALU.mult))
                        if from_third(g):
                            dve.wait_ge(turned, g - 1)
                        c.link(nc.vector.tensor_copy(
                            part.rearrange("p t w h a d -> p t (w h) a d")[:, :, :, 0, :],
                            low.rearrange("p t (h d) -> p t h d", d=DH1)))
                        low5 = low.rearrange("p t (w h d) -> p t w h d", w=2, d=DH1)
                        for w, lo in enumerate((1, 2)):
                            last = nc.vector.tensor_tensor(part[:, :, w, :, lo, :], low5[:, :, w, :, :],
                                                           part[:, :, w, :, 0, :], ALU.subtract)
                        c.link(last)
                        for w, (lo, hi) in enumerate(((1, 2), (2, 1))):
                            nc.vector.tensor_copy(part[:, :, w, :, hi, :], part[:, :, w, :, 0, :])
                            last = nc.vector.tensor_copy(part[:, :, w, :, 3, :], part[:, :, w, :, lo, :])
                        last.then_inc(split, 1)

                    pairs(dve, step, c, 3)

                @block.tensor
                def _(pe):
                    def step(g, q):
                        pe.wait_ge(split, g + 1)
                        if from_third(g):
                            pe.wait_ge(t_copied, g)
                            pe.sem_inc(banks_free, 1)
                        else:
                            pe.wait_ge(t_copied, 1)
                        for b in range(2):
                            for w in range(2):
                                for s in range(2):
                                    for j in range(2):
                                        n = (w * 2 + s) * 2 + j
                                        last = nc.tensor.transpose(
                                            ps[:, 2 * q + b, n * (P // 2):(n + 1) * (P // 2)].bitcast(F16),
                                            parts[:, q, 2 * b + j, w, 4 * s:4 * s + 4, :, :].rearrange(
                                                "p h a d -> p (h a d)"), idn16[:, :])
                        last.then_inc(turned, 1)

                    pairs(pe, step)

                @block.scalar
                def _(act):
                    def step(g, q):
                        act.wait_ge(turned, g + 1)
                        for b in range(2):
                            last = nc.scalar.copy(qk_t[:, bass.ds(g * 2 + b, 1), :].rearrange("p a n -> p (a n)"),
                                                  ps[:, 2 * q + b, :].bitcast(F16))
                        last.then_inc(t_copied, 1)

                    nc.scalar.copy(idn16[:, :], idn[:, :]).then_inc(t_copied, 1)
                    pairs(act, step)

            fetched = [sem("l1_fetched_even"), sem("l1_fetched_odd")]
            s_ps, shifted, exped = sem("l1_s_ps"), sem("l1_shifted"), sem("l1_exped")
            pt_ps, pt_dve, pt_act, o_ps = sem("l1_pt_ps"), sem("l1_pt_dve"), sem("l1_pt_act"), sem("l1_o_ps")
            o_ready, ot_ps, ot_copied, out_ps = (sem(f"l1_{n}") for n in ("o_ready", "ot_ps", "ot_copied", "out_ps"))
            heads_copied, view_ps, out_added = sem("l1_heads_copied"), sem("l1_view_ps"), sem("l1_out_added")
            scores_seen, outputs_seen = sem("l1_scores_seen"), sem("l1_outputs_seen")
            UPI = HEADS1
            UNITS = B * UPI
            STEP = 2 * UPI
            AHEAD = 3
            SB = 4
            LAG = 2
            pick = idn[:, :].rearrange("p (s v) -> p s v", v=VPAD)[:, :, 0:VW]

            def o_view(q):
                return ps[:, 6 + q, 0:2 * HEADS1 * VW].rearrange("p (h v) -> p h v", v=VW)

            def o_turned(q):
                return ps[0:C, 6 + q, N:2 * N]

            def o_out(q):
                return ps[:, 6 + q, 0:2 * C].rearrange("p (t c) -> p t c", t=2)

            def units(k, i, lag):
                n = k + lag
                if isinstance(i, int) and not 0 <= STEP * i + n < UNITS:
                    return None
                return i * STEP + n if not isinstance(i, int) else STEP * i + n, n % UPI

            def image(k, i, off):
                if (k - off) % UPI:
                    return None
                r = (k - off) // UPI
                if isinstance(i, int) and not 0 <= 2 * i + r < B:
                    return None
                return i * 2 + r if not isinstance(i, int) else 2 * i + r

            O_HEADS, O_NORM, O_ADD = 13, 15, 19
            O_VIEW, O_TURN, O_PROJ = 12, 14, 16
            O_COPY = 17

            def stream(eng, step, start=0):
                last = B // 2 - 1
                for k in range(start, STEP):
                    step(0, k)
                with eng.Fori(1, last) as i:
                    for k in range(STEP):
                        step(i, k)
                for k in range(STEP + O_ADD):
                    step(last, k)

            with nc.Block() as block:
                @block.sync
                def _(sp):
                    def fetch(b, q):
                        sp.dma_start(val_b[:, q, :, :, :].rearrange("p m h v -> p (m h v)"),
                                     vals[:, bass.ds(b * 2, 2), :, :].rearrange("p m h v -> p (m h v)")
                                     ).then_inc(fetched[q], 16)
                        sp.dma_start(qk_b[:, q, :, :, :, :].rearrange("p w s j n -> p (w s j n)"),
                                     qk_t[:, bass.ds(b, 1), :].rearrange("p a n -> p (a n)")).then_inc(fetched[q], 16)

                    fetch(0, 0)
                    fetch(1, 1)
                    with sp.Fori(1, B // 2) as i:
                        for q in range(2):
                            sp.wait_ge(s_ps, i * STEP + (q * UPI - UPI))
                            sp.wait_ge(o_ps, 2 * i + (q - 1))
                            fetch(i * 2 + q, q)

                @block.tensor
                def _(pe):
                    def scores(k, i):
                        if (unit := units(k, i, AHEAD)) is None:
                            return
                        nt, hp = unit[1] // 4, unit[1] % 4
                        q = (k + AHEAD) // UPI % 2
                        if unit[1] == 0:
                            pe.wait_ge(fetched[q], (i + (k + AHEAD) // STEP) * 32 + 32)
                        for a in range(2):
                            r = 32 * hp
                            last = nc.tensor.matmul(
                                ps[:, (k + AHEAD) % SB, a * N:(a + 1) * N],
                                qk_b[r:r + 32, q, 0, a, nt, :],
                                qk_b[r:r + 32, q, 1, a, :, :].rearrange("p j n -> p (j n)"),
                                start=True, stop=True)
                        last.then_inc(s_ps, 1)

                    def step(i, k):
                        scores(k, i)
                        if units(k, i, -LAG) is not None:
                            pe.wait_ge(pt_act if k % 2 else pt_dve, i * (STEP // 2) + ((k - LAG) // 2 + 1))
                        if (unit := units(k, i, 0)) is not None:
                            pe.wait_ge(exped, unit[0] + 1)
                            for a in range(2):
                                for m in range(2):
                                    last = nc.tensor.transpose(ps[:, 4 + k % 2, (2 * a + m) * P:(2 * a + m + 1) * P],
                                                               prob[:, k % SB, a, m * P:(m + 1) * P], idn[:, :])
                            last.then_inc(pt_ps, 1)
                        if (unit := units(k, i, -LAG)) is not None:
                            n = k - LAG
                            nt, hp, q = unit[1] // 4, unit[1] % 4, n // UPI % 2
                            if unit[1] == 0 and (b := image(k, i, 2 * UPI + LAG)) is not None:
                                pe.wait_ge(out_added, b + 1)
                            for m in range(2):
                                for a in range(2):
                                    r = VPAD * (2 * (hp % 2) + a)
                                    col = (2 * nt + hp // 2) * P
                                    last = nc.tensor.matmul(ps[r:r + VPAD, 6 + q, col:col + P],
                                                            val_b[:, q, m, hp + 4 * a, :],
                                                            prob_t[:, n % 4, (2 * a + m) * P:(2 * a + m + 1) * P],
                                                            start=(m == 0), stop=(m == 1), skip_group_check=True)
                            if unit[1] == UPI - 1:
                                last.then_inc(o_ps, 1)
                        if (b := image(k, i, O_VIEW)) is not None:
                            q = (k - O_VIEW) // UPI % 2
                            pe.wait_ge(heads_copied, b + 1)
                            pe.sem_inc(outputs_seen, 1)
                            for n in range(4):
                                last = nc.tensor.matmul(ps[:, 6 + q, n * 4 * VW:(n + 1) * 4 * VW],
                                                        o_heads[:, n * P:(n + 1) * P], pick, start=True, stop=True)
                            last.then_inc(view_ps, 1)
                        if (b := image(k, i, O_TURN)) is not None:
                            q = (k - O_TURN) // UPI % 2
                            pe.wait_ge(o_ready, b + 1)
                            pe.sem_inc(outputs_seen, 1)
                            for j in range(2):
                                last = nc.tensor.transpose(o_turned(q)[:, j * P:(j + 1) * P],
                                                           o_tok[:, j, :, :].rearrange("p h d -> p (h d)"), idn[:, :])
                            last.then_inc(ot_ps, 1)
                        if (b := image(k, i, O_PROJ)) is not None:
                            q = (k - O_PROJ) // UPI % 2
                            pe.wait_ge(ot_copied, b + 1)
                            for j in range(2):
                                last = nc.tensor.matmul(o_out(q)[:, j, :], o_ch[:, j * P:(j + 1) * P],
                                                        proj_w[:, :], start=True, stop=True)
                            last.then_inc(out_ps, 1)

                    for k in range(-AHEAD, 0):
                        scores(k, 0)
                    stream(pe, step)

                @block.scalar
                def _(act):
                    def step(i, k):
                        if (unit := units(k, i, 0)) is not None:
                            act.wait_ge(shifted, unit[0] + 1)
                            for a in range(2):
                                last = nc.scalar.activation(prob[:, k % SB, a, :], prob[:, k % SB, a, :], ACT.Exp,
                                                            bias=nmax[:, k % SB, a:a + 1], scale=-1.0)
                            last.then_inc(exped, 1)
                        if (unit := units(k, i, -2)) is not None and k % 2:
                            act.wait_ge(pt_ps, unit[0] + 1)
                            nc.scalar.copy(prob_t[:, (k - 2) % 4, :], ps[:, 4 + k % 2, :]).then_inc(pt_act, 1)
                        if (b := image(k, i, O_COPY)) is not None:
                            act.wait_ge(ot_ps, b + 1)
                            nc.scalar.copy(o_ch[0:C, :], o_turned((k - O_COPY) // UPI % 2)).then_inc(ot_copied, 1)

                    stream(act, step)

                @block.vector
                def _(dve):
                    c = dve_chain.on(dve)

                    def step(i, k):
                        if (unit := units(k, i, 0)) is not None:
                            nt, hp = unit[1] // 4, unit[1] % 4
                            dve.wait_ge(s_ps, unit[0] + 1)
                            dve.sem_inc(scores_seen, 1)
                            for a in range(2):
                                last = nc.vector.tensor_tensor_reduce(
                                    out=prob[:, k % SB, a, :], in0=ps[:, k % SB, a * N:(a + 1) * N],
                                    in1=rel_bias[:, nt, hp + 4 * a, :], scale=1.0, scalar=3e38,
                                    op0=ALU.add, op1=ALU.min, accum_out=nmax[:, k % SB, a:a + 1])
                            last.then_inc(shifted, 1)
                        if (unit := units(k, i, -2)) is not None and k % 2 == 0:
                            dve.wait_ge(pt_ps, unit[0] + 1)
                            nc.vector.tensor_copy(prob_t[:, (k - 2) % 4, :], ps[:, 4 + k % 2, :]).then_inc(pt_dve, 1)
                        if (b := image(k, i, O_HEADS)) is not None:
                            dve.wait_ge(o_ps, b + 1)
                            nc.vector.tensor_copy(o_heads[:, :], ps[:, 6 + (k - O_HEADS) // UPI % 2, :]
                                                  ).then_inc(heads_copied, 1)
                        if (b := image(k, i, O_NORM)) is not None:
                            view = o_view((k - O_NORM) // UPI % 2)
                            dve.wait_ge(view_ps, b + 1)
                            nc.vector.reciprocal(inv_sum[:, :], view[:, :, DH1]).then_inc(sums_inverted, 1)
                            dve.wait_ge(sums_inverted, b + 1)
                            nc.vector.tensor_tensor(o_tok[:, :, :, :].rearrange("p t h d -> p (t h) d"), view[:, :, 0:DH1],
                                                    inv_sum[:, :].unsqueeze(2).broadcast_to((P, 2 * HEADS1, DH1)),
                                                    ALU.mult).then_inc(o_ready, 1)
                        if (b := image(k, i, O_ADD)) is not None:
                            dve.wait_ge(out_ps, b + 1)
                            xb = x_tok[:, bass.ds(b * 2, 2), :]
                            nc.vector.tensor_tensor(xb, xb, o_out((k - O_ADD) // UPI % 2), ALU.add).then_inc(out_added, 1)

                    stream(dve, step)

        def similarity():
            map_w = sbl("map_w", [KC, C])
            x_one = sbl("x2_one", [KC, 2, GTOK])
            x_zero = sbl("x2_zero", [KC, 2, GTOK])
            ones = sbl("x2_ones", [P, P])
            inv_sq = sbl("inv_sq", [P, NT])
            diag = sbl("inv_sq_diag", [P, 2, TPG, P])
            tx = sbl("tx", [P, TPG, C])
            dots = sbl("dots", [P, TPG, N])
            inv = sbl("inv_norms", [P, 2, TPG, N])
            o_ch = sbl("o2_ch", [P, N])
            squared, x_copied, diag_ready, inv_ps, dot_ps, relu_d, tx_ps, tx_copied, sim, o_ps, o_copied, ot_ps = (
                sem(f"l2_{n}") for n in ("squared", "x_copied", "diag_ready", "inv_ps", "dot_ps", "relu", "tx_ps",
                                         "tx_copied", "sim", "o_ps", "o_copied", "ot_ps"))

            sim_seen = sem("l2_sim_seen")

            def stream(eng, step, c=None, links=0):
                step(0, 0)
                with eng.Fori(0, GROUPS // 2 - 1) as i:
                    if c is not None:
                        c.loop(i, 2 * links)
                    step(i * 2 + 1, 1)
                    step(i * 2 + 2, 0)
                if c is not None:
                    c.end(GROUPS // 2 - 1)
                step(GROUPS - 1, 1)
                step(GROUPS, 0)

            with nc.Block() as block:
                @block.sync
                def _(sp):
                    load(sp, "l2", map_w[:, :], L2)

                @block.scalar
                def _(act):
                    nc.scalar.activation(sq[:, :, :], xn_tok[:, :, :], ACT.Square).then_inc(squared, 1)
                    for q in range(2):
                        nc.scalar.activation(x_zero[C:KC, q, :], xn_ch[C:KC, 0:GTOK], ACT.Copy, scale=0.0)

                    def prepare(g, q):
                        if is_group(g):
                            nc.scalar.copy(x_one[:, q, :], xn_ch[:, bass.ds(g * GTOK, GTOK)])
                            nc.scalar.copy(x_zero[0:C, q, :], xn_ch[0:C, bass.ds(g * GTOK, GTOK)]).then_inc(x_copied, 1)

                    def step(g, q):
                        if is_group(g - 1):
                            act.wait_ge(o_ps, g)
                            nc.scalar.copy(o_ch[:, :], ps[:, 7, 0:N]).then_inc(o_copied, 1)
                        prepare(g + 1, 1 - q)
                        if is_group(g):
                            act.wait_ge(dot_ps, g + 1)
                            nc.scalar.activation(dots[:, :, :],
                                                 ps[:, 2 * q:2 * q + 2, :].rearrange("p b (t n) -> p (b t) n", n=N),
                                                 ACT.Relu).then_inc(relu_d, 1)
                            act.wait_ge(tx_ps, g + 1)
                            nc.scalar.copy(tx[:, :, :], ps[:, 6, 0:TPG * C].rearrange("p (t c) -> p t c", t=TPG)
                                           ).then_inc(tx_copied, 1)

                    prepare(0, 0)
                    stream(act, step)

                @block.tensor
                def _(pe):
                    def products(g, q):
                        if not is_group(g):
                            return
                        pe.wait_ge(x_copied, g + 1)
                        for t in range(TPG):
                            last = nc.tensor.matmul(ps[:, 2 * q + t // 2, (t % 2) * N:(t % 2 + 1) * N],
                                                    x_zero[:, q, t * P:(t + 1) * P],
                                                    x_one[:, q, t // 2 * N:(t // 2 + 1) * N],
                                                    start=True, stop=True)
                        last.then_inc(dot_ps, 1)
                        pe.wait_ge(diag_ready, g + 1)
                        nc.tensor.matmul(ps[:, 4 + q, :], ones[:, :], diag[:, q, :, :].rearrange("p t n -> p (t n)"),
                                         start=True, stop=True).then_inc(inv_ps, 1)

                    def mapped(g, q):
                        if is_group(g):
                            for t in range(TPG):
                                last = nc.tensor.matmul(ps[:, 6, t * C:(t + 1) * C], x_one[:, q, t * P:(t + 1) * P],
                                                        map_w[:, :], start=True, stop=True)
                            last.then_inc(tx_ps, 1)

                    def step(g, q):
                        if is_group(g - 1):
                            pe.wait_ge(o_copied, g)
                            for j in range(2):
                                last = nc.tensor.transpose(ps[:, 7, N + j * P:N + (j + 1) * P],
                                                           o_ch[:, j * P:(j + 1) * P], idn[:, :])
                            last.then_inc(ot_ps, 1)
                        products(g + 1, 1 - q)
                        if is_group(g):
                            pe.wait_ge(tx_copied, g + 1)
                            pe.wait_ge(sim, g + 1)
                            pe.sem_inc(sim_seen, 1)
                            for j in range(2):
                                for b in range(2):
                                    last = nc.tensor.matmul(ps[b * C:(b + 1) * C, 7, 0:N], tx[:, 2 * b + j, :],
                                                            dots[:, 2 * b + j, :], start=(j == 0), stop=(j == 1),
                                                            skip_group_check=True)
                            last.then_inc(o_ps, 1)
                        mapped(g + 1, 1 - q)

                    pe.wait_ge(loaded["l2"], want["l2"])
                    products(0, 0)
                    mapped(0, 0)
                    stream(pe, step)

                @block.vector
                def _(dve):
                    c = dve_chain.on(dve)
                    c.link(nc.vector.memset(ones[:, :], 1.0))
                    dve.wait_ge(squared, 1)
                    c.link(nc.vector.tensor_reduce(inv_sq[:, :], sq[:, :, :], AX.X, ALU.add))
                    c.link(nc.vector.tensor_scalar(inv_sq[:, :], inv_sq[:, :], 1e-30, None, ALU.max))
                    c.link(nc.vector.reciprocal(inv_sq[:, :], inv_sq[:, :]))

                    def diagonal(g, q):
                        if is_group(g):
                            nc.vector.tensor_tensor(diag[:, q, :, :], idn[:, :].unsqueeze(1).broadcast_to((P, TPG, P)),
                                                    inv_sq[:, bass.ds(g * TPG, TPG)].unsqueeze(2).broadcast_to(
                                                        (P, TPG, P)), ALU.mult).then_inc(diag_ready, 1)

                    def step(g, q):
                        diagonal(g + 1, 1 - q)
                        if is_group(g):
                            dve.wait_ge(inv_ps, g + 1)
                            for b in range(2):
                                last = nc.vector.tensor_tensor(
                                    inv[:, q, 2 * b:2 * b + 2, :],
                                    ps[:, 4 + q, b * N:(b + 1) * N].unsqueeze(1).broadcast_to((P, 2, N)),
                                    inv_sq[:, bass.ds(g * TPG + 2 * b, 2)].unsqueeze(2).broadcast_to((P, 2, N)), ALU.mult)
                            c.link(last)
                        if is_group(g - 1):
                            dve.wait_ge(ot_ps, g)
                            xg = x_tok[:, bass.ds((g - 1) * TPG, TPG), :].rearrange("p (b j) c -> p b j c", b=2)
                            for b in range(2):
                                last = nc.vector.tensor_tensor(
                                    xg[:, b, :, :], xg[:, b, :, :],
                                    ps[:, 7, N:2 * N].rearrange("p (j b c) -> p b j c", j=2, b=2)[:, b, :, :], ALU.add)
                            c.link(last)
                        if is_group(g):
                            dve.wait_ge(relu_d, g + 1)
                            c.link(nc.vector.scalar_tensor_tensor(inv[:, q, :, :], inv[:, q, :, :], 1e16, dots[:, :, :],
                                                                  ALU.min, ALU.mult))
                            nc.vector.tensor_tensor(dots[:, :, :], inv[:, q, :, :], dots[:, :, :], ALU.mult).then_inc(sim, 1)

                    diagonal(0, 0)
                    stream(dve, step, c, 3)

        def convolution():
            TAPS = 5
            cw = sbl("conv_w", [P, TAPS, C])
            clip = sbl("conv_clip", [P, TAPS, C])
            sign = sbl("conv_sign", [P, TAPS, C])
            img = sbl("conv_img", [P, 2, 2, 2, PADS, SIDE])
            o_ch = sbl("conv_o_ch", [P, 2, N])
            signed, filled_act, filled_dve, o_ps, o_copied, ot_ps, w_ready, added, added_seen = (
                sem(f"l3_{n}") for n in ("signed", "filled_act", "filled_dve", "o_ps", "o_copied", "ot_ps", "w_ready",
                                         "added", "added_seen"))

            def fill(copy, g, q, b):
                src = xn_ch[0:C, bass.ds(g * GTOK + b * N, N)].rearrange("c (i j) -> c i j", j=SIDE)
                copy(img[0:C, q, b, 0, 1:SIDE + 1, 1:], src[:, :, :SIDE - 1])
                copy(img[C:P, q, b, 0, 1:SIDE + 1, :], src)
                copy(img[0:C, q, b, 1, 1:SIDE + 1, :SIDE - 1], src[:, :, 1:])
                return copy(img[C:P, q, b, 1, 0:SIDE, :SIDE - 1], src[:, :, 1:])

            with nc.Block() as block:
                @block.sync
                def _(sp):
                    load(sp, "l3", cw[:, :, :], L3)

                @block.scalar
                def _(act):
                    act.wait_ge(loaded["l3"], 16)
                    nc.scalar.activation(sign[:, :, :], cw[:, :, :], ACT.Sign).then_inc(signed, 1)
                    act.wait_ge(w_ready, 1)

                    def step(g, q):
                        if is_group(g + 1):
                            if from_third(g + 1):
                                act.wait_ge(o_ps, g)
                            fill(nc.scalar.copy, g + 1, 1 - q, 0).then_inc(filled_act, 1)
                        act.wait_ge(o_ps, g + 1)
                        nc.scalar.copy(o_ch[:, q, :], ps[:, q, 0:N]).then_inc(o_copied, 1)

                    fill(nc.scalar.copy, 0, 0, 0).then_inc(filled_act, 1)
                    pairs(act, step)

                @block.tensor
                def _(pe):
                    pe.wait_ge(w_ready, 1)

                    def turn(g, q):
                        pe.wait_ge(o_copied, g + 1)
                        for j in range(2):
                            last = nc.tensor.transpose(ps[:, q, N + j * P:N + (j + 1) * P],
                                                       o_ch[:, q, j * P:(j + 1) * P], idn[:, :])
                        last.then_inc(ot_ps, 1)

                    def step(g, q):
                        pe.wait_ge(filled_act, g + 1)
                        pe.wait_ge(filled_dve, g + 1)
                        if from_third(g):
                            pe.wait_ge(added, g - 1)
                        pe.sem_inc(added_seen, 1)
                        for tap, (side, dy) in enumerate(((0, 0), (0, 1), (0, 2), (1, 0), (1, 2))):
                            for b in range(2):
                                last = nc.tensor.matmul(
                                    ps[b * C:(b + 1) * C, q, 0:N], cw[:, tap, :],
                                    img[:, q, b, side, dy:dy + SIDE, :].rearrange("c i j -> c (i j)"),
                                    start=(tap == 0), stop=(tap == TAPS - 1), skip_group_check=True)
                        last.then_inc(o_ps, 1)
                        if is_group(g - 1):
                            turn(g - 1, 1 - q)

                    pairs(pe, step)
                    turn(GROUPS - 1, 1)

                @block.vector
                def _(dve):
                    c = dve_chain.on(dve)
                    c.link(nc.vector.memset(img[:, :, :, :, :, :], 0.0))
                    dve.wait_ge(loaded["l3"], 16)
                    c.link(nc.vector.tensor_scalar(clip[:, :, :], cw[:, :, :], 1.0, -1.0, ALU.min, ALU.max))
                    dve.wait_ge(signed, 1)
                    c.link(nc.vector.tensor_tensor(sign[:, :, :], sign[:, :, :], clip[:, :, :], ALU.subtract))
                    nc.vector.tensor_tensor(cw[:, :, :], sign[:, :, :], clip[:, :, :], ALU.add).then_inc(w_ready, 1)

                    def add(g, q):
                        dve.wait_ge(ot_ps, g + 1)
                        xg = x_tok[:, bass.ds(g * TPG, TPG), :].rearrange("p (b j) c -> p b j c", b=2)
                        turned = ps[:, q, N:2 * N].rearrange("p (j b c) -> p b j c", j=2, b=2)
                        for b in range(2):
                            last = nc.vector.tensor_tensor(xg[:, b, :, :], xg[:, b, :, :], turned[:, b, :, :], ALU.add)
                        last.then_inc(added, 1)

                    def step(g, q):
                        if is_group(g + 1):
                            if from_third(g + 1):
                                dve.wait_ge(o_ps, g)
                            fill(nc.vector.tensor_copy, g + 1, 1 - q, 1).then_inc(filled_dve, 1)
                        if is_group(g - 1):
                            add(g - 1, 1 - q)

                    fill(nc.vector.tensor_copy, 0, 0, 1).then_inc(filled_dve, 1)
                    pairs(dve, step)
                    add(GROUPS - 1, 1)

        swiglu_tiles = []
        for pair in range(E // 2):
            for n in range(PAIR0):
                tile = pair * PAIR0 + n
                swiglu_tiles.append((tile * P, tile * C, E + pair if n == 0 else 2 * pair + (n - 1) // FULL0))

        def gelu_tiles(hidden):
            per = hidden // P
            return [(n * P, n * C, n // per) for n in range(E * per)]

        pair_tiles = [(n * P, n * C, E + n) for n in range(E // 2)]

        local, stages = [], [0]

        def sbl(name, shape, dt=F32):
            return local[-1].enter_context(nc.sbuf_tensor(f"{name}_stage{stages[0]}", shape, dt))

        def stage(fn):
            with ExitStack() as s:
                local.append(s)
                stages[0] += 1
                fn()
                local.pop()

        def block0_experts():
            norm_stage(1e-5, stacked=True)
            experts(swiglu_tiles, ACT.Silu, True, "plus", F0, also=bias_bands, norm=GroupNorm(1e-6, False, 7))


        norm_stage(1e-6, stacked=True)
        stage(linear_attention)
        stage(block0_experts)
        start_loads(F1)
        stage(attention)
        norm_stage(1e-5, stacked=True, prepare=F1)
        stage(lambda: experts(gelu_tiles(H_L1), ACT.Gelu, False, "all", F1, norm=GroupNorm(1e-6, False, 7)))
        start_loads(F2)
        stage(similarity)
        norm_stage(1e-5, stacked=True, prepare=F2)
        stage(lambda: experts(gelu_tiles(H_L2), ACT.Gelu, False, "two", F2, norm=GroupNorm(1e-6, False, 7)))
        start_loads(F3)
        stage(convolution)
        norm_stage(1e-5, stacked=True, prepare=F3)
        stage(lambda: experts(pair_tiles, ACT.Gelu, False, "floor", F3, add_tokens=True))
        with nc.Block() as block:
            @block.sync
            def _(sp):
                sp.dma_start(out, x_tok[:, :, :]).then_inc(stored, 16)
                sp.wait_ge(stored, 16)
                for key, s in loaded.items():
                    if want[key]:
                        sp.wait_ge(s, want[key])


def layouts(a):
    f = np.float32

    def rows(w_t, bias=None):
        bias = np.zeros(w_t.shape[1], f) if bias is None else bias
        return np.concatenate([w_t, bias[None]], 0)

    def diag(a_, b_):
        z = np.zeros((2 * a_.shape[0], 2 * a_.shape[1]), f)
        z[:a_.shape[0], :a_.shape[1]], z[a_.shape[0]:, a_.shape[1]:] = a_, b_
        return z

    d = {}
    d["x"] = a["x"].reshape(B, C, 2, P).transpose(3, 0, 2, 1).reshape(P, NT, C)
    d["ident"] = np.eye(P, dtype=f)
    d["rank"] = np.tile(np.arange(E, 0, -1, dtype=f), (P, 1))
    wq = a["L0_conv_W_qkv"].T
    d["l0_qvk"] = np.concatenate([wq[:, 0:HID0], wq[:, 2 * HID0:], wq[:, HID0:2 * HID0]], 1)
    d["l0_out"] = a["L0_conv_W_out"].T
    d["l0_mem"] = a["L0_conv_memory"].reshape(C, MEM)
    head = np.arange(HID0) // DH0
    d["l0_mask"] = (head[:, None] == head[None]).astype(f)
    d["l0_rows"] = np.stack([a["L0_conv_b_out"], a["L0_conv_ln_g"], a["L0_conv_ln_b"]])

    selector = np.zeros((KG, E + E // 2, P), f)
    for r in PARTS_AT:
        for e in range(E):
            selector[r + e, e] = 1
            selector[r + e, E + e // 2, e % 2 * C:(e % 2 + 1) * C] = 1
    d["selector"] = selector

    def up(w):
        out = np.zeros((C, 4 * PAIR0 * P), f)
        for pair in range(E // 2):
            at = pair * PAIR0 * P
            for s in range(2):
                w_t = w[2 * pair + s].T
                out[:, at + s * C:at + s * C + TAIL0] = w_t[:, FULL0 * P:]
                out[:, at + (1 + s * FULL0) * P:at + (1 + (s + 1) * FULL0) * P] = w_t[:, :FULL0 * P]
        return out

    down = np.zeros((P, 4 * PAIR0 * C), f)
    for pair in range(E // 2):
        at = pair * PAIR0 * C
        for s in range(2):
            w_t = a["L0_ffn_w2"][2 * pair + s].T
            down[s * C:s * C + TAIL0, at:at + C] = w_t[FULL0 * P:]
            for n in range(FULL0):
                c0 = at + (1 + s * FULL0 + n) * C
                down[:, c0:c0 + C] = w_t[n * P:(n + 1) * P]
    d["f0_w1"], d["f0_w3"], d["f0_w2"] = up(a["L0_ffn_w1"]), up(a["L0_ffn_w3"]), down
    d["f0_router"], d["f0_router_b"] = a["L0_ffn_router_w"].T, np.zeros((1, E), f)

    def side_by_side(w):
        return w.transpose(1, 0, 2).reshape(w.shape[1], -1)

    def qkv(n):
        return rows(diag(a[f"L1_conv_{n}1_w"].T, a[f"L1_conv_{n}2_w"].T),
                    np.concatenate([a[f"L1_conv_{n}1_b"], a[f"L1_conv_{n}2_b"]]))

    d["l1_qkv"] = np.concatenate([qkv("q"), qkv("k"), qkv("v")], 1)
    heads = [2 * c + s + 4 * a_ for c in range(2) for s in range(2) for a_ in range(2)]
    order = np.concatenate([np.arange(h * DH1, (h + 1) * DH1) for h in heads] + [[C]])
    d["l1_proj"] = qkv("proj")[order]
    d["l1_scale"] = np.concatenate([a["L1_conv_logit_scale"].reshape(-1), np.ones(HEADS1, f)])
    r = np.arange(-(SIDE - 1), SIDE).astype(f) / f(SIDE - 1 + 1e-8)
    gh, gw = np.meshgrid(r, r, indexing="ij")
    tab = np.stack([gh, gw]) * f(3.2)
    tab = (np.sign(tab) * (f(1) - np.exp(-np.abs(tab)))).reshape(2, -1)
    d["l1_tab"] = np.concatenate([tab, np.ones((1, REL * REL), f)])[:, ::-1]
    d["l1_m1"] = rows(a["L1_conv_mlp_w1"].T, a["L1_conv_mlp_b1"])
    d["l1_m2"] = a["L1_conv_mlp_w2"].T
    def gelu_experts(n, w1, b1, w2, b2, router, router_b):
        d[f"f{n}_w1"] = side_by_side(w1)
        d[f"f{n}_b1"] = b1.reshape(-1, P).T
        d[f"f{n}_w2"] = side_by_side(w2.reshape(-1, P, C))
        d[f"f{n}_b2"] = np.zeros((KG, C), f)
        for r in PARTS_AT:
            d[f"f{n}_b2"][r:r + E] = b2
        d[f"f{n}_router"], d[f"f{n}_router_b"] = router, router_b.reshape(1, E)

    gelu_experts(1, a["L1_ffn_W1"], a["L1_ffn_b1"], a["L1_ffn_W2"], a["L1_ffn_b2"], a["L1_ffn_gate_w"], a["L1_ffn_gate_b"])
    gelu_experts(2, a["L2_ffn_W1"], a["L2_ffn_b1"], a["L2_ffn_W2"], a["L2_ffn_b2"], a["L2_ffn_Wg"], a["L2_ffn_bg"])
    gelu_experts(3, a["L3_ffn_w1"], a["L3_ffn_b1"], a["L3_ffn_w2"], a["L3_ffn_b2"], a["L3_ffn_router_w"].T,
                 np.zeros(E, f))
    d["l2_map"] = rows(a["L2_conv_W"].T, a["L2_conv_bias"])
    w = a["L3_conv_W"].transpose(1, 2, 3, 0)
    conv = np.zeros((P, 5, C), f)
    conv[:C, 0:3], conv[C:, 0:3] = w[:, :, 0], w[:, :, 1]
    conv[:C, 3], conv[C:, 3], conv[:C, 4] = w[:, 0, 2], w[:, 1, 2], w[:, 2, 2]
    d["l3_conv"] = conv
    return {k: np.ascontiguousarray(v) for k, v in d.items()}


def build(nc, d, out, scratch):
    metaformer(
        nc, d["x"], d["ident"], d["rank"], d["selector"],
        [d["l0_qvk"], d["l0_out"], d["l0_mem"], d["l0_mask"], d["l0_rows"]],
        (d["f0_w1"], d["f0_w3"], d["f0_w2"], None, None, d["f0_router"], d["f0_router_b"]),
        dict(qkv_w=d["l1_qkv"], proj_w=d["l1_proj"], scale=d["l1_scale"], tab=d["l1_tab"],
             m1=d["l1_m1"], m2=d["l1_m2"], scratch=scratch),
        (d["f1_w1"], None, d["f1_w2"], d["f1_b1"], d["f1_b2"], d["f1_router"], d["f1_router_b"]),
        d["l2_map"],
        (d["f2_w1"], None, d["f2_w2"], d["f2_b1"], d["f2_b2"], d["f2_router"], d["f2_router_b"]),
        d["l3_conv"],
        (d["f3_w1"], None, d["f3_w2"], d["f3_b1"], d["f3_b2"], d["f3_router"], d["f3_router_b"]),
        out)


def kernel(**inputs):
    import concourse.bacc as bacc
    from concourse.bass_utils import run_bass_kernel_spmd

    nc = bacc.Bacc("TRN2", target_bir_lowering=False, num_devices=1)
    arrays = layouts({k: np.asarray(v) for k, v in inputs.items()})
    d = {k: nc.dram_tensor(k, v.shape, mybir.dt.from_np(v.dtype), kind="ExternalInput").ap()
         for k, v in arrays.items()}
    out = nc.dram_tensor("out", (P, NT, C), F32, kind="ExternalOutput").ap()
    scratch = nc.dram_tensor("bias_bands", (SIDE, HEADS1, REL, SIDE), F32, kind="Internal").ap()
    build(nc, d, out, scratch)
    got = run_bass_kernel_spmd(nc, [arrays], core_ids=[0]).results[0]["out"]
    return got.reshape(P, B, 2, C).transpose(1, 3, 2, 0).reshape(B, C, SIDE, SIDE)
```
